# Optimizing a Trainium2 kernel written in Bass

```python
import numpy as np
import jax
import jax.numpy as jnp

def _softmax(x, axis=-1):
    return jax.nn.softmax(x, axis=axis)

def _gelu(x):
    return jax.nn.gelu(x, approximate=True)

def _silu(x):
    return jax.nn.silu(x)

def _sigmoid(x):
    return jax.nn.sigmoid(x)

def _layernorm(x, axis=-1, eps=1e-05):
    m = jnp.mean(x, axis=axis, keepdims=True)
    v = jnp.var(x, axis=axis, keepdims=True)
    return (x - m) / jnp.sqrt(v + eps)

def _scatter_add(tgt, idx, src, axis=0):
    return tgt.at[idx].add(src)

def _segment_sum(src, seg, n):
    return jax.ops.segment_sum(src, seg, n)
kernel_name = 'mk_conv_attn_hybrid_d2_conv_nhwc1024_r4_87fbb2'

def setup_inputs(seed: int=0):
    np.random.seed(seed)
    _w = jnp.asarray

    def _rec_inputs():
        import jax
        import jax.numpy as jnp
        _gk = jax.random.key(seed)
        x = -0.0002928 + 1 * jax.random.normal(jax.random.fold_in(_gk, 1), (1, 32, 32, 256), jnp.float32)
        return x
    x = _rec_inputs()

    def _L0_conv_setup():
        import jax, jax.numpy as jnp
        import numpy as np
        E, S, B, H, F = (8, 32, 32, 256, 1024)
        key = jax.random.key(seed)
        k0, k1, k2, k3, k4 = jax.random.split(key, 5)
        return {'x': jax.random.normal(k0, (1, S, B, H), dtype=jnp.float32), 'gate_w': jax.random.normal(k1, (H, E), dtype=jnp.float32) * 0.02, 'w1': jax.random.normal(k2, (E, H, F), dtype=jnp.float32) * 0.02, 'w3': jax.random.normal(k3, (E, H, F), dtype=jnp.float32) * 0.02, 'w2': jax.random.normal(k4, (E, F, H), dtype=jnp.float32) * 0.02}
    _L0_conv_all = _L0_conv_setup()
    _L0_conv_in = {k: v for k, v in _L0_conv_all.items() if k in ('gate_w', 'w1', 'w3', 'w2')}
    del _L0_conv_all

    def _L1_attn_setup():
        import math
        import jax, jax.numpy as jnp
        import numpy as np
        B, T, C, H = (2, 512, 256, 16)
        key = jax.random.key(seed)
        k1, k2, k3 = jax.random.split(key, 3)
        x = jax.random.normal(k1, (B, T, C), dtype=jnp.float32)
        Wqkv = jax.random.normal(k2, (C, 3 * C), dtype=jnp.float32) * 0.02
        bqkv = jnp.zeros((3 * C,), dtype=jnp.float32)
        Wo = jax.random.normal(k3, (C, C), dtype=jnp.float32) * (0.02 / math.sqrt(2 * 12))
        bo = jnp.zeros((C,), dtype=jnp.float32)
        return {'x': x, 'Wqkv': Wqkv, 'bqkv': bqkv, 'Wo': Wo, 'bo': bo}
    _L1_attn_all = _L1_attn_setup()
    _L1_attn_in = {k: v for k, v in _L1_attn_all.items() if k in ('Wqkv', 'bqkv', 'Wo', 'bo')}
    del _L1_attn_all

    def _L1_ffn_setup():
        import jax, jax.numpy as jnp
        import numpy as np
        NUM_EXPERTS = 8
        TOP_K = 2
        N_EMBD = 256
        D_FFN = 512
        key = jax.random.key(seed)
        k1, k2, k3, k4 = jax.random.split(key, 4)
        x = jax.random.normal(k1, (4, 512, N_EMBD), dtype=jnp.float32)
        router_w = jax.random.normal(k2, (NUM_EXPERTS, N_EMBD), dtype=jnp.float32) * 0.02
        w1 = jax.random.normal(k3, (N_EMBD, D_FFN * NUM_EXPERTS), dtype=jnp.float32) * 0.02
        w2 = jax.random.normal(k4, (D_FFN * NUM_EXPERTS, N_EMBD), dtype=jnp.float32) * 0.02
        return {'x': x, 'router_w': router_w, 'w1': w1, 'w2': w2}
    _L1_ffn_all = _L1_ffn_setup()
    _L1_ffn_in = {k: v for k, v in _L1_ffn_all.items() if k in ('router_w', 'w1', 'w2')}
    del _L1_ffn_all
    return {'x': x, 'L0_conv_gate_w': _L0_conv_in['gate_w'], 'L0_conv_w1': _L0_conv_in['w1'], 'L0_conv_w3': _L0_conv_in['w3'], 'L0_conv_w2': _L0_conv_in['w2'], 'L1_attn_Wqkv': _L1_attn_in['Wqkv'], 'L1_attn_bqkv': _L1_attn_in['bqkv'], 'L1_attn_Wo': _L1_attn_in['Wo'], 'L1_attn_bo': _L1_attn_in['bo'], 'L1_ffn_router_w': _L1_ffn_in['router_w'], 'L1_ffn_w1': _L1_ffn_in['w1'], 'L1_ffn_w2': _L1_ffn_in['w2']}

def reference(x, L0_conv_gate_w, L0_conv_w1, L0_conv_w3, L0_conv_w2, L1_attn_Wqkv, L1_attn_bqkv, L1_attn_Wo, L1_attn_bo, L1_ffn_router_w, L1_ffn_w1, L1_ffn_w2):
    import jax
    import jax.numpy as jnp

    def _L0_conv_ref(x, gate_w, w1, w3, w2):
        import jax, jax.numpy as jnp
        import numpy as np
        E, S, B, H, F = (8, 32, 32, 256, 1024)
        logits = jnp.einsum('zsbh,he->zsbe', x, gate_w)
        probs = jax.nn.softmax(logits, axis=-1)
        w0 = jnp.max(probs, axis=-1, keepdims=True)
        cond0 = probs == w0
        masked = jnp.where(cond0, jnp.zeros_like(probs), probs)
        w1v = jnp.max(masked, axis=-1, keepdims=True)
        cond1 = masked == w1v
        m = 1.0 / (w0 + w1v)
        ew = cond0.astype(x.dtype) * (m * w0) + cond1.astype(x.dtype) * (m * w1v)
        h = jnp.einsum('zsbh,ehf->ezsbf', x, w1)
        g = jnp.einsum('zsbh,ehf->ezsbf', x, w3)
        y = jnp.einsum('ezsbf,efh->ezsbh', jax.nn.silu(h) * g, w2)
        out = jnp.einsum('ezsbh,zsbe->zsbh', y, ew)
        return out

    def _L1_attn_ref(x, Wqkv, bqkv, Wo, bo):
        import math
        import jax, jax.numpy as jnp
        import numpy as np
        B, T, C, H = (2, 512, 256, 16)
        b, t, c = x.shape
        h = H
        d = c // h
        qkv = x @ Wqkv + bqkv
        q, k, v = jnp.split(qkv, 3, axis=-1)

        def heads(z):
            return z.reshape(b, t, h, d).transpose(0, 2, 1, 3)
        q, k, v = (heads(q), heads(k), heads(v))
        att = jnp.einsum('bhqd,bhkd->bhqk', q, k) / math.sqrt(c)
        mask = jnp.tril(jnp.ones((t, t), dtype=bool))
        att = jnp.where(mask, att, -jnp.inf)
        att = jax.nn.softmax(att, axis=-1)
        out = jnp.einsum('bhqk,bhkd->bhqd', att, v)
        out = out.transpose(0, 2, 1, 3).reshape(b, t, c)
        return out @ Wo + bo

    def _L1_ffn_ref(x, router_w, w1, w2):
        import jax, jax.numpy as jnp
        import numpy as np
        NUM_EXPERTS = 8
        TOP_K = 2
        N_EMBD = 256
        D_FFN = 512
        B, T, D = x.shape
        xf = x.reshape(B * T, D)
        N = B * T
        logits = xf @ router_w.T
        probs = jax.nn.softmax(logits, axis=-1)
        top_v, top_i = jax.lax.top_k(probs, TOP_K)
        top_v = top_v / jnp.sum(top_v, axis=-1, keepdims=True)
        gate = jnp.zeros((N, NUM_EXPERTS), dtype=x.dtype)
        gate = gate.at[jnp.arange(N)[:, None], top_i].set(top_v)
        w1r = w1.reshape(D, NUM_EXPERTS, D_FFN)
        w2r = w2.reshape(NUM_EXPERTS, D_FFN, D)
        out = jnp.zeros((N, D), dtype=x.dtype)
        for e in range(NUM_EXPERTS):
            h = jax.nn.gelu(xf @ w1r[:, e, :], approximate=False)
            out = out + gate[:, e:e + 1] * (h @ w2r[e])
        return out.reshape(B, T, D)

    def _gn(v, G=32, eps=1e-05):
        B_, H_, W_, C_ = v.shape
        g = v.reshape(B_, H_, W_, G, C_ // G)
        m = jnp.mean(g, axis=(1, 2, 4), keepdims=True)
        s = jnp.var(g, axis=(1, 2, 4), keepdims=True)
        return ((g - m) / jnp.sqrt(s + eps)).reshape(v.shape)

    def _ln_c(v, eps=1e-06):
        m = jnp.mean(v, axis=-1, keepdims=True)
        s = jnp.var(v, axis=-1, keepdims=True)
        return (v - m) / jnp.sqrt(s + eps)

    def _ln_t(v, eps=1e-05):
        m = jnp.mean(v, axis=-1, keepdims=True)
        s = jnp.var(v, axis=-1, keepdims=True)
        return (v - m) / jnp.sqrt(s + eps)

    def _to_tokens(v):
        B_, H_, W_, C_ = v.shape
        return v.reshape(B_, H_ * W_, C_)

    def _from_tokens(t, like):
        return t.reshape(like.shape)
    x = x + _L0_conv_ref(_gn(x), L0_conv_gate_w, L0_conv_w1, L0_conv_w3, L0_conv_w2)
    t = _to_tokens(x)
    t = t + _L1_attn_ref(_ln_t(t), L1_attn_Wqkv, L1_attn_bqkv, L1_attn_Wo, L1_attn_bo)
    t = t + _L1_ffn_ref(_ln_t(t), L1_ffn_router_w, L1_ffn_w1, L1_ffn_w2)
    x = _from_tokens(t, x)
    return x

_drawn_inputs = setup_inputs


def setup_inputs(seed=0):
    import zlib

    import numpy as np

    out = dict(_drawn_inputs(seed))
    spreads = {'L1_attn_bqkv': (0.0, 0.8), 'L1_attn_bo': (0.0, 0.1)}
    factors = {'L1_attn_Wqkv': 8.0, 'L1_attn_Wo': 6.867}
    for name, (base, spread) in spreads.items():
        noise = np.random.default_rng([zlib.crc32(name.encode()), seed]).standard_normal(out[name].shape)
        drawn = base * np.exp(spread * noise) if base else spread * noise
        out[name] = jnp.asarray(drawn.astype(out[name].dtype))
    for name, factor in factors.items():
        out[name] = (out[name] * factor).astype(out[name].dtype)
    return out
```

```python
from contextlib import ExitStack

import concourse.bass as bass
from concourse import mybir

F32 = mybir.dt.float32
F32R = mybir.dt.float32r
BF16 = mybir.dt.bfloat16
ALU = mybir.AluOpType
ACT = mybir.ActivationFunctionType
AX_X = mybir.AxisListType.X

P = 128
T = 1024
C = 256
KC = C // P
TT = T // P
HALF = 512
NH = T // HALF
E = 8
GROUP = 8
HEADS = 16
D = C // HEADS
PAIRS = HEADS // 2
HG = 4
GROUPS = HEADS // HG
QT = HALF // P
MASKED = -1e30
GN_EPS = LN_EPS = 1e-5


class Moe:

    def __init__(self, name, f, gated):
        self.name, self.gated = name, gated
        self.nf = f // P
        self.stages = NH * self.nf
        self.ups = KC * (2 if gated else 1)
        self.per_chunk = self.nf // 2
        self.cols = self.ups * P + C
        self.staged = 16 * (3 if gated else 2)


STEPS = [(qb, kt) for qb in range(NH) for kt in range(QT * (qb + 1))]


def build(nc, xT_d, gate_d, w1_d, w3_d, w2_d, wqkv_d, bqkv_d, wo_d, bo_d, router_d, v1_d, v2_d, outT_d):
    L0 = Moe("l0", w1_d.shape[2], True)
    L1 = Moe("l1", v1_d.shape[1] // E, False)

    def at(name, shape, dt, offset):
        return nc.alloc_sbuf_tensor_at(name, shape, dt, offset=offset)

    cursor = [16512]

    def place(name, shape, dt, size=4):
        offset = cursor[0]
        n = size
        for s in shape[1:]:
            n *= s
        cursor[0] += (n + 31) // 32 * 32
        return at(name, shape, dt, offset), offset

    w_hi, WHI = place("w_hi", [P, L0.nf, 768], F32R)
    w_lo, WLO = place("w_lo", [P, L0.nf, 768], F32R)
    stage0, STG = place("stage0", [P, 2, L0.per_chunk * L0.cols], F32)
    acc, _ = place("acc", [P, KC, T], F32)
    xn, XN_AT = place("xn", [P, KC, T], F32)
    x_hi, _ = place("x_hi", [P, KC, T], F32R)
    x_lo, _ = place("x_lo", [P, KC, T], F32R)
    gates, GATES = place("gates", [P, E, T], F32)
    sil, SIL = place("sil", [P, 2, HALF], F32)
    prod, _ = place("prod", [P, 2, HALF], F32)
    a_hi, _ = place("a_hi", [P, 2, HALF], F32R)
    a_lo, _ = place("a_lo", [P, 2, HALF], F32R)
    gated_y, _ = place("gated_y", [P, 2 * NH, HALF], F32)
    ident, _ = place("ident", [P, P], F32)
    identb, _ = place("identb", [P, P], BF16, 2)
    mask_q, _ = place("mask_q", [P, P], BF16, 2)
    mask_k, _ = place("mask_k", [P, P], BF16, 2)
    mean_mat, _ = place("mean_mat", [P, P], F32)
    group_mat, _ = place("group_mat", [P, P], F32)
    spread, _ = place("spread", [2 * E, E, P], F32R)
    gate_w, _ = place("gate_w", [P, KC, E], F32)
    router_w, _ = place("router_w", [P, KC, E], F32)
    stats, _ = place("stats", [P, KC, NH, 6], F32)
    small, _ = place("small", [P, 32], F32)
    rstd, _ = place("rstd", [P, TT], F32)
    rt, _ = place("rt", [P, 10, TT, E], F32)
    rs, _ = place("rs", [P, 10, TT], F32)
    order, _ = place("order", [P, TT, E], F32)
    split_g, _ = place("split_g", [P, TT, 2 * E], F32)
    gates_t, _ = place("gates_t", [2 * E, T], F32R)
    eps, _ = place("eps", [P, 1], F32)
    bqk, _ = place("bqk", [P, 2, KC], F32)
    bv, _ = place("bv", [P, C], F32)
    key_ones, _ = place("key_ones", [P, 1], F32)
    key_tmp, _ = place("key_tmp", [P, 1], F32)
    v_sb, _ = place("v_sb", [P, TT, HEADS, 2 * D], F32)
    probs, PROBS = place("probs", [P, 2 * HG, HALF], F32)
    assert cursor[0] <= nc.sbuf_usable_end

    spread_f = at("spread_f", [2 * E, E, P], F32, GATES)
    squares = at("squares", [P, KC, T], F32, GATES)
    stage1 = at("stage1", [P, 2, L1.per_chunk * L1.cols], F32, STG)
    q_st = at("q_st", [P, 2, 2, T], F32R, WHI)
    k_st = at("k_st", [P, 2, 2, T], F32R, WHI + 16384)
    o_sb = at("o_sb", [P, GROUPS, T], F32, WHI + 32768)
    max_t = at("max_t", [P, 2, TT, P], F32, STG + 8192)
    wo_sb = at("wo_sb", [P, GROUPS, C], F32, STG + 16384)
    qk_hi = at("qk_hi", [P, 2, KC, T], F32R, GATES)
    qk_lo = at("qk_lo", [P, 2, KC, T], F32R, GATES + 16384)
    wqkv_hi = at("wqkv_hi", [P, KC, 3 * C], F32R, SIL)
    wqkv_lo = at("wqkv_lo", [P, KC, 3 * C], F32R, SIL + 6144)
    pick = at("pick", [P, 4, 4, P], F32R, SIL + 12288)
    sums = at("sums", [P, HALF], F32, SIL + 20480)
    rsum = at("rsum", [P, HALF], F32, SIL + 22528)
    wqkv = at("wqkv", [P, KC, 3 * C], F32, PROBS)
    pick_f = at("pick_f", [P, 4, 4, P], F32, PROBS + 6144)
    maxes = at("maxes", [P, 2, HG, TT], F32, XN_AT)

    ctx = ExitStack()
    banks = ctx.enter_context(nc.psum_tensor("banks", [P, 8 * HALF], F32))
    bank = [banks[:, i * HALF:(i + 1) * HALF] for i in range(8)]

    def sem(name):
        return ctx.enter_context(nc.semaphore(name))

    x_in, gatew_in, routerw_in, attn_in, wo_in, out_done = (sem(n) for n in (
        "x_in", "gatew_in", "routerw_in", "attn_in", "wo_in", "out_done"))
    pool_step, dve_step = sem("pool_step"), sem("dve_step")
    group_ready, consts_ready, cleared = sem("group_ready"), sem("consts_ready"), sem("cleared")
    gn_stats, gn_mean, gn_var, gn_std = sem("gn_stats"), sem("gn_mean"), sem("gn_var"), sem("gn_std")
    ln_mean, ln_center, ln_square, ln_var = sem("ln_mean"), sem("ln_center"), sem("ln_square"), sem("ln_var")
    ln_std, ln_rstd, ln_spread = sem("ln_std"), sem("ln_rstd"), sem("ln_spread")
    split_done = sem("split_done")
    logits_done, logits_centred, logits_exp = sem("logits_done"), sem("logits_centred"), sem("logits_exp")
    gate_split, gate_turned, gate_rows = sem("gate_split"), sem("gate_turned"), sem("gate_rows")
    spread_mm = sem("spread_mm")
    spread_even, spread_odd = sem("spread_even"), sem("spread_odd")
    moe_sems = {}
    for m in (L0, L1):
        moe_sems[m.name] = {n: sem(f"{m.name}_{n}") for n in (
            "staged0", "staged1", "whi_done", "wlo_done", "up_done", "sil_done", "up_free",
            "a_hi_done", "a_ready", "a_free", "y_free", "gy_free")}
    wqkv_hi_done, wqkv_lo_done = sem("wqkv_hi_done"), sem("wqkv_lo_done")
    proj_mm, proj_hi, proj_free = sem("proj_mm"), sem("proj_hi"), sem("proj_free")
    v_mm, v_done = sem("v_mm"), sem("v_done")
    stack_mm, stack_done = sem("stack_mm"), sem("stack_done")
    smax_mm, smax_done = sem("smax_mm"), sem("smax_done")
    maxcol_ready, maxrow_mm, qmax_done = sem("maxcol_ready"), sem("maxrow_mm"), sem("qmax_done")
    st_mm, exp_done, pv_done, po_done = sem("st_mm"), sem("exp_done"), sem("pv_done"), sem("po_done")
    wo_mm, attn_added = sem("wo_mm"), sem("attn_added")

    def staging(m, b):
        st = (stage0 if m.gated else stage1)[:, b, :]
        n = m.ups * m.per_chunk * P
        return (st[:, 0:n].rearrange("p (u f) -> p u f", u=m.ups),
                st[:, n:n + m.per_chunk * C].rearrange("p (f c) -> p f c", c=C))

    def load_stage(eng, m, e, b):
        s = moe_sems[m.name][f"staged{b}"]
        w = m.per_chunk * P
        ups, downs = staging(m, b)
        if m.gated:
            for i, src in enumerate((w1_d, w3_d)):
                eng.dma_start(ups[:, KC * i:KC * (i + 1), :],
                              src[bass.ds(e, 1), :, b * w:(b + 1) * w].rearrange("a (k p) f -> p (a k) f", p=P)
                              ).then_inc(s, 16)
            eng.dma_start(downs, w2_d[bass.ds(e, 1), b * w:(b + 1) * w, :].rearrange(
                "a (f p) c -> p (a f) c", p=P)).then_inc(s, 16)
        else:
            eng.dma_start(ups, v1_d.rearrange("(k p) f -> p k f", p=P)[:, :, bass.ds(e * (m.nf * P) + b * w, w)]
                          ).then_inc(s, 16)
            eng.dma_start(downs, v2_d[bass.ds(e * (m.nf * P) + b * w, w), :].rearrange("(f p) c -> p f c", p=P)
                          ).then_inc(s, 16)

    def slot_parts(m, f, buf):
        ups, downs = staging(m, f // m.per_chunk)
        i = f % m.per_chunk
        n = m.ups * P
        return ((buf[:, f, 0:n].rearrange("p (u c) -> p u c", c=P), ups[:, :, i * P:(i + 1) * P]),
                (buf[:, f, n:n + C], downs[:, i, :]))

    block = ctx.enter_context(nc.Block())

    @block.sync
    def _(sp):
        for k in range(KC):
            sp.dma_start(acc[:, k, :], xT_d[k * P:(k + 1) * P, :]).then_inc(x_in, 16)
        sp.dma_start(gate_w[:, :, :], gate_d.rearrange("(k p) e -> p k e", p=P)).then_inc(gatew_in, 16)
        s0, s1 = moe_sems["l0"], moe_sems["l1"]
        for b in range(2):
            load_stage(sp, L0, 0, b)
        sp.dma_start(router_w[:, :, :], router_d.rearrange("(k p) e -> p k e", p=P)).then_inc(routerw_in, 16)
        for i in range(2):
            for k in range(KC):
                lo = i * C + k * P
                sp.dma_start(bqk[:, i, k:k + 1], bqkv_d[lo:lo + P].rearrange("(p a) -> p a", a=1)
                             ).then_inc(attn_in, 16)
        sp.dma_start(bv[:, :], bqkv_d[2 * C:3 * C].partition_broadcast(P)).then_inc(attn_in, 16)
        sp.dma_start(wqkv[:, :, :], wqkv_d.rearrange("(k p) n -> p k n", p=P)).then_inc(attn_in, 16)
        with sp.Fori(1, E) as e:
            for b in range(2):
                sp.wait_ge(s0["wlo_done"], (e - 1) * L0.nf + (b + 1) * L0.per_chunk)
                load_stage(sp, L0, e, b)
        sp.wait_ge(s0["wlo_done"], E * L0.nf)
        for b in range(2):
            load_stage(sp, L1, 0, b)
        sp.wait_ge(cleared, 2)
        for j in range(HG):
            sp.dma_start(wo_sb[2 * D * j:2 * D * j + D, :, :],
                         wo_d.rearrange("(g j d) c -> j d g c", j=HG, d=D)[j]).then_inc(wo_in, 16)
        sp.dma_start(wo_sb[D:D + 1, 0, :], bo_d.rearrange("(a c) -> a c", a=1)).then_inc(wo_in, 16)
        with sp.Fori(1, E) as e:
            for b in range(2):
                sp.wait_ge(s1["wlo_done"], (e - 1) * L1.nf + (b + 1) * L1.per_chunk)
                load_stage(sp, L1, e, b)
        for n in range(NH):
            sp.wait_ge(s1["gy_free"], 4 + 4 * (E - 1) + 2 * (n + 1))
            sp.dma_start(outT_d.rearrange("(k p) t -> p k t", p=P)[:, :, n * HALF:(n + 1) * HALF],
                         acc[:, :, n * HALF:(n + 1) * HALF]).then_inc(out_done, 16)
        sp.wait_ge(out_done, 16 * NH)

    @block.gpsimd
    def _(pool):
        n = [0]

        def link(ins):
            n[0] += 1
            ins.then_inc(pool_step, 1)
            pool.wait_ge(pool_step, n[0])

        for m in (L0, L1):
            pool.sem_inc(moe_sems[m.name]["gy_free"], 2 * NH)
        link(pool.memset(group_mat[:, :], 1.0 / GROUP))
        grouped = group_mat[:, :].rearrange("p (g c) -> p g c", c=GROUP)
        link(pool.affine_select(out=grouped, in_=grouped, compare_op=ALU.is_ge, fill=0.0, base=0,
                                pattern=[[-GROUP, P // GROUP], [0, GROUP]], channel_multiplier=1))
        link(pool.affine_select(out=grouped, in_=grouped, compare_op=ALU.is_ge, fill=0.0, base=GROUP - 1,
                                pattern=[[GROUP, P // GROUP], [0, GROUP]], channel_multiplier=-1))
        pool.memset(eps[:, :], GN_EPS).then_inc(group_ready, 1)
        link(pool.memset(mean_mat[:, :], 1.0 / C))
        link(pool.memset(ident[:, :], 0.0))
        link(pool.affine_select(out=ident[:, :], in_=ident[:, :], compare_op=ALU.not_equal, fill=1.0, base=0,
                                pattern=[[-1, P]], channel_multiplier=1))
        link(pool.memset(spread_f[:, :, :], 0.0))
        for half in range(2):
            link(pool.affine_select(out=spread_f[:, :, :], in_=spread_f[:, :, :], compare_op=ALU.not_equal,
                                    fill=1.0, base=-half * E, pattern=[[-1, E], [0, P]],
                                    channel_multiplier=1))
        link(pool.tensor_copy(spread[:, :, :], spread_f[:, :, :]))
        for e in range(E):
            link(pool.memset(order[:, :, e:e + 1], float(E - e)))
        link(pool.tensor_copy(identb[:, :], ident[:, :]))
        link(pool.memset(mask_q[:, :], 0.0))
        link(pool.affine_select(out=mask_q[:, :], in_=mask_q[:, :], compare_op=ALU.is_ge, fill=MASKED, base=0,
                                pattern=[[-1, P]], channel_multiplier=1))
        link(pool.memset(mask_k[:, :], 0.0))
        link(pool.affine_select(out=mask_k[:, :], in_=mask_k[:, :], compare_op=ALU.is_ge, fill=MASKED, base=0,
                                pattern=[[1, P]], channel_multiplier=-1))
        link(pool.memset(pick_f[:, :, :, :], 0.0))
        for which, copies in ((0, (0, 1)), (1, (2,)), (2, (0, 2)), (3, (1,))):
            for c in copies:
                part = pick_f[:, which].rearrange("p a (h r d) -> p a h r d", h=2, r=4)[:, :, :, c, :]
                link(pool.affine_select(out=part, in_=part, compare_op=ALU.not_equal, fill=1.0, base=0,
                                        pattern=[[-2 * D, 4], [-D, 2], [-1, D]], channel_multiplier=1))
        link(pool.memset(v_sb[:, :, :, D:2 * D], 1.0))
        link(pool.memset(key_ones[:, :], 1.0))
        link(pool.affine_select(out=key_tmp[:, :], in_=key_ones[:, :], compare_op=ALU.is_ge, fill=0.0, base=-112,
                                pattern=[[0, 1]], channel_multiplier=1))
        for base, sign in ((-48, 1), (63, -1)):
            link(pool.affine_select(out=key_ones[:, :], in_=key_ones[:, :], compare_op=ALU.is_ge, fill=0.0,
                                    base=base, pattern=[[0, 1]], channel_multiplier=sign))
        pool.tensor_tensor(key_ones[:, :], key_ones[:, :], key_tmp[:, :], ALU.add).then_inc(consts_ready, 1)

        def add_gated(m):
            s = moe_sems[m.name]
            with pool.Fori(0, E) as e:
                for i in range(2 * NH):
                    th, k = i // KC, i % KC
                    pool.wait_ge(s["y_free"], e * 4 + i + 5)
                    pool.tensor_tensor(acc[:, k, th * HALF:(th + 1) * HALF],
                                       acc[:, k, th * HALF:(th + 1) * HALF], gated_y[:, i, :], ALU.add
                                       ).then_inc(s["gy_free"], 1)

        add_gated(L0)
        pool.wait_ge(moe_sems["l0"]["gy_free"], 2 * NH * (E + 1))
        pool.tensor_copy(pick[:, :, :, :], pick_f[:, :, :, :]).then_inc(cleared, 1)
        pool.wait_ge(moe_sems["l0"]["wlo_done"], E * L0.nf)
        pool.memset(wo_sb[:, :, :], 0.0).then_inc(cleared, 1)
        pool.memset(max_t[:, :, :, :], 0.0).then_inc(cleared, 1)
        add_gated(L1)

    @block.tensor
    def _(pe):
        done = [0]

        def three(out, pairs, start, stop):
            terms = [(wh, xh) for wh, wl, xh, xl in pairs] + [(wh, xl) for wh, wl, xh, xl in pairs] + \
                    [(wl, xh) for wh, wl, xh, xl in pairs]
            for i, (w, x) in enumerate(terms):
                last = pe.matmul(out, w, x, start=start and i == 0, stop=stop and i == len(terms) - 1)
            return last

        def layer_norm(i):
            for th in range(NH):
                for k in range(KC):
                    mm = pe.matmul(bank[th][:, :], mean_mat[:, :], acc[:, k, th * HALF:(th + 1) * HALF],
                                   start=k == 0, stop=k == KC - 1)
                mm.then_inc(ln_mean, 1)
            pe.wait_ge(ln_square, NH * (i + 1))
            for tt in range(TT):
                for k in range(KC):
                    mm = pe.matmul(bank[2][:, tt:tt + 1], squares[:, k, tt * P:(tt + 1) * P], mean_mat[:, 0:1],
                                   start=k == 0, stop=k == KC - 1)
            mm.then_inc(ln_var, 1)
            pe.wait_ge(ln_rstd, i + 1)
            for tt in range(TT):
                mm = pe.matmul(bank[3 + tt // QT][:, (tt % QT) * P:(tt % QT + 1) * P],
                               rstd[:, tt:tt + 1].to_broadcast([P, P]), ident[:, :], start=True, stop=True)
            mm.then_inc(ln_spread, 1)

        def routing(i, weights):
            for tt in range(TT):
                for k in range(KC):
                    mm = pe.matmul(bank[5][:, tt * E:(tt + 1) * E], xn[:, k, tt * P:(tt + 1) * P],
                                   weights[:, k, :], start=k == 0, stop=k == KC - 1)
            mm.then_inc(logits_done, 1)
            pe.wait_ge(gate_split, i + 1)
            for tt in range(TT):
                mm = pe.transpose(bank[6 + tt // QT][0:2 * E, (tt % QT) * P:(tt % QT + 1) * P],
                                  split_g[:, tt, :], ident[:, :])
            mm.then_inc(gate_turned, 1)
            pe.wait_ge(gate_rows, i + 1)
            for n in range(E * NH):
                e, th = n // NH, n % NH
                if n >= 2:
                    pe.wait_ge((spread_even, spread_odd)[n % 2], i * E + n // 2)
                pe.matmul(bank[6 + n % 2][:, :], spread[:, e, :], gates_t[:, th * HALF:(th + 1) * HALF],
                          start=True, stop=True).then_inc(spread_mm, 1)

        def experts(m):
            s = moe_sems[m.name]
            kinds = m.ups // KC

            def up(e, st):
                f, th = st // NH, st % NH
                if th == 0:
                    pe.wait_ge(s["wlo_done"], e * m.nf + f + 1)
                pe.wait_ge(s["up_free"], e * m.stages + st + 1)
                for kind in range(kinds):
                    mm = three(bank[2 * kind + st % 2][:, :],
                               [(w_hi[:, f, (KC * kind + k) * P:(KC * kind + k + 1) * P],
                                 w_lo[:, f, (KC * kind + k) * P:(KC * kind + k + 1) * P],
                                 x_hi[:, k, th * HALF:(th + 1) * HALF],
                                 x_lo[:, k, th * HALF:(th + 1) * HALF]) for k in range(KC)], True, True)
                mm.then_inc(s["up_done"], 1)

            def down(e, st):
                f, th = st // NH, st % NH
                if f == 0:
                    pe.wait_ge(s["y_free"], e * 4 + 2 * (th + 1))
                pe.wait_ge(s["a_ready"], e * m.stages + st + 3)
                for k in range(KC):
                    col = m.ups * P + k * P
                    mm = three(bank[4 + KC * th + k][:, :],
                               [(w_hi[:, f, col:col + P], w_lo[:, f, col:col + P],
                                 a_hi[:, st % 2, :], a_lo[:, st % 2, :])], f == 0, f == m.nf - 1)
                mm.then_inc(s["a_free"], 1)

            up(0, 0)
            with pe.Fori(0, E - 1) as e:
                for st in range(m.stages):
                    if st < m.stages - 1:
                        up(e, st + 1)
                    else:
                        up(e + 1, 0)
                    down(e, st)
            for st in range(m.stages):
                if st < m.stages - 1:
                    up(E - 1, st + 1)
                down(E - 1, st)

        for m in (L0, L1):
            pe.sem_inc(moe_sems[m.name]["a_free"], m.stages)

        pe.wait_ge(group_ready, 1)
        pe.wait_ge(gn_stats, 1)
        pe.matmul(bank[0][:, 0:KC], group_mat[:, :], small[:, 0:KC], start=True, stop=True).then_inc(gn_mean, 1)
        pe.wait_ge(gn_stats, 2)
        pe.matmul(bank[1][:, 0:KC], group_mat[:, :], small[:, KC:2 * KC], start=True, stop=True
                  ).then_inc(gn_var, 1)
        pe.wait_ge(consts_ready, 1)
        pe.wait_ge(gatew_in, 16)
        pe.wait_ge(split_done, 2)
        routing(0, gate_w)
        pe.wait_ge(spread_even, E)
        pe.wait_ge(spread_odd, E)
        experts(L0)

        pe.wait_ge(moe_sems["l0"]["gy_free"], 4 + 4 * E)
        layer_norm(0)

        pe.wait_ge(wqkv_lo_done, 1)
        pe.wait_ge(split_done, 4)
        n = 0
        for qk in range(2):
            for mt in range(KC):
                for th in range(NH):
                    if n >= 2:
                        pe.wait_ge(proj_free, n - 1)
                    col = qk * C + mt * P
                    three(bank[n % 2][:, :],
                          [(wqkv_hi[:, k, col:col + P], wqkv_lo[:, k, col:col + P],
                            x_hi[:, k, th * HALF:(th + 1) * HALF],
                            x_lo[:, k, th * HALF:(th + 1) * HALF]) for k in range(KC)],
                          True, True).then_inc(proj_mm, 1)
                    n += 1
        for tt in range(TT):
            if tt >= 2:
                pe.wait_ge(v_done, tt - 1)
            three(bank[2 + tt % 2][:, 0:C],
                  [(x_hi[:, k, tt * P:(tt + 1) * P], x_lo[:, k, tt * P:(tt + 1) * P],
                    wqkv_hi[:, k, 2 * C:3 * C], wqkv_lo[:, k, 2 * C:3 * C]) for k in range(KC)],
                  True, True).then_inc(v_mm, 1)

        stacks = [0]

        def stack(g):
            if g == 0:
                pe.wait_ge(cleared, 1)
                pe.wait_ge(proj_free, 2 * KC * NH)
            for pr in range(2):
                p = 2 * g + pr
                mt, a = p // 4, p % 4
                for qk in range(2):
                    for th in range(NH):
                        i = stacks[0]
                        if i >= 2:
                            pe.wait_ge(stack_done, i - 1)
                        for lo in range(2):
                            mm = pe.matmul(bank[4 + i % 2][:, :], pick[:, 2 * qk + lo, a, :],
                                           (qk_lo if lo else qk_hi)[:, qk, mt, th * HALF:(th + 1) * HALF],
                                           start=lo == 0, stop=lo == 1)
                        mm.then_inc(stack_mm, 1)
                        stacks[0] += 1

        smax = [0]

        def score_rows(g, j, i):
            n = smax[0]
            if n >= 2:
                pe.wait_ge(smax_done, n - 1)
            rows = slice(64 * (j % 2), 64 * (j % 2) + 64)
            keys = (i + 1) * P
            for c in range(0, keys, HALF):
                w = min(HALF, keys - c)
                out = bank[2 * (n % 2) + c // HALF]
                mm = pe.matmul(out[:, 0:w], q_st[rows, g % 2, j // 2, i * P:(i + 1) * P],
                               k_st[rows, g % 2, j // 2, c:c + w], start=True, stop=True)
            mm = pe.matmul(out[:, w - P:w], identb[:, :], mask_q[:, :], start=False, stop=True,
                           skip_group_check=True)
            mm.then_inc(smax_mm, 1)
            smax[0] += 1

        def max_rows(g):
            pe.wait_ge(maxcol_ready, g + 1)
            pe.wait_ge(smax_done, 32 * (g + 1))
            for pr in range(2):
                for tt in range(TT):
                    mm = pe.transpose(bank[2 * pr + tt // QT][:, (tt % QT) * P:(tt % QT + 1) * P],
                                      max_t[:, pr, tt, :], ident[:, :])
                mm.then_inc(maxrow_mm, 1)

        def score_cols(g, step, j):
            qb, kt = STEPS[step]
            n = (g * len(STEPS) + step) * HG + j
            if n >= 2:
                pe.wait_ge(exp_done, n - 1)
            c0 = max(0, kt - QT * qb) * P
            rows = slice(64 * (j % 2), 64 * (j % 2) + 64)
            out = bank[4 + n % 2]
            mm = pe.matmul(out[:, c0:HALF], k_st[rows, g % 2, j // 2, kt * P:(kt + 1) * P],
                           q_st[rows, g % 2, j // 2, qb * HALF + c0:(qb + 1) * HALF], start=True,
                           stop=True)
            if kt >= QT * qb:
                mm = pe.matmul(out[:, c0:c0 + P], identb[:, :], mask_k[:, :], start=False, stop=True,
                               skip_group_check=True)
            mm.then_inc(st_mm, 1)

        def values(g, step):
            qb, kt = STEPS[step]
            c0 = max(0, kt - QT * qb) * P
            if kt == 0 and g * NH + qb >= 2:
                pe.wait_ge(po_done, g * NH + qb - 1)
            pe.wait_ge(exp_done, (g * len(STEPS) + step + 1) * HG)
            for j in range(HG):
                mm = pe.matmul(bank[6 + qb][2 * D * j:2 * D * (j + 1), c0:HALF],
                               v_sb[:, kt, HG * g + j, :], probs[:, (step % 2) * HG + j, c0:HALF],
                               start=kt == 0, stop=kt == QT * (qb + 1) - 1)
            mm.then_inc(pv_done, 1)

        tiles = [(j, i) for j in range(HG) for i in range(TT)]
        pe.wait_ge(v_done, TT)
        stack(0)
        pe.wait_ge(stack_done, 8)
        for j, i in tiles:
            score_rows(0, j, i)
        for g in range(GROUPS):
            if g + 1 < GROUPS:
                stack(g + 1)
            max_rows(g)
            pe.wait_ge(qmax_done, 4 * (g + 1))
            pe.wait_ge(stack_done, 8 * min(g + 2, GROUPS))
            todo = list(tiles) if g + 1 < GROUPS else []
            for step in range(len(STEPS)):
                for j in range(HG):
                    score_cols(g, step, j)
                for _ in range(3):
                    if todo:
                        score_rows(g + 1, *todo.pop(0))
                if step:
                    values(g, step - 1)
            values(g, len(STEPS) - 1)

        pe.wait_ge(po_done, GROUPS * NH)
        pe.wait_ge(wo_in, 16 * (HG + 1))
        for n in range(KC * NH):
            th, k = n // KC, n % KC
            for g in range(GROUPS):
                mm = pe.matmul(bank[n][:, :], wo_sb[:, g, k * P:(k + 1) * P],
                               o_sb[:, g, th * HALF:(th + 1) * HALF], start=g == 0, stop=g == GROUPS - 1)
            mm.then_inc(wo_mm, 1)

        pe.wait_ge(attn_added, KC * NH)
        layer_norm(1)
        pe.wait_ge(routerw_in, 16)
        pe.wait_ge(split_done, 6)
        routing(1, router_w)
        pe.wait_ge(spread_even, 2 * E)
        pe.wait_ge(spread_odd, 2 * E)
        experts(L1)

    @block.scalar
    def _(act):
        def layer_norm(i):
            for th in range(NH):
                c = slice(th * HALF, (th + 1) * HALF)
                act.wait_ge(ln_center, NH * i + th + 1)
                act.activation(squares[:, :, c], xn[:, :, c], ACT.Square).then_inc(ln_square, 1)
            act.wait_ge(ln_var, i + 1)
            act.activation(small[:, 8:8 + TT], bank[2][:, 0:TT], ACT.Sqrt, bias=eps[:, 0:1]).then_inc(ln_std, 1)

        def exp_logits(i):
            act.wait_ge(logits_centred, i + 1)
            act.activation(rt[:, 1], rt[:, 0], ACT.Exp).then_inc(logits_exp, 1)

        def spread_gates(i):
            for e in range(E):
                act.wait_ge(spread_mm, i * E * NH + NH * e + 1)
                act.activation(gates[:, e, 0:HALF], bank[6][:, :], ACT.Copy).then_inc(spread_even, 1)

        def split_hi(m, e, f):
            s = moe_sems[m.name]
            act.wait_ge(s[f"staged{f // m.per_chunk}"], m.staged * (e + 1))
            act.wait_ge(s["a_free"], e * m.stages + NH * (f + 1))
            for dst, src in slot_parts(m, f, w_hi):
                ins = act.activation(dst, src, ACT.Copy)
            ins.then_inc(s["whi_done"], 1)

        def experts(m):
            s = moe_sems[m.name]

            def stage(e, st):
                act.wait_ge(s["up_done"], e * m.stages + st + 1)
                if m.gated:
                    act.wait_ge(s["up_free"], e * m.stages + st + 1)
                    act.activation(sil[:, st % 2, :], bank[st % 2][:, :], ACT.Silu
                                   ).then_inc(s["sil_done"], 1)
                else:
                    act.wait_ge(s["a_ready"], e * m.stages + st + 1)
                    act.activation(prod[:, st % 2, :], bank[st % 2][:, :], ACT.Gelu
                                   ).then_inc(s["up_free"], 1)

            def expert(e, more):
                for st in range(m.stages):
                    stage(e, st)
                    if st == 1:
                        split_hi(m, e, m.nf - 1)
                    elif st % 2 and more:
                        split_hi(m, e + 1, (st - 3) // 2)

            with act.Fori(0, E - 1) as e:
                expert(e, True)
            expert(E - 1, False)

        act.wait_ge(group_ready, 1)
        act.wait_ge(gn_var, 1)
        act.activation(small[:, 8:8 + KC], bank[1][:, 0:KC], ACT.Sqrt, bias=eps[:, 0:1]).then_inc(gn_std, 1)
        exp_logits(0)
        for f in range(L0.nf - 1):
            split_hi(L0, 0, f)
        spread_gates(0)
        experts(L0)

        layer_norm(0)
        act.wait_ge(attn_in, 16 * (2 * KC + 2))
        act.activation(wqkv_hi[:, :, :], wqkv[:, :, :], ACT.Copy).then_inc(wqkv_hi_done, 1)
        n = 0
        for qk in range(2):
            for mt in range(KC):
                for th in range(NH):
                    act.wait_ge(proj_mm, n + 1)
                    act.activation(qk_hi[:, qk, mt, th * HALF:(th + 1) * HALF], bank[n % 2][:, :],
                                   ACT.Identity, bias=bqk[:, qk, mt:mt + 1]).then_inc(proj_hi, 1)
                    n += 1

        def stack(g):
            for n in range(8):
                pr, qk, th = n // 4, n // 2 % 2, n % 2
                i = 8 * g + n
                act.wait_ge(stack_mm, i + 1)
                if g >= 2 and n == 0:
                    act.wait_ge(pv_done, len(STEPS) * (g - 1))
                dst = (k_st if qk else q_st)[:, g % 2, pr, th * HALF:(th + 1) * HALF]
                if qk:
                    act.activation(dst, bank[4 + i % 2][:, :], ACT.Identity, bias=key_ones[:, 0:1]
                                   ).then_inc(stack_done, 1)
                else:
                    act.activation(dst, bank[4 + i % 2][:, :], ACT.Copy).then_inc(stack_done, 1)

        act.wait_ge(consts_ready, 1)
        stack(0)
        for g in range(GROUPS):
            if g + 1 < GROUPS:
                stack(g + 1)
            for step, (qb, kt) in enumerate(STEPS):
                c0 = max(0, kt - QT * qb) * P
                for j in range(HG):
                    n = (g * len(STEPS) + step) * HG + j
                    act.wait_ge(st_mm, n + 1)
                    if j == 0 and g * len(STEPS) + step >= 2:
                        act.wait_ge(pv_done, g * len(STEPS) + step - 1)
                    act.activation(probs[:, (step % 2) * HG + j, c0:HALF], bank[4 + n % 2][:, c0:HALF],
                                   ACT.Exp, scale=float(C) ** -0.5).then_inc(exp_done, 1)

        layer_norm(1)
        act.wait_ge(wo_mm, KC * NH)
        exp_logits(1)
        for f in range(L1.nf - 1):
            split_hi(L1, 0, f)
        spread_gates(1)
        experts(L1)

    @block.vector
    def _(dve):
        n_link = [0]

        def link(ins):
            n_link[0] += 1
            ins.then_inc(dve_step, 1)
            dve.wait_ge(dve_step, n_link[0])

        def f32(ap):
            return ap.bitcast(F32)

        def split_x():
            for th in range(NH):
                c = slice(th * HALF, (th + 1) * HALF)
                link(dve.tensor_copy(x_hi[:, :, c], xn[:, :, c]))
                dve.tensor_tensor(x_lo[:, :, c], xn[:, :, c], f32(x_hi[:, :, c]), ALU.subtract
                                  ).then_inc(split_done, 1)

        def layer_norm(i):
            for th in range(NH):
                c = slice(th * HALF, (th + 1) * HALF)
                dve.wait_ge(ln_mean, NH * i + th + 1)
                for k in range(KC):
                    ins = dve.tensor_tensor(xn[:, k, c], acc[:, k, c], bank[th][:, :], ALU.subtract)
                ins.then_inc(ln_center, 1)
            dve.wait_ge(ln_std, i + 1)
            dve.reciprocal(rstd[:, :], small[:, 8:8 + TT]).then_inc(ln_rstd, 1)
            dve.wait_ge(ln_center, NH * (i + 1))
            dve.wait_ge(ln_spread, i + 1)
            for th in range(NH):
                c = slice(th * HALF, (th + 1) * HALF)
                for k in range(KC):
                    link(dve.tensor_tensor(xn[:, k, c], xn[:, k, c], bank[3 + th][:, :], ALU.mult))
            split_x()

        def over(col):
            return col.unsqueeze(2).to_broadcast([P, TT, E])

        def routing(i, first_of_ties):
            logits = bank[5][:, 0:TT * E].rearrange("p (t e) -> p t e", e=E)
            dve.wait_ge(logits_done, i + 1)
            link(dve.tensor_reduce(rs[:, 0], logits, AX_X, ALU.max))
            dve.tensor_tensor(rt[:, 0], logits, over(rs[:, 0]), ALU.subtract).then_inc(logits_centred, 1)
            dve.wait_ge(logits_exp, i + 1)
            link(dve.tensor_reduce(rs[:, 1], rt[:, 1], AX_X, ALU.add))
            link(dve.reciprocal(rs[:, 2], rs[:, 1]))
            link(dve.tensor_tensor(rt[:, 2], rt[:, 1], over(rs[:, 2]), ALU.mult))

            def top(values, value, hot, tmp):
                link(dve.tensor_reduce(value, values, AX_X, ALU.max))
                link(dve.tensor_tensor(hot, values, over(value), ALU.is_equal))
                if first_of_ties:
                    link(dve.tensor_tensor(tmp, hot, order[:, :, :], ALU.mult))
                    link(dve.tensor_reduce(rs[:, 8], tmp, AX_X, ALU.max))
                    link(dve.tensor_tensor(hot, tmp, over(rs[:, 8]), ALU.is_equal))

            top(rt[:, 2], rs[:, 3], rt[:, 3], rt[:, 4])
            if first_of_ties:
                link(dve.scalar_tensor_tensor(out=rt[:, 5], in0=rt[:, 3], scalar=-2.0, in1=rt[:, 2],
                                              op0=ALU.mult, op1=ALU.add))
            else:
                link(dve.tensor_tensor(rt[:, 4], rt[:, 2], rt[:, 3], ALU.mult))
                link(dve.tensor_tensor(rt[:, 5], rt[:, 2], rt[:, 4], ALU.subtract))
            top(rt[:, 5], rs[:, 4], rt[:, 6], rt[:, 4])
            link(dve.tensor_tensor(rs[:, 5], rs[:, 3], rs[:, 4], ALU.add))
            link(dve.reciprocal(rs[:, 6], rs[:, 5]))
            link(dve.tensor_tensor(rs[:, 7], rs[:, 6], rs[:, 3], ALU.mult))
            link(dve.tensor_tensor(rs[:, 9], rs[:, 6], rs[:, 4], ALU.mult))
            link(dve.tensor_tensor(rt[:, 7], rt[:, 3], over(rs[:, 7]), ALU.mult))
            link(dve.tensor_tensor(rt[:, 8], rt[:, 6], over(rs[:, 9]), ALU.mult))
            link(dve.tensor_tensor(rt[:, 9], rt[:, 7], rt[:, 8], ALU.add))
            link(dve.tensor_copy(split_g[:, :, 0:E].bitcast(F32R), rt[:, 9]))
            dve.tensor_tensor(split_g[:, :, E:2 * E].bitcast(F32R), rt[:, 9], split_g[:, :, 0:E],
                              ALU.subtract).then_inc(gate_split, 1)
            dve.wait_ge(gate_turned, i + 1)
            for h in range(NH):
                ins = dve.tensor_copy(gates_t[:, h * HALF:(h + 1) * HALF], bank[6 + h][0:2 * E, :])
            ins.then_inc(gate_rows, 1)

        def spread_gates(i):
            for e in range(E):
                dve.wait_ge(spread_mm, i * E * NH + NH * e + 2)
                dve.tensor_copy(gates[:, e, HALF:T], bank[7][:, :]).then_inc(spread_odd, 1)

        def split_lo(m, e, f):
            s = moe_sems[m.name]
            dve.wait_ge(s["whi_done"], e * m.nf + f + 1)
            for (hi, src), (lo, _) in zip(slot_parts(m, f, w_hi), slot_parts(m, f, w_lo)):
                ins = dve.tensor_tensor(lo, src, f32(hi), ALU.subtract)
            ins.then_inc(s["wlo_done"], 1)

        def experts(m):
            s = moe_sems[m.name]

            def stage(e, st):
                n = e * m.stages + st
                b = st % 2
                if m.gated:
                    dve.wait_ge(s["sil_done"], n + 1)
                    dve.tensor_tensor(prod[:, b, :], sil[:, b, :], bank[2 + b][:, :], ALU.mult
                                      ).then_inc(s["up_free"], 1)
                dve.wait_ge(s["up_free"], n + 3)
                dve.wait_ge(s["a_free"], n - 1 + m.stages)
                dve.tensor_copy(a_hi[:, b, :], prod[:, b, :]).then_inc(s["a_hi_done"], 1)
                dve.wait_ge(s["a_hi_done"], n + 1)
                dve.tensor_tensor(a_lo[:, b, :], prod[:, b, :], f32(a_hi[:, b, :]), ALU.subtract
                                  ).then_inc(s["a_ready"], 1)

            def expert(e, more):
                for st in range(m.stages):
                    stage(e, st)
                    if st == 1:
                        split_lo(m, e, m.nf - 1)
                    elif st % 2 and more:
                        split_lo(m, e + 1, (st - 3) // 2)
                for i in range(2 * NH):
                    th, k = i // KC, i % KC
                    dve.wait_ge(s["a_free"], e * m.stages + m.stages - 1 + th + m.stages)
                    dve.wait_ge(s["gy_free"], e * 4 + i + 1)
                    dve.tensor_tensor(gated_y[:, i:i + 1, :], gates[:, bass.ds(e, 1), th * HALF:(th + 1) * HALF],
                                      bank[4 + i][:, :].unsqueeze(1), ALU.mult).then_inc(s["y_free"], 1)

            with dve.Fori(0, E - 1) as e:
                expert(e, True)
            expert(E - 1, False)

        for m in (L0, L1):
            s = moe_sems[m.name]
            dve.sem_inc(s["up_free"], 2)
            dve.sem_inc(s["a_ready"], 2)
            dve.sem_inc(s["y_free"], 4)

        dve.wait_ge(x_in, 16 * KC)
        for k in range(KC):
            for th in range(NH):
                link(dve.bn_stats(stats[:, k, th, :], acc[:, k, th * HALF:(th + 1) * HALF]))
            link(dve.bn_aggr(small[:, 4 + 2 * k:6 + 2 * k], stats[:, k, :, :]))
        mv = small[:, 4:8].rearrange("p (k s) -> p s k", s=2)
        mean, dev, square = small[:, 16:16 + KC], small[:, 18:18 + KC], small[:, 20:20 + KC]
        inv = small[:, 22:22 + KC]
        dve.tensor_copy(small[:, 0:KC], mv[:, 0, :]).then_inc(gn_stats, 1)
        dve.wait_ge(gn_mean, 1)
        link(dve.tensor_copy(mean, bank[0][:, 0:KC]))
        link(dve.tensor_tensor(dev, mv[:, 0, :], mean, ALU.subtract))
        link(dve.tensor_tensor(square, dev, dev, ALU.mult))
        dve.tensor_tensor(small[:, KC:2 * KC], square, mv[:, 1, :], ALU.add).then_inc(gn_stats, 1)
        dve.wait_ge(gn_std, 1)
        link(dve.reciprocal(inv, small[:, 8:8 + KC]))
        for k in range(KC):
            link(dve.tensor_scalar(xn[:, k, :], acc[:, k, :], mean[:, k:k + 1], inv[:, k:k + 1],
                                   ALU.subtract, ALU.mult))
        split_x()
        routing(0, False)
        for f in range(L0.nf - 1):
            split_lo(L0, 0, f)
        spread_gates(0)
        experts(L0)

        layer_norm(0)
        dve.wait_ge(wqkv_hi_done, 1)
        dve.tensor_tensor(wqkv_lo[:, :, :], wqkv[:, :, :], f32(wqkv_hi[:, :, :]), ALU.subtract
                          ).then_inc(wqkv_lo_done, 1)
        n = 0
        for qk in range(2):
            for mt in range(KC):
                for th in range(NH):
                    c = slice(th * HALF, (th + 1) * HALF)
                    dve.wait_ge(proj_hi, n + 1)
                    dve.scalar_tensor_tensor(out=qk_lo[:, qk, mt, c], in0=bank[n % 2][:, :],
                                             scalar=bqk[:, qk, mt:mt + 1], in1=f32(qk_hi[:, qk, mt, c]),
                                             op0=ALU.add, op1=ALU.subtract).then_inc(proj_free, 1)
                    n += 1
        for tt in range(TT):
            dve.wait_ge(v_mm, tt + 1)
            dve.tensor_tensor(v_sb[:, tt, :, 0:D], bank[2 + tt % 2][:, 0:C].rearrange("p (h d) -> p h d", d=D),
                              bv[:, :].rearrange("p (h d) -> p h d", d=D), ALU.add).then_inc(v_done, 1)

        def row_max(g, j, i):
            n = (g * HG + j) * TT + i
            dve.wait_ge(smax_mm, n + 1)
            keys = (i + 1) * P
            out = maxes[:, g % 2, j, i:i + 1]
            b = 2 * (n % 2) * HALF
            dve.tensor_reduce(out, banks[:, b:b + keys], AX_X, ALU.max).then_inc(smax_done, 1)

        def store_max(g):
            dve.wait_ge(smax_done, HG * TT * (g + 1))
            if g == 0:
                dve.wait_ge(cleared, 3)
            else:
                dve.wait_ge(maxrow_mm, 2 * g)
            for pr in range(2):
                top = maxes[:, g % 2, 2 * pr:2 * pr + 2, :].rearrange("p j t -> p t j")
                cols = max_t[:, pr].rearrange("p t (j c) -> p t j c", j=2)
                hi, lo = cols[:, :, :, 3 * D], cols[:, :, :, 3 * D + 1]
                link(dve.tensor_scalar(hi.bitcast(F32R), top, -1.0, None, ALU.mult))
                ins = dve.scalar_tensor_tensor(out=lo.bitcast(F32R), in0=top, scalar=-1.0, in1=hi,
                                               op0=ALU.mult, op1=ALU.subtract)
            ins.then_inc(maxcol_ready, 1)
            for pr in range(2):
                dve.wait_ge(maxrow_mm, 2 * g + pr + 1)
                for th in range(NH):
                    rows = q_st[:, g % 2, pr, th * HALF:(th + 1) * HALF]
                    dve.tensor_tensor(rows, f32(rows), bank[2 * pr + th][:, :], ALU.add).then_inc(qmax_done, 1)

        def output(g, qb):
            dve.wait_ge(pv_done, len(STEPS) * g + QT * (qb + 1) + (QT if qb else 0))
            po = bank[6 + qb][:, :]
            link(dve.stream_shuffle(sums[:, :], po, [D + r % D for r in range(2 * D)]))
            link(dve.reciprocal(rsum[:, :], sums[:, :]))
            dve.tensor_tensor(o_sb[:, g, qb * HALF:(qb + 1) * HALF], po, rsum[:, :], ALU.mult
                              ).then_inc(po_done, 1)

        tiles = [(j, i) for j in range(HG) for i in range(TT)]
        for j, i in tiles:
            row_max(0, j, i)
        for g in range(GROUPS):
            store_max(g)
            todo = list(tiles) if g + 1 < GROUPS else []
            for j, i in todo[:15]:
                row_max(g + 1, j, i)
            output(g, 0)
            for j, i in todo[15:]:
                row_max(g + 1, j, i)
            output(g, 1)
        for n in range(KC * NH):
            th, k = n // KC, n % KC
            dve.wait_ge(wo_mm, n + 1)
            c = slice(th * HALF, (th + 1) * HALF)
            dve.tensor_tensor(acc[:, k, c], acc[:, k, c], bank[n][:, :], ALU.add).then_inc(attn_added, 1)

        dve.wait_ge(attn_added, KC * NH)
        layer_norm(1)
        routing(1, True)
        for f in range(L1.nf - 1):
            split_lo(L1, 0, f)
        spread_gates(1)
        experts(L1)

    ctx.close()


def kernel(x, L0_conv_gate_w, L0_conv_w1, L0_conv_w3, L0_conv_w2, L1_attn_Wqkv, L1_attn_bqkv, L1_attn_Wo,
           L1_attn_bo, L1_ffn_router_w, L1_ffn_w1, L1_ffn_w2):
    import numpy as np
    import concourse.bacc as bacc
    from concourse.bass_utils import run_bass_kernel_spmd

    nc = bacc.Bacc("TRN2", target_bir_lowering=False, num_devices=1)
    x = np.asarray(x)
    named = [
        ("xT", np.ascontiguousarray(x.reshape(T, C).T)),
        ("gate_w", np.ascontiguousarray(L0_conv_gate_w)),
        ("w1", np.ascontiguousarray(L0_conv_w1)),
        ("w3", np.ascontiguousarray(L0_conv_w3)),
        ("w2", np.ascontiguousarray(L0_conv_w2)),
        ("Wqkv", np.ascontiguousarray(L1_attn_Wqkv)),
        ("bqkv", np.ascontiguousarray(L1_attn_bqkv)),
        ("Wo", np.ascontiguousarray(L1_attn_Wo)),
        ("bo", np.ascontiguousarray(L1_attn_bo)),
        ("router_wT", np.ascontiguousarray(np.asarray(L1_ffn_router_w).T)),
        ("ffn_w1", np.ascontiguousarray(L1_ffn_w1)),
        ("ffn_w2", np.ascontiguousarray(L1_ffn_w2)),
    ]
    arrays, args = {}, []
    for name, a in named:
        arrays[f"in_{name}"] = a
        args.append(nc.dram_tensor(f"in_{name}", a.shape, mybir.dt.from_np(a.dtype), kind="ExternalInput").ap())
    args.append(nc.dram_tensor("outT", (C, T), F32, kind="ExternalOutput").ap())
    build(nc, *args)
    r = run_bass_kernel_spmd(nc, [arrays], core_ids=[0])
    outT = r.results[0]["outT"]
    return np.ascontiguousarray(outT.T).reshape(x.shape)
```

```python
from contextlib import ExitStack

import concourse.bass as bass
from concourse import mybir

F32 = mybir.dt.float32
F32R = mybir.dt.float32r
F16 = mybir.dt.float16
I32 = mybir.dt.int32
U32 = mybir.dt.uint32
BF16 = mybir.dt.bfloat16
ALU = mybir.AluOpType
ACT = mybir.ActivationFunctionType
AX_X = mybir.AxisListType.X

P = 128
T = 1024
C = 256
KC = C // P
TT = T // P
HALF = 512
NH = T // HALF
E = 8
GROUP = 8
HEADS = 16
D = C // HEADS
PAIRS = HEADS // 2
HG = 4
GROUPS = HEADS // HG
QT = HALF // P
MASKED = -1e30
NB = 3 * P
NT = NB // P
BLOCKS = -(-T // NB)
ROW = C + E
GN_EPS = LN_EPS = 1e-5


class Moe:

    def __init__(self, name, f, gated):
        self.name, self.gated = name, gated
        self.nf = f // P
        self.ups = KC * (2 if gated else 1)
        self.per_chunk = self.nf // 2
        self.cols = self.ups * P + C
        self.staged = 16 * (3 if gated else 2)


STEPS = [(qb, kt) for qb in range(NH) for kt in range(QT * (qb + 1))]


def build(nc, x_d, xT_d, gate_d, w1_d, w3_d, w2_d, wqkv_d, bqkv_d, wo_d, bo_d, router_d, v1_d, v2_d, rows0_d, res0_d, rows1_d, res1_d):
    L0 = Moe("l0", w1_d.shape[2], True)
    L1 = Moe("l1", v1_d.shape[1] // E, False)

    def at(name, shape, dt, offset):
        return nc.alloc_sbuf_tensor_at(name, shape, dt, offset=offset)

    cursor = [16512]

    def place(name, shape, dt, size=4):
        offset = cursor[0]
        n = size
        for s in shape[1:]:
            n *= s
        cursor[0] += (n + 31) // 32 * 32
        return at(name, shape, dt, offset), offset

    w_hi, WHI = place("w_hi", [P, L0.nf, 768], F32R)
    w_lo, WLO = place("w_lo", [P, L0.nf, 768], F32R)
    stage0, STG = place("stage0", [P, 2, L0.per_chunk * L0.cols], F32)
    xT, XT = place("xT", [P, KC, T], F32)
    xnT, XNT = place("xnT", [P, KC, T], F32)
    rows, _ = place("rows", [P, TT, ROW], F32)
    tok, _ = place("tok", [P, TT, C], F32)
    got, EXP = place("got", [P, 2, NT, ROW], F32)
    xg_hi, XG = place("xg_hi", [P, 2, KC, NB], F32R)
    xg_lo, _ = place("xg_lo", [P, 2, KC, NB], F32R)
    hot, _ = place("hot", [P, TT, NB], F16, 2)
    sil, _ = place("sil", [P, 2, NB], F32)
    prod, _ = place("prod", [P, 2, NB], F32)
    a_hi, _ = place("a_hi", [P, 2, NB], F32R)
    a_lo, _ = place("a_lo", [P, 2, NB], F32R)
    gated_y, _ = place("gated_y", [P, 2, NT, C], F32)
    got_o, _ = place("got_o", [P, NT, ROW], F32)
    xo_hi, _ = place("xo_hi", [P, KC, NB], F32R)
    xo_lo, _ = place("xo_lo", [P, KC, NB], F32R)
    hot_o, _ = place("hot_o", [P, TT, NB], F16, 2)
    gated_o, EXP_END = place("gated_o", [P, NT, C], F32)
    ident, _ = place("ident", [P, P], F32)
    identb, _ = place("identb", [P, P], BF16, 2)
    mask_q, _ = place("mask_q", [P, P], BF16, 2)
    mask_k, _ = place("mask_k", [P, P], BF16, 2)
    group_mat, _ = place("group_mat", [P, P], F32)
    before, _ = place("before", [P, P], BF16, 2)
    ones, _ = place("ones", [P, P], BF16, 2)
    places, _ = place("places", [P, BLOCKS * NB], F16, 2)
    token_of, _ = place("token_of", [P, TT, 2], F16, 2)
    spare_row, _ = place("spare_row", [P, NT], F32)
    sel, _ = place("sel", [P, TT, E], BF16, 2)
    pos, _ = place("pos", [P, TT, E], F32)
    count, _ = place("count", [P, E], I32)
    extra, _ = place("extra", [P, E], F32)
    extra2, _ = place("extra2", [P, E], F32)
    earlier, _ = place("earlier", [P, E, E], F32)
    extra_of, _ = place("extra_of", [P, E, E], F32)
    ran_before, _ = place("ran_before", [P, E], I32)
    found, _ = place("found", [P, 2, NT, 2], F32)
    found_o, _ = place("found_o", [P, NT, 2], F32)
    from_row, _ = place("from_row", [P, 2, NT], U32)
    to_row, _ = place("to_row", [P, 2, NT], U32)
    from_row_o, _ = place("from_row_o", [P, NT], U32)
    to_row_o, _ = place("to_row_o", [P, NT], U32)
    missing, _ = place("missing", [P, 2, NT], F32)
    gate_w, _ = place("gate_w", [P, KC, E], F32)
    router_w, _ = place("router_w", [P, KC, E], F32)
    stats, _ = place("stats", [P, KC, NH, 6], F32)
    small, _ = place("small", [P, 32], F32)
    tok_stats, _ = place("tok_stats", [P, TT, 6], F32)
    tok_mv, _ = place("tok_mv", [P, TT, 2], F32)
    std, _ = place("std", [P, TT], F32)
    rstd, _ = place("rstd", [P, TT], F32)
    rt, _ = place("rt", [P, 10, TT, E], F32)
    rs, _ = place("rs", [P, 10, TT], F32)
    order, _ = place("order", [P, TT, E], F32)
    eps, _ = place("eps", [P, 1], F32)
    bqk, _ = place("bqk", [P, 2, KC], F32)
    bv, _ = place("bv", [P, C], F32)
    key_ones, _ = place("key_ones", [P, 1], F32)
    key_tmp, _ = place("key_tmp", [P, 1], F32)
    v_sb, _ = place("v_sb", [P, TT, HEADS, 2 * D], F32)
    probs, PROBS = place("probs", [P, 2 * HG, HALF], F32)
    assert cursor[0] <= nc.sbuf_usable_end

    x_hi = at("x_hi", [P, KC, T], F32R, XT)
    x_lo = at("x_lo", [P, KC, T], F32R, XNT)
    stage1 = at("stage1", [P, 2, L1.per_chunk * L1.cols], F32, STG)
    q_st = at("q_st", [P, 2, 2, T], F32R, WHI)
    k_st = at("k_st", [P, 2, 2, T], F32R, WHI + 16384)
    o_sb = at("o_sb", [P, GROUPS, T], F32, WHI + 32768)
    max_t = at("max_t", [P, 2, TT, P], F32, STG + 8192)
    wo_sb = at("wo_sb", [P, GROUPS, C], F32, STG + 16384)
    qk_hi = at("qk_hi", [P, 2, KC, T], F32R, EXP)
    qk_lo = at("qk_lo", [P, 2, KC, T], F32R, EXP + 16384)
    wqkv_hi = at("wqkv_hi", [P, KC, 3 * C], F32R, EXP + 32768)
    wqkv_lo = at("wqkv_lo", [P, KC, 3 * C], F32R, EXP + 38912)
    pick = at("pick", [P, 4, 4, P], F32R, EXP + 45056)
    sums = at("sums", [P, HALF], F32, EXP + 53248)
    rsum = at("rsum", [P, HALF], F32, EXP + 55296)
    maxes = at("maxes", [P, 2, HG, TT], F32, EXP + 57344)
    assert EXP + 57600 <= EXP_END + NT * C * 4
    wqkv = at("wqkv", [P, KC, 3 * C], F32, PROBS)
    pick_f = at("pick_f", [P, 4, 4, P], F32, PROBS + 6144)

    ctx = ExitStack()
    banks = ctx.enter_context(nc.psum_tensor("banks", [P, 8 * HALF], F32))
    bank = [banks[:, i * HALF:(i + 1) * HALF] for i in range(8)]

    def sem(name):
        return ctx.enter_context(nc.semaphore(name))

    x_in, gatew_in, routerw_in, attn_in, wo_in = (sem(n) for n in (
        "x_in", "gatew_in", "routerw_in", "attn_in", "wo_in"))
    tok_in = [sem(f"tok{th}_in") for th in range(NH)]
    pool_step, dve_step, dma_go = sem("pool_step"), sem("dve_step"), sem("dma_go")
    act_left, dve_left = sem("act_left"), sem("dve_left")
    group_ready, spare_ready, consts_ready, cleared = (
        sem("group_ready"), sem("spare_ready"), sem("consts_ready"), sem("cleared"))
    gn_stats, gn_mean, gn_var, gn_std = sem("gn_stats"), sem("gn_mean"), sem("gn_var"), sem("gn_std")
    normed, xnT_ready, turned, rows_copied = sem("normed"), sem("xnT_ready"), sem("turned"), sem("rows_copied")
    ln_var, ln_std = sem("ln_var"), sem("ln_std")
    turned_hi, turned_lo = sem("turned_hi"), sem("turned_lo")
    logits_done, logits_centred, logits_exp = sem("logits_done"), sem("logits_centred"), sem("logits_exp")
    rows_ready, sel_ready, ranked, counts_ready, ran_ready = (
        sem("rows_ready"), sem("sel_ready"), sem("ranked"), sem("counts_ready"), sem("ran_ready"))
    moe_sems = {}
    for m in (L0, L1):
        moe_sems[m.name] = {n: sem(f"{m.name}_{n}") for n in (
            "res_in", "rows_out", "staged0", "staged1", "whi_done", "wlo_done",
            "hot_ready", "found", "from_ready", "missing", "to_ready", "gathered0", "gathered1", "xt", "xhi", "xlo",
            "up_done", "sil_done", "up_free", "a_hi_done", "a_ready", "a_free", "y_done", "gy_ready",
            "added", "gy_free")}
        moe_sems[m.name].update({"o_" + n: sem(f"{m.name}_o_{n}") for n in (
            "hot_ready", "found", "from_ready", "missing", "to_ready", "gathered", "xt", "xhi", "xlo",
            "read", "written", "up_done", "sil_done", "prod_done", "a_hi_done", "a_ready", "a_free", "gy_ready", "added")})
    wqkv_hi_done, wqkv_lo_done = sem("wqkv_hi_done"), sem("wqkv_lo_done")
    proj_mm, proj_hi, proj_free = sem("proj_mm"), sem("proj_hi"), sem("proj_free")
    v_mm, v_done = sem("v_mm"), sem("v_done")
    stack_mm, stack_done = sem("stack_mm"), sem("stack_done")
    smax_mm, smax_done = sem("smax_mm"), sem("smax_done")
    maxcol_ready, maxrow_mm, qmax_done = sem("maxcol_ready"), sem("maxrow_mm"), sem("qmax_done")
    st_mm, exp_done, pv_done, po_done = sem("st_mm"), sem("exp_done"), sem("pv_done"), sem("po_done")
    wo_mm, attn_added = sem("wo_mm"), sem("attn_added")
    OB = BLOCKS - 1

    def staging(m, b):
        st = (stage0 if m.gated else stage1)[:, b, :]
        n = m.ups * m.per_chunk * P
        return (st[:, 0:n].rearrange("p (u f) -> p u f", u=m.ups),
                st[:, n:n + m.per_chunk * C].rearrange("p (f c) -> p f c", c=C))

    def load_stage(eng, m, e, b):
        s = moe_sems[m.name][f"staged{b}"]
        w = m.per_chunk * P
        ups, downs = staging(m, b)
        if m.gated:
            for i, src in enumerate((w1_d, w3_d)):
                eng.dma_start(ups[:, KC * i:KC * (i + 1), :],
                              src[bass.ds(e, 1), :, b * w:(b + 1) * w].rearrange("a (k p) f -> p (a k) f", p=P)
                              ).then_inc(s, 16)
            eng.dma_start(downs, w2_d[bass.ds(e, 1), b * w:(b + 1) * w, :].rearrange(
                "a (f p) c -> p (a f) c", p=P)).then_inc(s, 16)
        else:
            eng.dma_start(ups, v1_d.rearrange("(k p) f -> p k f", p=P)[:, :, bass.ds(e * (m.nf * P) + b * w, w)]
                          ).then_inc(s, 16)
            eng.dma_start(downs, v2_d[bass.ds(e * (m.nf * P) + b * w, w), :].rearrange("(f p) c -> p f c", p=P)
                          ).then_inc(s, 16)

    def slot_parts(m, f, buf):
        ups, downs = staging(m, f // m.per_chunk)
        i = f % m.per_chunk
        n = m.ups * P
        return ((buf[:, f, 0:n].rearrange("p (u c) -> p u c", c=P), ups[:, :, i * P:(i + 1) * P]),
                (buf[:, f, n:n + C], downs[:, i, :]))

    def branch(eng, m, e, work, signals):
        tokens = eng.value_load(count[0:1, bass.ds(e, 1)], min_val=0, max_val=T)
        for b in range(1, BLOCKS):
            with eng.If(tokens > b * NB):
                work(b)
            with eng.Else():
                for name, n in signals:
                    eng.sem_inc(moe_sems[m.name][name], n)

    block = ctx.enter_context(nc.Block())

    @block.sync
    def _(sp):
        s0, s1 = moe_sems["l0"], moe_sems["l1"]
        for k in range(KC):
            sp.dma_start(xT[:, k, :], xT_d[k * P:(k + 1) * P, :]).then_inc(x_in, 16)
        sp.dma_start(gate_w[:, :, :], gate_d.rearrange("(k p) e -> p k e", p=P)).then_inc(gatew_in, 16)
        load_stage(sp, L0, 0, 0)
        sp.dma_start(res0_d[0:T, :], x_d).then_inc(s0["res_in"], 16)
        load_stage(sp, L0, 0, 1)
        sp.wait_ge(spare_ready, 1)
        for d, s in ((res0_d, s0), (res1_d, s1)):
            sp.dma_start(d[T:T + NB, :].rearrange("(t p) c -> p t c", p=P), gated_o[:, :, :]
                         ).then_inc(s["res_in"], 16)
        sp.dma_start(router_w[:, :, :], router_d.rearrange("(k p) e -> p k e", p=P)).then_inc(routerw_in, 16)
        for i in range(2):
            for k in range(KC):
                lo = i * C + k * P
                sp.dma_start(bqk[:, i, k:k + 1], bqkv_d[lo:lo + P].rearrange("(p a) -> p a", a=1)
                             ).then_inc(attn_in, 16)
        sp.dma_start(bv[:, :], bqkv_d[2 * C:3 * C].partition_broadcast(P)).then_inc(attn_in, 16)
        sp.dma_start(wqkv[:, :, :], wqkv_d.rearrange("(k p) n -> p k n", p=P)).then_inc(attn_in, 16)

        def store_rows(m, rows_d):
            sp.wait_ge(rows_ready, 1 + (not m.gated))
            sp.dma_start(rows_d.rearrange("(t p) c -> p t c", p=P), rows[:, :, :]
                         ).then_inc(moe_sems[m.name]["rows_out"], 16)

        store_rows(L0, rows0_d)
        with sp.Fori(1, E) as e:
            for b in range(2):
                sp.wait_ge(s0["wlo_done"], (e - 1) * L0.nf + (b + 1) * L0.per_chunk)
                load_stage(sp, L0, e, b)
        sp.wait_ge(s0["wlo_done"], E * L0.nf)
        for b in range(2):
            load_stage(sp, L1, 0, b)
        sp.wait_ge(s0["added"], 16 * NT * E)
        sp.wait_ge(s0["o_added"], E * OB)
        for th in range(NH):
            sp.dma_start(tok[:, QT * th:QT * (th + 1), :],
                         res0_d[th * HALF:(th + 1) * HALF, :].rearrange("(t p) c -> p t c", p=P)
                         ).then_inc(tok_in[th], 16)
        sp.wait_ge(cleared, 2)
        for j in range(HG):
            sp.dma_start(wo_sb[2 * D * j:2 * D * j + D, :, :],
                         wo_d.rearrange("(g j d) c -> j d g c", j=HG, d=D)[j]).then_inc(wo_in, 16)
        sp.dma_start(wo_sb[D:D + 1, 0, :], bo_d.rearrange("(a c) -> a c", a=1)).then_inc(wo_in, 16)
        sp.wait_ge(attn_added, TT)
        sp.dma_start(res1_d[0:T, :].rearrange("(t p) c -> p t c", p=P), tok[:, :, :]).then_inc(s1["res_in"], 16)
        store_rows(L1, rows1_d)
        with sp.Fori(1, E) as e:
            for b in range(2):
                sp.wait_ge(s1["wlo_done"], (e - 1) * L1.nf + (b + 1) * L1.per_chunk)
                load_stage(sp, L1, e, b)
        sp.wait_ge(s1["added"], 16 * NT * E)
        sp.wait_ge(s1["o_added"], E * OB)

    @block.gpsimd
    def _(pool):
        n = [0]

        def link(ins):
            n[0] += 1
            ins.then_inc(pool_step, 1)
            pool.wait_ge(pool_step, n[0])

        for m in (L0, L1):
            pool.sem_inc(moe_sems[m.name]["gy_free"], 2)
        link(pool.memset(group_mat[:, :], 1.0 / GROUP))
        grouped = group_mat[:, :].rearrange("p (g c) -> p g c", c=GROUP)
        link(pool.affine_select(out=grouped, in_=grouped, compare_op=ALU.is_ge, fill=0.0, base=0,
                                pattern=[[-GROUP, P // GROUP], [0, GROUP]], channel_multiplier=1))
        link(pool.affine_select(out=grouped, in_=grouped, compare_op=ALU.is_ge, fill=0.0, base=GROUP - 1,
                                pattern=[[GROUP, P // GROUP], [0, GROUP]], channel_multiplier=-1))
        pool.memset(eps[:, :], GN_EPS).then_inc(group_ready, 1)
        pool.memset(gated_o[:, :, :], 0.0).then_inc(spare_ready, 1)
        link(pool.memset(ident[:, :], 0.0))
        link(pool.affine_select(out=ident[:, :], in_=ident[:, :], compare_op=ALU.not_equal, fill=1.0, base=0,
                                pattern=[[-1, P]], channel_multiplier=1))
        link(pool.memset(ones[:, :], 1.0))
        link(pool.affine_select(out=before[:, :], in_=ones[:, :], compare_op=ALU.is_gt, fill=0.0, base=0,
                                pattern=[[1, P]], channel_multiplier=-1))
        link(pool.iota(places[:, :], [[1, BLOCKS * NB]], base=0, channel_multiplier=0,
                       allow_small_or_imprecise_dtypes=True))
        link(pool.memset(token_of[:, :, :], 1.0))
        link(pool.iota(token_of[:, :, 0:1], [[P, TT]], base=0, channel_multiplier=1,
                       allow_small_or_imprecise_dtypes=True))
        link(pool.iota(spare_row[:, :], [[P, NT]], base=T, channel_multiplier=1,
                       allow_small_or_imprecise_dtypes=True))
        for e in range(E):
            link(pool.memset(order[:, :, e:e + 1], float(E - e)))
        link(pool.memset(earlier[:, :, :], 1.0))
        link(pool.affine_select(out=earlier[:, :, :], in_=earlier[:, :, :], compare_op=ALU.is_gt, fill=0.0, base=0,
                                pattern=[[1, E], [-1, E]], channel_multiplier=0))
        link(pool.tensor_copy(identb[:, :], ident[:, :]))
        link(pool.memset(mask_q[:, :], 0.0))
        link(pool.affine_select(out=mask_q[:, :], in_=mask_q[:, :], compare_op=ALU.is_ge, fill=MASKED, base=0,
                                pattern=[[-1, P]], channel_multiplier=1))
        link(pool.memset(mask_k[:, :], 0.0))
        link(pool.affine_select(out=mask_k[:, :], in_=mask_k[:, :], compare_op=ALU.is_ge, fill=MASKED, base=0,
                                pattern=[[1, P]], channel_multiplier=-1))
        link(pool.memset(pick_f[:, :, :, :], 0.0))
        for which, copies in ((0, (0, 1)), (1, (2,)), (2, (0, 2)), (3, (1,))):
            for c in copies:
                part = pick_f[:, which].rearrange("p a (h r d) -> p a h r d", h=2, r=4)[:, :, :, c, :]
                link(pool.affine_select(out=part, in_=part, compare_op=ALU.not_equal, fill=1.0, base=0,
                                        pattern=[[-2 * D, 4], [-D, 2], [-1, D]], channel_multiplier=1))
        link(pool.memset(v_sb[:, :, :, D:2 * D], 1.0))
        link(pool.memset(key_ones[:, :], 1.0))
        link(pool.affine_select(out=key_tmp[:, :], in_=key_ones[:, :], compare_op=ALU.is_ge, fill=0.0, base=-112,
                                pattern=[[0, 1]], channel_multiplier=1))
        for base, sign in ((-48, 1), (63, -1)):
            link(pool.affine_select(out=key_ones[:, :], in_=key_ones[:, :], compare_op=ALU.is_ge, fill=0.0,
                                    base=base, pattern=[[0, 1]], channel_multiplier=sign))
        pool.tensor_tensor(key_ones[:, :], key_ones[:, :], key_tmp[:, :], ALU.add).then_inc(consts_ready, 1)

        def gather(m, rows_d, e, par):
            s = moe_sems[m.name]
            pool.wait_ge(s["from_ready"], e + 1)
            pool.sem_inc(dma_go, 1)
            for t in range(NT):
                pool.indirect_dma_start(got[:, par, t, :], None, rows_d,
                                        bass.IndirectOffsetOnAxis(from_row[:, par, t:t + 1], 0)
                                        ).then_inc(s[f"gathered{par}"], 16)

        def further(m, rows_d, res_d, ran, e, b):
            s = moe_sems[m.name]
            q = e * OB + b - 1
            pool.wait_ge(s["o_from_ready"], q + 1)
            pool.sem_inc(dma_go, 1)
            for t in range(NT):
                pool.indirect_dma_start(got_o[:, t, :], None, rows_d,
                                        bass.IndirectOffsetOnAxis(from_row_o[:, t:t + 1], 0)
                                        ).then_inc(s["o_read"], 16)
            pool.wait_ge(s["o_read"], 16 * NT * (ran + b))
            pool.sem_inc(s["o_gathered"], 1)
            pool.wait_ge(s["o_to_ready"], q + 1)
            pool.wait_ge(s["o_gy_ready"], q + 1)
            pool.sem_inc(dma_go, 1)
            for t in range(NT):
                pool.indirect_dma_start(res_d, bass.IndirectOffsetOnAxis(to_row_o[:, t:t + 1], 0),
                                        gated_o[:, t, :], None, compute_op=ALU.add
                                        ).then_inc(s["o_written"], 16)
            pool.wait_ge(s["o_written"], 16 * NT * (ran + b))
            pool.sem_inc(s["o_added"], 1)

        def experts(m, rows_d, res_d):
            s = moe_sems[m.name]

            def expert(e, par, more):
                ran = pool.value_load(ran_before[0:1, bass.ds(e, 1)], min_val=0, max_val=E * OB)
                branch(pool, m, e, lambda b: further(m, rows_d, res_d, ran, e, b),
                       (("o_gathered", 1), ("o_added", 1)))
                if more:
                    gather(m, rows_d, e + 1, 1 - par)
                pool.wait_ge(s["to_ready"], e + 1)
                pool.wait_ge(s["gy_ready"], e + 2)
                pool.sem_inc(dma_go, 1)
                for t in range(NT):
                    pool.indirect_dma_start(res_d, bass.IndirectOffsetOnAxis(to_row[:, par, t:t + 1], 0),
                                            gated_y[:, par, t, :], None, compute_op=ALU.add
                                            ).then_inc(s["added"], 16)
                pool.wait_ge(s["added"], 16 * NT * (e + 1))
                pool.sem_inc(s["gy_free"], 1)

            pool.wait_ge(s["rows_out"], 16)
            pool.wait_ge(s["res_in"], 32)
            if m.gated:
                pool.wait_ge(moe_sems["l1"]["res_in"], 16)
            gather(m, rows_d, 0, 0)
            pool.wait_ge(ran_ready, 1 + (not m.gated))
            with pool.Fori(0, E // 2 - 1) as pair:
                e = 2 * pair
                expert(e, 0, True)
                expert(e + 1, 1, True)
            expert(E - 2, 0, True)
            expert(E - 1, 1, False)

        experts(L0, rows0_d, res0_d)
        pool.wait_ge(moe_sems["l0"]["wlo_done"], E * L0.nf)
        pool.tensor_copy(pick[:, :, :, :], pick_f[:, :, :, :]).then_inc(cleared, 1)
        pool.memset(wo_sb[:, :, :], 0.0).then_inc(cleared, 1)
        pool.memset(max_t[:, :, :, :], 0.0).then_inc(cleared, 1)
        experts(L1, rows1_d, res1_d)

    @block.tensor
    def _(pe):
        done = [0]

        def three(out, pairs, start, stop):
            terms = [(wh, xh) for wh, wl, xh, xl in pairs] + [(wh, xl) for wh, wl, xh, xl in pairs] + \
                    [(wl, xh) for wh, wl, xh, xl in pairs]
            for i, (w, x) in enumerate(terms):
                last = pe.matmul(out, w, x, start=start and i == 0, stop=stop and i == len(terms) - 1)
            return last

        def rank(i, weights):
            for tt in range(TT):
                for k in range(KC):
                    mm = pe.matmul(bank[7][:, tt * E:(tt + 1) * E], xnT[:, k, tt * P:(tt + 1) * P],
                                   weights[:, k, :], start=k == 0, stop=k == KC - 1)
            mm.then_inc(logits_done, 1)
            pe.wait_ge(sel_ready, i + 1)
            pe.matmul(bank[6][:, 0:TT * E], before[:, :], sel[:, :, :], start=True, stop=True)
            for d in range(1, TT):
                pe.matmul(bank[6][:, d * E:TT * E], ones[:, :], sel[:, 0:TT - d, :], start=False, stop=True,
                          skip_group_check=True)
            for tt in range(TT):
                mm = pe.matmul(bank[5][:, 0:E], ones[:, :], sel[:, tt, :], start=tt == 0, stop=tt == TT - 1)
            mm.then_inc(ranked, 1)

        def find(out, one_hot):
            for t in range(NT):
                for tt in range(TT):
                    mm = pe.matmul(out[:, 2 * t:2 * t + 2], one_hot[:, tt, t * P:(t + 1) * P],
                                   token_of[:, tt, :], start=tt == 0, stop=tt == TT - 1)
            return mm

        def turn(out, source, k):
            for t in range(NT):
                mm = pe.transpose(out[:, t * P:(t + 1) * P], source[:, t, k * P:(k + 1) * P], ident[:, :])
            return mm

        def up_products(m, f, h, g, hi, lo):
            for kind, out in enumerate((h, g)[:m.ups // KC]):
                mm = three(out, [(w_hi[:, f, (KC * kind + k) * P:(KC * kind + k + 1) * P],
                                  w_lo[:, f, (KC * kind + k) * P:(KC * kind + k + 1) * P],
                                  hi[:, k, :], lo[:, k, :]) for k in range(KC)], True, True)
            return mm

        def down_products(m, f, par):
            n = m.ups * P
            for t in range(NT):
                c = slice(t * P, (t + 1) * P)
                mm = three(bank[4 + t][:, 0:C],
                           [(a_hi[:, par, c], a_lo[:, par, c], w_hi[:, f, n:n + C], w_lo[:, f, n:n + C])],
                           f == 0, f == m.nf - 1)
            return mm

        def further(m, e, b):
            s = moe_sems[m.name]
            q = e * OB + b - 1
            pe.wait_ge(s["o_hot_ready"], q + 1)
            find(bank[7], hot_o).then_inc(s["o_found"], 1)
            pe.wait_ge(s["o_from_ready"], q + 1)
            pe.wait_ge(s["o_gathered"], q + 1)
            for k in range(KC):
                if k:
                    pe.wait_ge(s["o_xlo"], KC * q + k)
                turn(bank[7], got_o, k).then_inc(s["o_xt"], 1)
            pe.wait_ge(s["o_xlo"], KC * (q + 1))
            pe.wait_ge(s["wlo_done"], (e + 1) * m.nf)
            for f in range(m.nf):
                up_products(m, f, bank[1][:, 0:NB], bank[3][:, 0:NB], xo_hi, xo_lo).then_inc(s["o_up_done"], 1)
                pe.wait_ge(s["o_a_ready"], m.nf * q + f + 1)
                if f == 0:
                    pe.wait_ge(s["gy_ready"], e + 1)
                down_products(m, f, 1).then_inc(s["o_a_free"], 1)
            pe.wait_ge(s["o_gy_ready"], q + 1)
            pe.wait_ge(s["o_a_free"], m.nf * (q + 1))

        def experts(m):
            s = moe_sems[m.name]
            x_banks = (bank[7], bank[7]) if m.gated else (bank[2], bank[3])

            def up(e, par, f):
                pe.wait_ge(s["wlo_done"], e * m.nf + f + 1)
                pe.wait_ge(s["up_free"], e * m.nf + f + 1)
                up_products(m, f, bank[f % 2][:, 0:NB], bank[2 + f % 2][:, 0:NB], xg_hi[:, par], xg_lo[:, par]
                            ).then_inc(s["up_done"], 1)

            def down(e, f):
                if f == 0:
                    pe.wait_ge(s["gy_ready"], e + 1)
                pe.wait_ge(s["a_ready"], e * m.nf + f + 3)
                down_products(m, f, f % 2).then_inc(s["a_free"], 1)

            def locate(e):
                pe.wait_ge(s["hot_ready"], e + 1)
                pe.wait_ge(s["xlo"], KC * e)
                find(bank[7], hot).then_inc(s["found"], 1)

            def bring(e, par, k):
                if k == 0:
                    pe.wait_ge(s["from_ready"], e + 1)
                    pe.wait_ge(s[f"gathered{par}"], 8 * NT * (e - par) + 16 * NT)
                elif m.gated:
                    pe.wait_ge(s["xlo"], KC * e + k)
                turn(x_banks[k], got[:, par], k).then_inc(s["xt"], 1)

            def expert(e, par, more):
                branch(pe, m, e, lambda b: further(m, e, b),
                       (("o_found", 1), ("o_xt", KC), ("o_up_done", m.nf), ("o_a_free", m.nf)))
                if more:
                    locate(e + 1)
                for f in range(m.nf):
                    if f < m.nf - 1:
                        up(e, par, f + 1)
                    elif more:
                        pe.wait_ge(s["xlo"], KC * (e + 2))
                        up(e + 1, 1 - par, 0)
                    if more and f == m.nf - 2:
                        bring(e + 1, 1 - par, 0)
                    down(e, f)
                    if more and f == m.nf - 2:
                        bring(e + 1, 1 - par, 1)

            pe.wait_ge(s["hot_ready"], 1)
            find(bank[7], hot).then_inc(s["found"], 1)
            bring(0, 0, 0)
            bring(0, 0, 1)
            pe.wait_ge(s["xlo"], KC)
            pe.wait_ge(counts_ready, 1 + (not m.gated))
            up(0, 0, 0)
            with pe.Fori(0, E // 2 - 1) as pair:
                e = 2 * pair
                expert(e, 0, True)
                expert(e + 1, 1, True)
            expert(E - 2, 0, True)
            expert(E - 1, 1, False)

        for m in (L0, L1):
            pe.sem_inc(moe_sems[m.name]["a_free"], m.nf)

        pe.wait_ge(group_ready, 1)
        pe.wait_ge(gn_stats, 1)
        pe.matmul(bank[0][:, 0:KC], group_mat[:, :], small[:, 0:KC], start=True, stop=True).then_inc(gn_mean, 1)
        pe.wait_ge(gn_stats, 2)
        pe.matmul(bank[1][:, 0:KC], group_mat[:, :], small[:, KC:2 * KC], start=True, stop=True
                  ).then_inc(gn_var, 1)
        pe.wait_ge(consts_ready, 1)
        pe.wait_ge(gatew_in, 16)
        pe.wait_ge(xnT_ready, 1)
        for tt in range(TT):
            for k in range(KC):
                mm = pe.transpose(bank[2 + tt // 2][:, (tt % 2) * C + k * P:(tt % 2) * C + (k + 1) * P],
                                  xnT[:, k, tt * P:(tt + 1) * P], ident[:, :])
            if tt % 2:
                mm.then_inc(turned, 1)
        rank(0, gate_w)
        pe.wait_ge(rows_copied, TT // 2)
        experts(L0)

        def turn_rows():
            for k in range(KC):
                for tt in range(TT):
                    mm = pe.transpose(bank[2 * k + tt // QT][:, (tt % QT) * P:(tt % QT + 1) * P],
                                      rows[:, tt, k * P:(k + 1) * P], ident[:, :])
                    if tt % QT == QT - 1:
                        mm.then_inc(turned, 1)

        pe.wait_ge(normed, 1)
        turn_rows()

        pe.wait_ge(wqkv_lo_done, 1)
        pe.wait_ge(turned_lo, KC * NH)
        n = 0
        for qk in range(2):
            for mt in range(KC):
                for th in range(NH):
                    if n >= 2:
                        pe.wait_ge(proj_free, n - 1)
                    col = qk * C + mt * P
                    three(bank[n % 2][:, :],
                          [(wqkv_hi[:, k, col:col + P], wqkv_lo[:, k, col:col + P],
                            x_hi[:, k, th * HALF:(th + 1) * HALF],
                            x_lo[:, k, th * HALF:(th + 1) * HALF]) for k in range(KC)],
                          True, True).then_inc(proj_mm, 1)
                    n += 1
        for tt in range(TT):
            if tt >= 2:
                pe.wait_ge(v_done, tt - 1)
            three(bank[2 + tt % 2][:, 0:C],
                  [(x_hi[:, k, tt * P:(tt + 1) * P], x_lo[:, k, tt * P:(tt + 1) * P],
                    wqkv_hi[:, k, 2 * C:3 * C], wqkv_lo[:, k, 2 * C:3 * C]) for k in range(KC)],
                  True, True).then_inc(v_mm, 1)

        stacks = [0]

        def stack(g):
            if g == 0:
                pe.wait_ge(cleared, 1)
                pe.wait_ge(proj_free, 2 * KC * NH)
            for pr in range(2):
                p = 2 * g + pr
                mt, a = p // 4, p % 4
                for qk in range(2):
                    for th in range(NH):
                        i = stacks[0]
                        if i >= 2:
                            pe.wait_ge(stack_done, i - 1)
                        for lo in range(2):
                            mm = pe.matmul(bank[4 + i % 2][:, :], pick[:, 2 * qk + lo, a, :],
                                           (qk_lo if lo else qk_hi)[:, qk, mt, th * HALF:(th + 1) * HALF],
                                           start=lo == 0, stop=lo == 1)
                        mm.then_inc(stack_mm, 1)
                        stacks[0] += 1

        smax = [0]

        def score_rows(g, j, i):
            n = smax[0]
            if n >= 2:
                pe.wait_ge(smax_done, n - 1)
            rows = slice(64 * (j % 2), 64 * (j % 2) + 64)
            keys = (i + 1) * P
            for c in range(0, keys, HALF):
                w = min(HALF, keys - c)
                out = bank[2 * (n % 2) + c // HALF]
                mm = pe.matmul(out[:, 0:w], q_st[rows, g % 2, j // 2, i * P:(i + 1) * P],
                               k_st[rows, g % 2, j // 2, c:c + w], start=True, stop=True)
            mm = pe.matmul(out[:, w - P:w], identb[:, :], mask_q[:, :], start=False, stop=True,
                           skip_group_check=True)
            mm.then_inc(smax_mm, 1)
            smax[0] += 1

        def max_rows(g):
            pe.wait_ge(maxcol_ready, g + 1)
            pe.wait_ge(smax_done, 32 * (g + 1))
            for pr in range(2):
                for tt in range(TT):
                    mm = pe.transpose(bank[2 * pr + tt // QT][:, (tt % QT) * P:(tt % QT + 1) * P],
                                      max_t[:, pr, tt, :], ident[:, :])
                mm.then_inc(maxrow_mm, 1)

        def score_cols(g, step, j):
            qb, kt = STEPS[step]
            n = (g * len(STEPS) + step) * HG + j
            if n >= 2:
                pe.wait_ge(exp_done, n - 1)
            c0 = max(0, kt - QT * qb) * P
            rows = slice(64 * (j % 2), 64 * (j % 2) + 64)
            out = bank[4 + n % 2]
            mm = pe.matmul(out[:, c0:HALF], k_st[rows, g % 2, j // 2, kt * P:(kt + 1) * P],
                           q_st[rows, g % 2, j // 2, qb * HALF + c0:(qb + 1) * HALF], start=True,
                           stop=True)
            if kt >= QT * qb:
                mm = pe.matmul(out[:, c0:c0 + P], identb[:, :], mask_k[:, :], start=False, stop=True,
                               skip_group_check=True)
            mm.then_inc(st_mm, 1)

        def values(g, step):
            qb, kt = STEPS[step]
            c0 = max(0, kt - QT * qb) * P
            if kt == 0 and g * NH + qb >= 2:
                pe.wait_ge(po_done, g * NH + qb - 1)
            pe.wait_ge(exp_done, (g * len(STEPS) + step + 1) * HG)
            for j in range(HG):
                mm = pe.matmul(bank[6 + qb][2 * D * j:2 * D * (j + 1), c0:HALF],
                               v_sb[:, kt, HG * g + j, :], probs[:, (step % 2) * HG + j, c0:HALF],
                               start=kt == 0, stop=kt == QT * (qb + 1) - 1)
            mm.then_inc(pv_done, 1)

        tiles = [(j, i) for j in range(HG) for i in range(TT)]
        pe.wait_ge(v_done, TT)
        stack(0)
        pe.wait_ge(stack_done, 8)
        for j, i in tiles:
            score_rows(0, j, i)
        for g in range(GROUPS):
            if g + 1 < GROUPS:
                stack(g + 1)
            max_rows(g)
            pe.wait_ge(qmax_done, 4 * (g + 1))
            pe.wait_ge(stack_done, 8 * min(g + 2, GROUPS))
            todo = list(tiles) if g + 1 < GROUPS else []
            for step in range(len(STEPS)):
                for j in range(HG):
                    score_cols(g, step, j)
                for _ in range(3):
                    if todo:
                        score_rows(g + 1, *todo.pop(0))
                if step:
                    values(g, step - 1)
            values(g, len(STEPS) - 1)

        pe.wait_ge(po_done, GROUPS * NH)
        pe.wait_ge(wo_in, 16 * (HG + 1))
        for tt in range(TT):
            if tt >= 4:
                pe.wait_ge(attn_added, tt - 3)
            for g in range(GROUPS):
                mm = pe.matmul(bank[tt % 4][:, 0:C], o_sb[:, g, tt * P:(tt + 1) * P], wo_sb[:, g, :],
                               start=g == 0, stop=g == GROUPS - 1)
            mm.then_inc(wo_mm, 1)

        pe.wait_ge(normed, 2)
        turn_rows()
        pe.wait_ge(routerw_in, 16)
        pe.wait_ge(xnT_ready, 1 + KC * NH)
        rank(1, router_w)
        experts(L1)

    @block.scalar
    def _(act):
        def tokens_std(i):
            act.wait_ge(ln_var, i + 1)
            act.activation(std[:, :], tok_mv[:, :, 1], ACT.Sqrt, bias=eps[:, 0:1]).then_inc(ln_std, 1)

        def exp_logits(i):
            act.wait_ge(logits_centred, i + 1)
            act.activation(rt[:, 1], rt[:, 0], ACT.Exp).then_inc(logits_exp, 1)

        def split_hi(m, e, f):
            s = moe_sems[m.name]
            act.wait_ge(s[f"staged{f // m.per_chunk}"], m.staged * (e + 1))
            act.wait_ge(s["a_free"], e * m.nf + f + 1)
            for dst, src in slot_parts(m, f, w_hi):
                ins = act.activation(dst, src, ACT.Copy)
            ins.then_inc(s["whi_done"], 1)

        def further(m, e, b):
            s = moe_sems[m.name]
            q = e * OB + b - 1
            for k in range(KC):
                act.wait_ge(s["o_xt"], KC * q + k + 1)
                act.activation(xo_hi[:, k, :], bank[7][:, 0:NB], ACT.Copy).then_inc(s["o_xhi"], 1)
            for f in range(m.nf):
                act.wait_ge(s["o_up_done"], m.nf * q + f + 1)
                if m.gated:
                    act.activation(sil[:, 1, :], bank[1][:, 0:NB], ACT.Silu).then_inc(s["o_sil_done"], 1)
                else:
                    act.activation(prod[:, 1, :], bank[1][:, 0:NB], ACT.Gelu).then_inc(s["o_prod_done"], 1)
            act.wait_ge(s["o_a_ready"], m.nf * (q + 1))
            act.sem_inc(act_left, 1)

        def experts(m):
            s = moe_sems[m.name]

            def round_x(e, par, k):
                act.wait_ge(s["xt"], KC * e + k + 1)
                b = bank[7] if m.gated else bank[2 + k]
                act.activation(xg_hi[:, par, k, :], b[:, 0:NB], ACT.Copy).then_inc(s["xhi"], 1)

            def stage(e, f):
                act.wait_ge(s["up_done"], e * m.nf + f + 1)
                if m.gated:
                    act.wait_ge(s["up_free"], e * m.nf + f + 1)
                    act.activation(sil[:, f % 2, :], bank[f % 2][:, 0:NB], ACT.Silu
                                   ).then_inc(s["sil_done"], 1)
                else:
                    act.wait_ge(s["a_ready"], e * m.nf + f + 1)
                    act.activation(prod[:, f % 2, :], bank[f % 2][:, 0:NB], ACT.Gelu
                                   ).then_inc(s["up_free"], 1)

            def expert(e, par, more):
                for f in range(m.nf):
                    stage(e, f)
                    if f == 0:
                        split_hi(m, e, m.nf - 2)
                        split_hi(m, e, m.nf - 1)
                        branch(act, m, e, lambda b: further(m, e, b),
                               (("o_xhi", KC), ("o_sil_done" if m.gated else "o_prod_done", m.nf)))
                    elif f >= 2 and more:
                        split_hi(m, e + 1, f - 2)
                    if more and f == m.nf - 2:
                        for k in range(KC):
                            round_x(e + 1, 1 - par, k)

            for k in range(KC):
                round_x(0, 0, k)
            act.wait_ge(counts_ready, 1 + (not m.gated))
            with act.Fori(0, E // 2 - 1) as pair:
                e = 2 * pair
                expert(e, 0, True)
                expert(e + 1, 1, True)
            expert(E - 2, 0, True)
            expert(E - 1, 1, False)

        act.wait_ge(group_ready, 1)
        act.wait_ge(gn_var, 1)
        act.activation(small[:, 8:8 + KC], bank[1][:, 0:KC], ACT.Sqrt, bias=eps[:, 0:1]).then_inc(gn_std, 1)
        exp_logits(0)
        for f in range(L0.nf - 2):
            split_hi(L0, 0, f)
        experts(L0)

        tokens_std(0)
        for k in range(KC):
            for th in range(NH):
                act.wait_ge(turned, TT // 2 + 2 * k + th + 1)
                act.activation(x_hi[:, k, th * HALF:(th + 1) * HALF], bank[2 * k + th][:, :], ACT.Copy
                               ).then_inc(turned_hi, 1)
        act.wait_ge(attn_in, 16 * (2 * KC + 2))
        act.activation(wqkv_hi[:, :, :], wqkv[:, :, :], ACT.Copy).then_inc(wqkv_hi_done, 1)
        n = 0
        for qk in range(2):
            for mt in range(KC):
                for th in range(NH):
                    act.wait_ge(proj_mm, n + 1)
                    act.activation(qk_hi[:, qk, mt, th * HALF:(th + 1) * HALF], bank[n % 2][:, :],
                                   ACT.Identity, bias=bqk[:, qk, mt:mt + 1]).then_inc(proj_hi, 1)
                    n += 1

        def stack(g):
            for n in range(8):
                pr, qk, th = n // 4, n // 2 % 2, n % 2
                i = 8 * g + n
                act.wait_ge(stack_mm, i + 1)
                if g >= 2 and n == 0:
                    act.wait_ge(pv_done, len(STEPS) * (g - 1))
                dst = (k_st if qk else q_st)[:, g % 2, pr, th * HALF:(th + 1) * HALF]
                if qk:
                    act.activation(dst, bank[4 + i % 2][:, :], ACT.Identity, bias=key_ones[:, 0:1]
                                   ).then_inc(stack_done, 1)
                else:
                    act.activation(dst, bank[4 + i % 2][:, :], ACT.Copy).then_inc(stack_done, 1)

        act.wait_ge(consts_ready, 1)
        stack(0)
        for g in range(GROUPS):
            if g + 1 < GROUPS:
                stack(g + 1)
            for step, (qb, kt) in enumerate(STEPS):
                c0 = max(0, kt - QT * qb) * P
                for j in range(HG):
                    n = (g * len(STEPS) + step) * HG + j
                    act.wait_ge(st_mm, n + 1)
                    if j == 0 and g * len(STEPS) + step >= 2:
                        act.wait_ge(pv_done, g * len(STEPS) + step - 1)
                    act.activation(probs[:, (step % 2) * HG + j, c0:HALF], bank[4 + n % 2][:, c0:HALF],
                                   ACT.Exp, scale=float(C) ** -0.5).then_inc(exp_done, 1)

        tokens_std(1)
        for k in range(KC):
            for th in range(NH):
                act.wait_ge(turned, TT // 2 + KC * NH + 2 * k + th + 1)
                act.activation(xnT[:, k, th * HALF:(th + 1) * HALF], bank[2 * k + th][:, :], ACT.Copy
                               ).then_inc(xnT_ready, 1)
        exp_logits(1)
        act.wait_ge(wo_mm, TT)
        for f in range(L1.nf - 2):
            split_hi(L1, 0, f)
        experts(L1)

    @block.vector
    def _(dve):
        n_link = [0]

        def link(ins):
            n_link[0] += 1
            ins.then_inc(dve_step, 1)
            dve.wait_ge(dve_step, n_link[0])

        def f32(ap):
            return ap.bitcast(F32)

        def layer_norm(i):
            for tt in range(TT):
                if i == 0 and tt % QT == 0:
                    dve.wait_ge(tok_in[tt // QT], 16)
                link(dve.bn_stats(tok_stats[:, tt, :], tok[:, tt, :]))
                ins = dve.bn_aggr(tok_mv[:, tt, :], tok_stats[:, tt, :])
            ins.then_inc(ln_var, 1)
            dve.wait_ge(ln_std, i + 1)
            link(dve.reciprocal(rstd[:, :], std[:, :]))
            for tt in range(TT):
                ins = dve.tensor_scalar(rows[:, tt, 0:C], tok[:, tt, :], tok_mv[:, tt, 0:1], rstd[:, tt:tt + 1],
                                        ALU.subtract, ALU.mult)
            ins.then_inc(normed, 1)

        def over(col):
            return col.unsqueeze(2).to_broadcast([P, TT, E])

        def routing(i, first_of_ties):
            logits = bank[7][:, 0:TT * E].rearrange("p (t e) -> p t e", e=E)
            dve.wait_ge(logits_done, i + 1)
            link(dve.tensor_reduce(rs[:, 0], logits, AX_X, ALU.max))
            dve.tensor_tensor(rt[:, 0], logits, over(rs[:, 0]), ALU.subtract).then_inc(logits_centred, 1)
            dve.wait_ge(logits_exp, i + 1)
            link(dve.tensor_reduce(rs[:, 1], rt[:, 1], AX_X, ALU.add))
            link(dve.reciprocal(rs[:, 2], rs[:, 1]))
            link(dve.tensor_tensor(rt[:, 2], rt[:, 1], over(rs[:, 2]), ALU.mult))

            def top(values, value, hot, tmp):
                link(dve.tensor_reduce(value, values, AX_X, ALU.max))
                link(dve.tensor_tensor(hot, values, over(value), ALU.is_equal))
                if first_of_ties:
                    link(dve.tensor_tensor(tmp, hot, order[:, :, :], ALU.mult))
                    link(dve.tensor_reduce(rs[:, 8], tmp, AX_X, ALU.max))
                    link(dve.tensor_tensor(hot, tmp, over(rs[:, 8]), ALU.is_equal))

            top(rt[:, 2], rs[:, 3], rt[:, 3], rt[:, 4])
            if first_of_ties:
                link(dve.scalar_tensor_tensor(out=rt[:, 5], in0=rt[:, 3], scalar=-2.0, in1=rt[:, 2],
                                              op0=ALU.mult, op1=ALU.add))
            else:
                link(dve.tensor_tensor(rt[:, 4], rt[:, 2], rt[:, 3], ALU.mult))
                link(dve.tensor_tensor(rt[:, 5], rt[:, 2], rt[:, 4], ALU.subtract))
            top(rt[:, 5], rs[:, 4], rt[:, 6], rt[:, 4])
            link(dve.tensor_tensor(rs[:, 5], rs[:, 3], rs[:, 4], ALU.add))
            link(dve.reciprocal(rs[:, 6], rs[:, 5]))
            link(dve.tensor_tensor(rs[:, 7], rs[:, 6], rs[:, 3], ALU.mult))
            link(dve.tensor_tensor(rs[:, 9], rs[:, 6], rs[:, 4], ALU.mult))
            link(dve.tensor_tensor(rt[:, 7], rt[:, 3], over(rs[:, 7]), ALU.mult))
            link(dve.tensor_tensor(rt[:, 8], rt[:, 6], over(rs[:, 9]), ALU.mult))
            if i == 0:
                dve.wait_ge(rows_copied, TT // 2)
            gates = rows[:, :, C:C + E]
            dve.tensor_tensor(gates, rt[:, 7], rt[:, 8], ALU.add).then_inc(rows_ready, 1)
            dve.wait_ge(rows_ready, i + 1)
            dve.tensor_scalar(sel[:, :, :], gates, 0.0, None, ALU.not_equal).then_inc(sel_ready, 1)
            dve.wait_ge(sel_ready, i + 1)
            dve.wait_ge(ranked, i + 1)
            dve.tensor_copy(count[:, :], bank[5][:, 0:E]).then_inc(counts_ready, 1)
            link(dve.scalar_tensor_tensor(out=pos[:, :, :], in0=bank[6][:, 0:TT * E].rearrange(
                "p (t e) -> p t e", e=E), scalar=1.0, in1=sel[:, :, :], op0=ALU.add, op1=ALU.mult))
            link(dve.tensor_scalar(pos[:, :, :], pos[:, :, :], -1.0, None, ALU.add))

        def one_hots(out, e, b, tiles):
            for tt in tiles:
                ins = dve.tensor_scalar(out[:, tt, :], places[:, b * NB:(b + 1) * NB],
                                        pos[:, tt, bass.ds(e, 1)], None, ALU.is_equal)
            return ins

        def split_lo(m, e, f):
            s = moe_sems[m.name]
            dve.wait_ge(s["whi_done"], e * m.nf + f + 1)
            for (hi, src), (lo, _) in zip(slot_parts(m, f, w_hi), slot_parts(m, f, w_lo)):
                ins = dve.tensor_tensor(lo, src, f32(hi), ALU.subtract)
            ins.then_inc(s["wlo_done"], 1)

        def further(m, e, b):
            s = moe_sems[m.name]
            q = e * OB + b - 1
            one_hots(hot_o, e, b, range(TT)).then_inc(s["o_hot_ready"], 1)
            dve.wait_ge(s["o_found"], q + 1)
            numbers = bank[7][:, 0:2 * NT].rearrange("p (t c) -> p t c", c=2)
            dve.tensor_copy(found_o[:, :, :], numbers)
            dve.tensor_copy(from_row_o[:, :], numbers[:, :, 0]).then_inc(s["o_from_ready"], 1)
            dve.wait_ge(s["o_from_ready"], q + 1)
            dve.scalar_tensor_tensor(out=missing[:, 1, :], in0=found_o[:, :, 1], scalar=0.0, in1=spare_row[:, :],
                                     op0=ALU.is_equal, op1=ALU.mult).then_inc(s["o_missing"], 1)
            dve.wait_ge(s["o_missing"], q + 1)
            dve.tensor_tensor(to_row_o[:, :], missing[:, 1, :], found_o[:, :, 0], ALU.add
                              ).then_inc(s["o_to_ready"], 1)
            for k in range(KC):
                dve.wait_ge(s["o_xhi"], KC * q + k + 1)
                dve.tensor_tensor(xo_lo[:, k, :], bank[7][:, 0:NB], f32(xo_hi[:, k, :]), ALU.subtract
                                  ).then_inc(s["o_xlo"], 1)
            for f in range(m.nf):
                n = m.nf * q + f
                if m.gated:
                    dve.wait_ge(s["o_sil_done"], n + 1)
                    dve.tensor_tensor(prod[:, 1, :], sil[:, 1, :], bank[3][:, 0:NB], ALU.mult
                                      ).then_inc(s["o_prod_done"], 1)
                dve.wait_ge(s["o_prod_done"], n + 1)
                dve.tensor_copy(a_hi[:, 1, :], prod[:, 1, :]).then_inc(s["o_a_hi_done"], 1)
                dve.wait_ge(s["o_a_hi_done"], n + 1)
                dve.tensor_tensor(a_lo[:, 1, :], prod[:, 1, :], f32(a_hi[:, 1, :]), ALU.subtract
                                  ).then_inc(s["o_a_ready"], 1)
            dve.wait_ge(s["o_a_free"], m.nf * (q + 1))
            for t in range(NT):
                ins = dve.tensor_scalar(gated_o[:, t, :], bank[4 + t][:, 0:C], got_o[:, t, bass.ds(e + C, 1)],
                                        None, ALU.mult)
            ins.then_inc(s["o_gy_ready"], 1)
            dve.wait_ge(s["o_added"], q + 1)
            dve.sem_inc(dve_left, 1)

        def sum_further():
            link(dve.tensor_scalar(extra[:, :], count[:, :], float(NB), None, ALU.is_gt))
            for b in range(2, BLOCKS):
                link(dve.tensor_scalar(extra2[:, :], count[:, :], float(b * NB), None, ALU.is_gt))
                link(dve.tensor_tensor(extra[:, :], extra[:, :], extra2[:, :], ALU.add))
            link(dve.tensor_tensor(extra_of[:, :, :], earlier[:, :, :],
                                   extra[:, :].unsqueeze(1).to_broadcast([P, E, E]), ALU.mult))
            link(dve.tensor_reduce(extra2[:, :], extra_of[:, :, :], AX_X, ALU.add))
            dve.tensor_copy(ran_before[:, :], extra2[:, :]).then_inc(ran_ready, 1)

        def experts(m):
            s = moe_sems[m.name]

            def stage(e, f):
                n = e * m.nf + f
                b = f % 2
                if m.gated:
                    dve.wait_ge(s["sil_done"], n + 1)
                    dve.tensor_tensor(prod[:, b, :], sil[:, b, :], bank[2 + b][:, 0:NB], ALU.mult
                                      ).then_inc(s["up_free"], 1)
                dve.wait_ge(s["up_free"], n + 3)
                dve.wait_ge(s["a_free"], n - 1 + m.nf)
                dve.tensor_copy(a_hi[:, b, :], prod[:, b, :]).then_inc(s["a_hi_done"], 1)
                dve.wait_ge(s["a_hi_done"], n + 1)
                dve.tensor_tensor(a_lo[:, b, :], prod[:, b, :], f32(a_hi[:, b, :]), ALU.subtract
                                  ).then_inc(s["a_ready"], 1)

            def located(e, par):
                dve.wait_ge(s["found"], e + 1)
                numbers = bank[7][:, 0:2 * NT].rearrange("p (t c) -> p t c", c=2)
                dve.tensor_copy(found[:, par], numbers)
                dve.tensor_copy(from_row[:, par, :], numbers[:, :, 0]).then_inc(s["from_ready"], 1)

            def destination(e, par):
                dve.wait_ge(s["from_ready"], e + 1)
                dve.scalar_tensor_tensor(out=missing[:, 0, :], in0=found[:, par, :, 1], scalar=0.0,
                                         in1=spare_row[:, :], op0=ALU.is_equal, op1=ALU.mult
                                         ).then_inc(s["missing"], 1)
                dve.wait_ge(s["missing"], e + 1)
                dve.wait_ge(s["gy_free"], e + 1)
                dve.tensor_tensor(to_row[:, par, :], missing[:, 0, :], found[:, par, :, 0], ALU.add
                                  ).then_inc(s["to_ready"], 1)

            def rest_x(e, par):
                for k in range(KC):
                    dve.wait_ge(s["xhi"], KC * e + k + 1)
                    b = bank[7] if m.gated else bank[2 + k]
                    dve.tensor_tensor(xg_lo[:, par, k, :], b[:, 0:NB], f32(xg_hi[:, par, k, :]), ALU.subtract
                                      ).then_inc(s["xlo"], 1)

            def expert(e, par, more):
                for f in range(m.nf):
                    stage(e, f)
                    if f == 0:
                        split_lo(m, e, m.nf - 2)
                        split_lo(m, e, m.nf - 1)
                        branch(dve, m, e, lambda b: further(m, e, b),
                               [("o_" + n, c) for n, c in (
                                   ("hot_ready", 1), ("from_ready", 1), ("missing", 1), ("to_ready", 1), ("xlo", KC),
                                   ("a_hi_done", m.nf), ("a_ready", m.nf), ("gy_ready", 1))] +
                               ([("o_prod_done", m.nf)] if m.gated else []))
                        if more:
                            located(e + 1, 1 - par)
                    elif f >= 2 and more:
                        split_lo(m, e + 1, f - 2)
                    if more == 2 and f == 1:
                        one_hots(hot, e + 2, 0, range(TT)).then_inc(s["hot_ready"], 1)
                    if more and f == m.nf - 2:
                        rest_x(e + 1, 1 - par)
                dve.wait_ge(s["a_free"], (e + 2) * m.nf)
                dve.wait_ge(s["gy_free"], e + 1)
                for t in range(NT):
                    ins = dve.tensor_scalar(gated_y[:, par, t, :], bank[4 + t][:, 0:C],
                                            got[:, par, t, bass.ds(e + C, 1)], None, ALU.mult)
                ins.then_inc(s["gy_ready"], 1)
                if more:
                    destination(e + 1, 1 - par)

            one_hots(hot, 0, 0, range(TT)).then_inc(s["hot_ready"], 1)
            located(0, 0)
            destination(0, 0)
            sum_further()
            one_hots(hot, 1, 0, range(TT)).then_inc(s["hot_ready"], 1)
            for f in range(m.nf - 2):
                split_lo(m, 0, f)
            rest_x(0, 0)
            with dve.Fori(0, E // 2 - 1) as pair:
                e = 2 * pair
                expert(e, 0, 2)
                expert(e + 1, 1, 2)
            expert(E - 2, 0, 1)
            expert(E - 1, 1, 0)

        for m in (L0, L1):
            s = moe_sems[m.name]
            dve.sem_inc(s["up_free"], 2)
            dve.sem_inc(s["a_ready"], 2)
            dve.sem_inc(s["gy_ready"], 1)

        dve.wait_ge(x_in, 16 * KC)
        for k in range(KC):
            for th in range(NH):
                link(dve.bn_stats(stats[:, k, th, :], xT[:, k, th * HALF:(th + 1) * HALF]))
            link(dve.bn_aggr(small[:, 4 + 2 * k:6 + 2 * k], stats[:, k, :, :]))
        mv = small[:, 4:8].rearrange("p (k s) -> p s k", s=2)
        mean, dev, square = small[:, 16:16 + KC], small[:, 18:18 + KC], small[:, 20:20 + KC]
        inv = small[:, 22:22 + KC]
        dve.tensor_copy(small[:, 0:KC], mv[:, 0, :]).then_inc(gn_stats, 1)
        dve.wait_ge(gn_mean, 1)
        link(dve.tensor_copy(mean, bank[0][:, 0:KC]))
        link(dve.tensor_tensor(dev, mv[:, 0, :], mean, ALU.subtract))
        link(dve.tensor_tensor(square, dev, dev, ALU.mult))
        dve.tensor_tensor(small[:, KC:2 * KC], square, mv[:, 1, :], ALU.add).then_inc(gn_stats, 1)
        dve.wait_ge(gn_std, 1)
        link(dve.reciprocal(inv, small[:, 8:8 + KC]))
        for k in range(KC):
            ins = dve.tensor_scalar(xnT[:, k, :], xT[:, k, :], mean[:, k:k + 1], inv[:, k:k + 1],
                                    ALU.subtract, ALU.mult)
        ins.then_inc(xnT_ready, 1)
        for i in range(TT // 2):
            dve.wait_ge(turned, i + 1)
            dve.tensor_copy(rows[:, 2 * i:2 * i + 2, 0:C], bank[2 + i][:, :].rearrange("p (t c) -> p t c", c=C)
                            ).then_inc(rows_copied, 1)
        routing(0, False)
        experts(L0)

        layer_norm(0)
        for k in range(KC):
            for th in range(NH):
                c = slice(th * HALF, (th + 1) * HALF)
                dve.wait_ge(turned_hi, 2 * k + th + 1)
                dve.tensor_tensor(x_lo[:, k, c], bank[2 * k + th][:, :], f32(x_hi[:, k, c]), ALU.subtract
                                  ).then_inc(turned_lo, 1)
        dve.wait_ge(wqkv_hi_done, 1)
        dve.tensor_tensor(wqkv_lo[:, :, :], wqkv[:, :, :], f32(wqkv_hi[:, :, :]), ALU.subtract
                          ).then_inc(wqkv_lo_done, 1)
        n = 0
        for qk in range(2):
            for mt in range(KC):
                for th in range(NH):
                    c = slice(th * HALF, (th + 1) * HALF)
                    dve.wait_ge(proj_hi, n + 1)
                    dve.scalar_tensor_tensor(out=qk_lo[:, qk, mt, c], in0=bank[n % 2][:, :],
                                             scalar=bqk[:, qk, mt:mt + 1], in1=f32(qk_hi[:, qk, mt, c]),
                                             op0=ALU.add, op1=ALU.subtract).then_inc(proj_free, 1)
                    n += 1
        for tt in range(TT):
            dve.wait_ge(v_mm, tt + 1)
            dve.tensor_tensor(v_sb[:, tt, :, 0:D], bank[2 + tt % 2][:, 0:C].rearrange("p (h d) -> p h d", d=D),
                              bv[:, :].rearrange("p (h d) -> p h d", d=D), ALU.add).then_inc(v_done, 1)

        def row_max(g, j, i):
            n = (g * HG + j) * TT + i
            dve.wait_ge(smax_mm, n + 1)
            keys = (i + 1) * P
            out = maxes[:, g % 2, j, i:i + 1]
            b = 2 * (n % 2) * HALF
            dve.tensor_reduce(out, banks[:, b:b + keys], AX_X, ALU.max).then_inc(smax_done, 1)

        def store_max(g):
            dve.wait_ge(smax_done, HG * TT * (g + 1))
            if g == 0:
                dve.wait_ge(cleared, 3)
            else:
                dve.wait_ge(maxrow_mm, 2 * g)
            for pr in range(2):
                top = maxes[:, g % 2, 2 * pr:2 * pr + 2, :].rearrange("p j t -> p t j")
                cols = max_t[:, pr].rearrange("p t (j c) -> p t j c", j=2)
                hi, lo = cols[:, :, :, 3 * D], cols[:, :, :, 3 * D + 1]
                link(dve.tensor_scalar(hi.bitcast(F32R), top, -1.0, None, ALU.mult))
                ins = dve.scalar_tensor_tensor(out=lo.bitcast(F32R), in0=top, scalar=-1.0, in1=hi,
                                               op0=ALU.mult, op1=ALU.subtract)
            ins.then_inc(maxcol_ready, 1)
            for pr in range(2):
                dve.wait_ge(maxrow_mm, 2 * g + pr + 1)
                for th in range(NH):
                    rows = q_st[:, g % 2, pr, th * HALF:(th + 1) * HALF]
                    dve.tensor_tensor(rows, f32(rows), bank[2 * pr + th][:, :], ALU.add).then_inc(qmax_done, 1)

        def output(g, qb):
            dve.wait_ge(pv_done, len(STEPS) * g + QT * (qb + 1) + (QT if qb else 0))
            po = bank[6 + qb][:, :]
            link(dve.stream_shuffle(sums[:, :], po, [D + r % D for r in range(2 * D)]))
            link(dve.reciprocal(rsum[:, :], sums[:, :]))
            dve.tensor_tensor(o_sb[:, g, qb * HALF:(qb + 1) * HALF], po, rsum[:, :], ALU.mult
                              ).then_inc(po_done, 1)

        tiles = [(j, i) for j in range(HG) for i in range(TT)]
        for j, i in tiles:
            row_max(0, j, i)
        for g in range(GROUPS):
            store_max(g)
            todo = list(tiles) if g + 1 < GROUPS else []
            for j, i in todo[:15]:
                row_max(g + 1, j, i)
            output(g, 0)
            for j, i in todo[15:]:
                row_max(g + 1, j, i)
            output(g, 1)
        for tt in range(TT):
            dve.wait_ge(wo_mm, tt + 1)
            dve.tensor_tensor(tok[:, tt, :], tok[:, tt, :], bank[tt % 4][:, 0:C], ALU.add
                              ).then_inc(attn_added, 1)

        dve.wait_ge(attn_added, TT)
        layer_norm(1)
        routing(1, True)
        experts(L1)

    ctx.close()


def kernel(x, L0_conv_gate_w, L0_conv_w1, L0_conv_w3, L0_conv_w2, L1_attn_Wqkv, L1_attn_bqkv, L1_attn_Wo,
           L1_attn_bo, L1_ffn_router_w, L1_ffn_w1, L1_ffn_w2):
    import numpy as np
    import concourse.bacc as bacc
    from concourse.bass_utils import run_bass_kernel_spmd

    nc = bacc.Bacc("TRN2", target_bir_lowering=False, num_devices=1)
    x = np.asarray(x)
    named = [
        ("x", np.ascontiguousarray(x.reshape(T, C))),
        ("xT", np.ascontiguousarray(x.reshape(T, C).T)),
        ("gate_w", np.ascontiguousarray(L0_conv_gate_w)),
        ("w1", np.ascontiguousarray(L0_conv_w1)),
        ("w3", np.ascontiguousarray(L0_conv_w3)),
        ("w2", np.ascontiguousarray(L0_conv_w2)),
        ("Wqkv", np.ascontiguousarray(L1_attn_Wqkv)),
        ("bqkv", np.ascontiguousarray(L1_attn_bqkv)),
        ("Wo", np.ascontiguousarray(L1_attn_Wo)),
        ("bo", np.ascontiguousarray(L1_attn_bo)),
        ("router_wT", np.ascontiguousarray(np.asarray(L1_ffn_router_w).T)),
        ("ffn_w1", np.ascontiguousarray(L1_ffn_w1)),
        ("ffn_w2", np.ascontiguousarray(L1_ffn_w2)),
    ]
    arrays, args = {}, []
    for name, a in named:
        arrays[f"in_{name}"] = a
        args.append(nc.dram_tensor(f"in_{name}", a.shape, mybir.dt.from_np(a.dtype), kind="ExternalInput").ap())
    args.append(nc.dram_tensor("rows0", (T, ROW), F32, kind="Internal").ap())
    args.append(nc.dram_tensor("res0", (T + NB, C), F32, kind="Internal").ap())
    args.append(nc.dram_tensor("rows1", (T, ROW), F32, kind="Internal").ap())
    args.append(nc.dram_tensor("out", (T + NB, C), F32, kind="ExternalOutput").ap())
    build(nc, *args)
    r = run_bass_kernel_spmd(nc, [arrays], core_ids=[0])
    out = r.results[0]["out"]
    return np.ascontiguousarray(out[:T]).reshape(x.shape)
```

```python
from contextlib import ExitStack

import concourse.bass as bass
from concourse import mybir

F32 = mybir.dt.float32
F32R = mybir.dt.float32r
F16 = mybir.dt.float16
I32 = mybir.dt.int32
U32 = mybir.dt.uint32
BF16 = mybir.dt.bfloat16
ALU = mybir.AluOpType
ACT = mybir.ActivationFunctionType
AX_X = mybir.AxisListType.X

P = 128
T = 1024
C = 256
KC = C // P
TT = T // P
HALF = 512
NH = T // HALF
E = 8
GROUP = 8
HEADS = 16
D = C // HEADS
HG = 4
GROUPS = HEADS // HG
QT = HALF // P
MASKED = -1e30
NT = 3
NB = NT * P
ROW = C + E
GN_EPS = LN_EPS = 1e-5


class Moe:

    def __init__(self, name, f, gated, nb):
        self.name, self.gated = name, gated
        self.nb = nb
        self.blocks = -(-T // nb)
        self.further = self.blocks - 1
        self.tiles = [(t, min(P, nb - t * P)) for t in range(-(-nb // P))]
        self.nf = f // P
        self.ups = KC * (2 if gated else 1)
        self.per_chunk = self.nf // 2
        self.cols = self.ups * P + C
        self.staged = 16 * (3 if gated else 2)
        self.bring_at = self.nf // 2 - 1


STEPS = [(qb, kt) for qb in range(NH) for kt in range(QT * (qb + 1))]
NSTEPS = len(STEPS)


def attention_order():
    def rows_of(g):
        pieces = []
        for pr in range(2):
            pieces += [("rows", g, 2 * pr + j, i, c) for j in range(2) for i in range(TT)
                       for c in range(1 + (i >= QT))]
            pieces.append(("maxcol", g, pr))
        at = pieces.index(("rows", g, 2, 3, 0)) + 1
        return pieces[:at] + [("maxrow", g, 0, th) for th in range(NH)] + pieces[at:]

    order = [("proj", qk, mt, th) for mt in range(KC) for qk in range(2) for th in range(NH)]
    values = [("v", tt) for tt in range(TT)]
    order += values[0:QT]
    for n, piece in enumerate(rows_of(0)):
        order.append(piece)
        if n % 4 == 3 and n // 4 + QT < TT:
            order.append(values[n // 4 + QT])
    for g in range(GROUPS):
        more = g + 1 < GROUPS
        rows = rows_of(g + 1) if more else []
        first = 2 if g else 0
        per = len(rows) / (HG * (NSTEPS - first))
        owed = 0.0
        for s in range(NSTEPS):
            for j in range(HG):
                order.append(("cols", g, s, j))
                if s == 0 and j == 1:
                    order += [("maxrow", g, 1, th) for th in range(NH)]
                if s >= first:
                    owed += per
                    while owed > 0.5 and rows:
                        order.append(rows.pop(0))
                        owed -= 1
                if j == 1 and s:
                    order.append(("values", g, s - 1))
                    if s - 1 == QT - 1:
                        order.append(("take", g, 0))
            if s == 1 and g:
                order.append(("out", g - 1, 1))
            if s == QT + 1:
                order.append(("out", g, 0))
            if not more and s == QT + 2:
                order += [("turn", 0, k) for k in range(KC)]
            if not more and s in (QT + 3, QT + 4):
                order += [("wo", 2 * (s - QT - 3)), ("wo", 2 * (s - QT - 3) + 1)]
        order += rows
        order += [("values", g, NSTEPS - 1), ("take", g, 1)]
    order += [("out", GROUPS - 1, 1)] + [("turn", 1, k) for k in range(KC)] + [("wo", tt) for tt in range(QT, TT)]
    return order


ORDER = attention_order()
BY_VECTOR = {piece: n for n, piece in enumerate(
    p for p in ORDER if p[0] in ("v", "rows", "maxrow", "out", "turn", "wo"))}
BY_SCALAR = {piece: n for n, piece in enumerate(p for p in ORDER if p[0] == "cols")}
PROJS = {piece: n for n, piece in enumerate(p for p in ORDER if p[0] == "proj")}
TURN_BANKS = 3
STACK_Q, STACK_K = ("hi", "hi", "lo"), ("hi", "lo", "hi")
STACKED = 2 * D
MAX_ROW = 3 * STACKED


def build(nc, x_d, xT_d, gate_d, w1_d, w3_d, w2_d, wqkv_d, bqkv_d, wo_d, bo_d, router_d, v1_d, v2_d,
          rows0_d, res0_d, rows1_d, res1_d):
    L0 = Moe("l0", w1_d.shape[2], True, 5 * P // 2)
    L1 = Moe("l1", v1_d.shape[1] // E, False, 3 * P)

    def at(name, shape, dt, offset):
        return nc.alloc_sbuf_tensor_at(name, shape, dt, offset=offset)

    cursor = [16512]

    def place(name, shape, dt, size=4):
        offset = cursor[0]
        n = size
        for s in shape[1:]:
            n *= s
        cursor[0] += (n + 31) // 32 * 32
        return at(name, shape, dt, offset), offset

    w_hi, WHI = place("w_hi", [P, L0.nf, L0.cols], F32R)
    w_lo, _ = place("w_lo", [P, L0.nf, L0.cols], F32R)
    stage0, STG = place("stage0", [P, 2, L0.per_chunk * L0.cols], F32)
    xT, XT = place("xT", [P, KC, T], F32)
    xnT, XNT = place("xnT", [P, KC, T], F32)
    rows, _ = place("rows", [P, TT, ROW], F32)
    tok, _ = place("tok", [P, TT, C], F32)
    got, EXP = place("got", [P, 2, NT, ROW], F32)
    xg_hi, _ = place("xg_hi", [P, 2, KC, NB], F32R)
    xg_lo, _ = place("xg_lo", [P, 2, KC, NB], F32R)
    hot, _ = place("hot", [P, TT, NB], F16, 2)
    sil, _ = place("sil", [P, 2, NB], F32)
    prod, _ = place("prod", [P, 2, NB], F32)
    a_hi, _ = place("a_hi", [P, 2, NB], F32R)
    a_lo, _ = place("a_lo", [P, 2, NB], F32R)
    gated_y, _ = place("gated_y", [P, 2, NT, C], F32)
    got_o, _ = place("got_o", [P, NT, ROW], F32)
    xo_hi, _ = place("xo_hi", [P, KC, NB], F32R)
    xo_lo, _ = place("xo_lo", [P, KC, NB], F32R)
    hot_o, _ = place("hot_o", [P, TT, NB], F16, 2)
    gated_o, EXP_END = place("gated_o", [P, NT, C], F32)
    ident, _ = place("ident", [P, P], F32)
    identb, _ = place("identb", [P, P], BF16, 2)
    mask_q, _ = place("mask_q", [P, P], BF16, 2)
    mask_k, _ = place("mask_k", [P, P], BF16, 2)
    group_mat, _ = place("group_mat", [P, P], F32)
    before, _ = place("before", [P, P], BF16, 2)
    ones, _ = place("ones", [P, P], BF16, 2)
    n_places = max(m.blocks * m.nb for m in (L0, L1))
    places, _ = place("places", [P, n_places], F16, 2)
    token_of, _ = place("token_of", [P, TT, 2], F16, 2)
    spare_row, _ = place("spare_row", [P, NT], F32)
    sel, _ = place("sel", [P, TT, E], BF16, 2)
    pos, _ = place("pos", [P, TT, E + 1], F32)
    gate_of, _ = place("gate_of", [P, 2, NT], F32)
    count, _ = place("count", [P, E], I32)
    extra, _ = place("extra", [P, E], F32)
    extra2, _ = place("extra2", [P, E], F32)
    earlier, _ = place("earlier", [P, E, E], F32)
    extra_of, _ = place("extra_of", [P, E, E], F32)
    ran_before, _ = place("ran_before", [P, E], I32)
    found, _ = place("found", [P, 2, NT, 2], F32)
    found_o, _ = place("found_o", [P, NT, 2], F32)
    from_row, _ = place("from_row", [P, 2, NT], U32)
    to_row, _ = place("to_row", [P, 2, NT], U32)
    from_row_o, _ = place("from_row_o", [P, NT], U32)
    to_row_o, _ = place("to_row_o", [P, NT], U32)
    missing, _ = place("missing", [P, 2, NT], F32)
    gate_w, _ = place("gate_w", [P, KC, E], F32)
    router_w, _ = place("router_w", [P, KC, E], F32)
    stats, _ = place("stats", [P, KC, NH, 6], F32)
    small, _ = place("small", [P, 32], F32)
    tok_stats, _ = place("tok_stats", [P, TT, 6], F32)
    tok_mv, _ = place("tok_mv", [P, TT, 2], F32)
    std, _ = place("std", [P, TT], F32)
    rstd, _ = place("rstd", [P, TT], F32)
    rt, _ = place("rt", [P, 10, TT, E], F32)
    rs, _ = place("rs", [P, 10, TT], F32)
    order, _ = place("order", [P, TT, E], F32)
    eps, _ = place("eps", [P, 1], F32)
    bqk, _ = place("bqk", [P, 2, KC], F32)
    bv, _ = place("bv", [P, C], F32)
    key_ones, _ = place("key_ones", [P, 2], F32)
    v_sb, _ = place("v_sb", [P, TT, HEADS, 2 * D], F32)
    probs, PROBS = place("probs", [P, 2 * HG, HALF], F32)
    assert cursor[0] <= nc.sbuf_usable_end

    def over(base, end):
        at_byte = [base]

        def put(name, shape, dt):
            n = 4
            for d in shape[1:]:
                n *= d
            t = at(name, shape, dt, at_byte[0])
            at_byte[0] += (n + 31) // 32 * 32
            assert at_byte[0] <= end
            return t
        return put

    x_hi = at("x_hi", [P, KC, T], F32R, XT)
    x_lo = at("x_lo", [P, KC, T], F32R, XNT)
    att_tok = at("att_tok", [P, TT, C], F32, XT)
    att = at("att", [P, KC, T], F32, XNT)
    wqkv = at("wqkv", [P, KC, 3 * C], F32, PROBS)
    in_slots = over(WHI, STG)
    q_st = in_slots("q_st", [P, 2, 2, T], F32R)
    k_st = in_slots("k_st", [P, 2, 2, 2, T], F32R)
    in_stages = over(STG, XT)
    stage1 = in_stages("stage1", [P, 2, L1.per_chunk * L1.cols], F32)
    max_t = in_stages("max_t", [P, 2, TT, P], F32)
    taken = in_stages("taken", [P, 2, HALF], F32)
    bo = in_stages("bo", [P, C], F32)
    wo_sb = in_stages("wo_sb", [P, KC, C], F32)
    in_experts = over(EXP, EXP_END + NT * C * 4)
    qk_hi = in_experts("qk_hi", [P, 2, KC, T], F32R)
    qk_lo = in_experts("qk_lo", [P, 2, KC, T], F32R)
    wqkv_hi = in_experts("wqkv_hi", [P, KC, 3 * C], F32R)
    wqkv_lo = in_experts("wqkv_lo", [P, KC, 3 * C], F32R)
    rsum = in_experts("rsum", [P, QT, HG], F32)
    maxes = in_experts("maxes", [P, 2, HG, TT, 2], F32)

    ctx = ExitStack()
    banks = ctx.enter_context(nc.psum_tensor("banks", [P, 8 * HALF], F32))
    bank = [banks[:, i * HALF:(i + 1) * HALF] for i in range(8)]

    def sem(name):
        return ctx.enter_context(nc.semaphore(name))

    x_in, gatew_in, routerw_in, attn_in, wo_in = (sem(n) for n in (
        "x_in", "gatew_in", "routerw_in", "attn_in", "wo_in"))
    tok_in = [sem(f"tok{th}_in") for th in range(NH)]
    pool_step, dve_step = sem("pool_step"), sem("dve_step")
    dma_go, act_left, dve_left = sem("dma_go"), sem("act_left"), sem("dve_left")
    ident_ready, blank_ready = sem("ident_ready"), sem("blank_ready")
    group_ready, spare_ready, consts_ready, cleared = (
        sem("group_ready"), sem("spare_ready"), sem("consts_ready"), sem("cleared"))
    gn_stats, gn_mean, gn_var, gn_std = sem("gn_stats"), sem("gn_mean"), sem("gn_var"), sem("gn_std")
    normed, xnT_ready, turned, rows_copied = sem("normed"), sem("xnT_ready"), sem("turned"), sem("rows_copied")
    ln_stats, ln_var, ln_std = sem("ln_stats"), sem("ln_var"), sem("ln_std")
    turned_hi, turned_lo = sem("turned_hi"), sem("turned_lo")
    logits_done, logits_centred, logits_exp = sem("logits_done"), sem("logits_centred"), sem("logits_exp")
    rows_ready, sel_ready, ranked, ran_ready = (
        sem("rows_ready"), sem("sel_ready"), sem("ranked"), sem("ran_ready"))
    moe_sems = {}
    for m in (L0, L1):
        moe_sems[m.name] = {n: sem(f"{m.name}_{n}") for n in (
            "res_in", "rows_out", "staged0", "staged1", "whi_done", "wlo_done",
            "hot_ready", "found", "from_ready", "missing", "to_ready", "gates", "gathered0", "gathered1",
            "xt", "xhi", "xlo",
            "up_done", "sil_done", "up_free", "a_hi_done", "a_ready", "a_free", "gy_ready",
            "added", "all_added", "gy_free")}
        moe_sems[m.name].update({"o_" + n: sem(f"{m.name}_o_{n}") for n in (
            "hot_ready", "found", "from_ready", "missing", "to_ready", "gathered", "xt", "xhi", "xlo",
            "up_done", "sil_done", "prod_done", "a_hi_done", "a_ready", "a_free", "gy_ready", "added")})
    wqkv_hi_done, wqkv_lo_done = sem("wqkv_hi_done"), sem("wqkv_lo_done")
    proj_mm, proj_hi, proj_free = sem("proj_mm"), sem("proj_hi"), sem("proj_free")
    stacked = [[sem(f"stacked{par}{pr}") for pr in range(2)] for par in range(2)]
    stacked_k1 = [[sem(f"stacked_k1_{par}{pr}") for pr in range(2)] for par in range(2)]
    key_rows, k_zeros = sem("key_rows"), sem("k_zeros")
    to_vector, by_vector = sem("to_vector"), sem("by_vector")
    to_scalar, by_scalar = sem("to_scalar"), sem("by_scalar")
    maxcol_ready, pv_done, taken_out, biased = sem("maxcol_ready"), sem("pv_done"), sem("taken_out"), sem("biased")

    def staging(m, b):
        st = (stage0 if m.gated else stage1)[:, b, :]
        n = m.ups * m.per_chunk * P
        return (st[:, 0:n].rearrange("p (u f) -> p u f", u=m.ups),
                st[:, n:n + m.per_chunk * C].rearrange("p (f c) -> p f c", c=C))

    def load_stage(eng, m, e, b):
        s = moe_sems[m.name][f"staged{b}"]
        w = m.per_chunk * P
        ups, downs = staging(m, b)
        if m.gated:
            for i, src in enumerate((w1_d, w3_d)):
                eng.dma_start(ups[:, KC * i:KC * (i + 1), :],
                              src[bass.ds(e, 1), :, b * w:(b + 1) * w].rearrange("a (k p) f -> p (a k) f", p=P)
                              ).then_inc(s, 16)
            eng.dma_start(downs, w2_d[bass.ds(e, 1), b * w:(b + 1) * w, :].rearrange(
                "a (f p) c -> p (a f) c", p=P)).then_inc(s, 16)
        else:
            eng.dma_start(ups, v1_d.rearrange("(k p) f -> p k f", p=P)[:, :, bass.ds(e * (m.nf * P) + b * w, w)]
                          ).then_inc(s, 16)
            eng.dma_start(downs, v2_d[bass.ds(e * (m.nf * P) + b * w, w), :].rearrange("(f p) c -> p f c", p=P)
                          ).then_inc(s, 16)

    def slot_parts(m, f, buf):
        ups, downs = staging(m, f // m.per_chunk)
        i = f % m.per_chunk
        n = m.ups * P
        return ((buf[:, f, 0:n].rearrange("p (u c) -> p u c", c=P), ups[:, :, i * P:(i + 1) * P]),
                (buf[:, f, n:n + C], downs[:, i, :]))

    def branch(eng, e, m, work):
        tokens = eng.value_load(count[0:1, bass.ds(e, 1)], min_val=0, max_val=T)

        def from_block(b, first):
            with eng.If(tokens > b * m.nb):
                if b == 1:
                    first = eng.value_load(ran_before[0:1, bass.ds(e, 1)], min_val=0, max_val=E * m.further)
                work(b, first + (b - 1))
                if b + 1 < m.blocks:
                    from_block(b + 1, first)

        from_block(1, None)

    def stack_free(eng, g):
        if g == 0:
            eng.wait_ge(cleared, 1)
            eng.wait_ge(k_zeros, 1)
        if g < 2:
            eng.wait_ge(proj_free, 2 * NH)
        else:
            eng.wait_ge(proj_free, len(PROJS))
            eng.wait_ge(by_scalar, BY_SCALAR["cols", g - 2, NSTEPS - 1, HG - 1] + 1)

    def stack_part(eng, g, pr, c, qk, h):
        mt, a = (2 * g + pr) // QT, (2 * g + pr) % QT
        first, n = (0, 2 * D) if h is None else (D * h, D)
        src = slice(2 * D * a + first, 2 * D * a + first + n)
        dst = slice(STACKED * c + first, STACKED * c + first + n)
        to = k_st[dst, g % 2, pr, h, :] if qk else q_st[dst, g % 2, pr, :]
        part = (qk_hi, qk_lo)[(STACK_K if qk else STACK_Q)[c] == "lo"]
        return eng.dma_start(to.bitcast(F32), part[src, qk, mt, :].bitcast(F32))

    block = ctx.enter_context(nc.Block())

    @block.sync
    def _(sp):
        s0, s1 = moe_sems["l0"], moe_sems["l1"]
        for k in range(KC):
            sp.dma_start(xT[:, k, :], xT_d[k * P:(k + 1) * P, :]).then_inc(x_in, 16)
        sp.dma_start(gate_w[:, :, :], gate_d.rearrange("(k p) e -> p k e", p=P)).then_inc(gatew_in, 16)
        load_stage(sp, L0, 0, 0)
        sp.dma_start(res0_d[0:T, :], x_d).then_inc(s0["res_in"], 16)
        load_stage(sp, L0, 0, 1)
        sp.wait_ge(spare_ready, 1)
        for d, s in ((res0_d, s0), (res1_d, s1)):
            sp.dma_start(d[T:T + NB, :].rearrange("(t p) c -> p t c", p=P), gated_o[:, :, :]
                         ).then_inc(s["res_in"], 16)
        sp.dma_start(router_w[:, :, :], router_d.rearrange("(k p) e -> p k e", p=P)).then_inc(routerw_in, 16)
        for i in range(2):
            for k in range(KC):
                lo = i * C + k * P
                sp.dma_start(bqk[:, i, k:k + 1], bqkv_d[lo:lo + P].rearrange("(p a) -> p a", a=1)
                             ).then_inc(attn_in, 16)
        sp.dma_start(bv[:, :], bqkv_d[2 * C:3 * C].partition_broadcast(P)).then_inc(attn_in, 16)
        sp.dma_start(wqkv[:, :, :], wqkv_d.rearrange("(k p) n -> p k n", p=P)).then_inc(attn_in, 16)

        def store_rows(m, rows_d):
            sp.wait_ge(rows_ready, 1 + (not m.gated))
            sp.wait_ge(rows_copied, TT // 2)
            sp.dma_start(rows_d.rearrange("(t p) c -> p t c", p=P), rows[:, :, :]
                         ).then_inc(moe_sems[m.name]["rows_out"], 16)

        store_rows(L0, rows0_d)
        with sp.Fori(1, E) as e:
            for b in range(2):
                sp.wait_ge(s0["wlo_done"], (e - 1) * L0.nf + (b + 1) * L0.per_chunk)
                load_stage(sp, L0, e, b)
        sp.wait_ge(s0["wlo_done"], E * L0.nf)
        for b in range(2):
            load_stage(sp, L1, 0, b)
        sp.wait_ge(s0["added"], 16 * NT * E)
        sp.wait_ge(s0["all_added"], 1)
        for th in range(NH):
            sp.dma_start(tok[:, QT * th:QT * (th + 1), :],
                         res0_d[th * HALF:(th + 1) * HALF, :].rearrange("(t p) c -> p t c", p=P)
                         ).then_inc(tok_in[th], 16)
        sp.wait_ge(s0["gy_ready"], E + 1)
        sp.dma_start(wo_sb[:, :, :], wo_d.rearrange("(k p) c -> p k c", p=P)).then_inc(wo_in, 16)
        sp.dma_start(bo[:, :], bo_d.partition_broadcast(P)).then_inc(wo_in, 16)
        for g in range(GROUPS):
            stack_free(sp, g)
            for pr in range(2):
                for c in range(3):
                    stack_part(sp, g, pr, c, 0, None).then_inc(stacked[g % 2][pr], 16)
                    stack_part(sp, g, pr, c, 1, 0).then_inc(stacked[g % 2][pr], 16)
        sp.wait_ge(by_vector, len(BY_VECTOR))
        sp.dma_start(res1_d[0:T, :].rearrange("(t p) c -> p t c", p=P), tok[:, :, :]).then_inc(s1["res_in"], 16)
        store_rows(L1, rows1_d)
        with sp.Fori(1, E) as e:
            for b in range(2):
                sp.wait_ge(s1["wlo_done"], (e - 1) * L1.nf + (b + 1) * L1.per_chunk)
                load_stage(sp, L1, e, b)
        sp.wait_ge(s1["added"], 16 * NT * E)
        sp.wait_ge(s1["all_added"], 1)

    @block.gpsimd
    def _(pool):
        n = [0]

        def link(ins):
            n[0] += 1
            ins.then_inc(pool_step, 1)
            pool.wait_ge(pool_step, n[0])

        for m in (L0, L1):
            pool.sem_inc(moe_sems[m.name]["gy_free"], 2)
        link(pool.memset(group_mat[:, :], 1.0 / GROUP))
        grouped = group_mat[:, :].rearrange("p (g c) -> p g c", c=GROUP)
        link(pool.affine_select(out=grouped, in_=grouped, compare_op=ALU.is_ge, fill=0.0, base=0,
                                pattern=[[-GROUP, P // GROUP], [0, GROUP]], channel_multiplier=1))
        link(pool.affine_select(out=grouped, in_=grouped, compare_op=ALU.is_ge, fill=0.0, base=GROUP - 1,
                                pattern=[[GROUP, P // GROUP], [0, GROUP]], channel_multiplier=-1))
        pool.memset(eps[:, :], GN_EPS).then_inc(group_ready, 1)
        pool.memset(gated_o[:, :, :], 0.0).then_inc(spare_ready, 1)
        pool.memset(hot[:, :, L0.nb:NB], 0.0)
        pool.memset(hot_o[:, :, L0.nb:NB], 0.0)
        pool.memset(gated_y[:, :, NT - 1, :], 0.0).then_inc(blank_ready, 1)
        link(pool.memset(ident[:, :], 0.0))
        link(pool.affine_select(out=ident[:, :], in_=ident[:, :], compare_op=ALU.not_equal, fill=1.0, base=0,
                                pattern=[[-1, P]], channel_multiplier=1))
        pool.sem_inc(ident_ready, 1)
        link(pool.memset(ones[:, :], 1.0))
        link(pool.affine_select(out=before[:, :], in_=ones[:, :], compare_op=ALU.is_gt, fill=0.0, base=0,
                                pattern=[[1, P]], channel_multiplier=-1))
        link(pool.iota(places[:, :], [[1, n_places]], base=0, channel_multiplier=0,
                       allow_small_or_imprecise_dtypes=True))
        link(pool.memset(token_of[:, :, :], 1.0))
        link(pool.iota(token_of[:, :, 0:1], [[P, TT]], base=0, channel_multiplier=1,
                       allow_small_or_imprecise_dtypes=True))
        link(pool.iota(spare_row[:, :], [[P, NT]], base=T, channel_multiplier=1,
                       allow_small_or_imprecise_dtypes=True))
        for e in range(E):
            link(pool.memset(order[:, :, e:e + 1], float(E - e)))
        link(pool.memset(earlier[:, :, :], 1.0))
        link(pool.affine_select(out=earlier[:, :, :], in_=earlier[:, :, :], compare_op=ALU.is_gt, fill=0.0, base=0,
                                pattern=[[1, E], [-1, E]], channel_multiplier=0))
        link(pool.tensor_copy(identb[:, :], ident[:, :]))
        link(pool.memset(mask_q[:, :], 0.0))
        link(pool.affine_select(out=mask_q[:, :], in_=mask_q[:, :], compare_op=ALU.is_ge, fill=MASKED, base=0,
                                pattern=[[-1, P]], channel_multiplier=1))
        link(pool.memset(mask_k[:, :], 0.0))
        link(pool.affine_select(out=mask_k[:, :], in_=mask_k[:, :], compare_op=ALU.is_ge, fill=MASKED, base=0,
                                pattern=[[1, P]], channel_multiplier=-1))
        link(pool.memset(v_sb[:, :, :, D:2 * D], 1.0))
        link(pool.memset(key_ones[:, :], 1.0))
        for base, sign in ((-MAX_ROW, 1), (MAX_ROW + 1, -1)):
            link(pool.affine_select(out=key_ones[:, :], in_=key_ones[:, :], compare_op=ALU.is_ge, fill=0.0,
                                    base=base, pattern=[[-2 * sign, 2]], channel_multiplier=sign))
        pool.sem_inc(consts_ready, 1)

        def gather(m, rows_d, e, par):
            s = moe_sems[m.name]
            pool.wait_ge(s["from_ready"], e + 1)
            pool.sem_inc(dma_go, 1)
            for t in range(NT):
                pool.indirect_dma_start(got[:, par, t, :], None, rows_d,
                                        bass.IndirectOffsetOnAxis(from_row[:, par, t:t + 1], 0)
                                        ).then_inc(s[f"gathered{par}"], 16)

        def further(m, rows_d, res_d, e, q, first):
            s = moe_sems[m.name]
            pool.wait_ge(s["o_from_ready"], q + 1)
            pool.sem_inc(dma_go, 1)
            for t in range(NT):
                pool.indirect_dma_start(got_o[:, t, :], None, rows_d,
                                        bass.IndirectOffsetOnAxis(from_row_o[:, t:t + 1], 0)
                                        ).then_inc(s["o_gathered"], 16)
            if not first:
                pool.wait_ge(s["added"], 16 * NT * e)
            pool.wait_ge(s["o_to_ready"], q + 1)
            pool.wait_ge(s["o_gy_ready"], q + 1)
            pool.sem_inc(dma_go, 1)
            for t in range(NT):
                pool.indirect_dma_start(res_d, bass.IndirectOffsetOnAxis(to_row_o[:, t:t + 1], 0),
                                        gated_o[:, t, :], None, compute_op=ALU.add
                                        ).then_inc(s["o_added"], 16)
            pool.wait_ge(s["o_added"], 16 * NT * (q + 1))
            pool.sem_inc(dma_go, 1)

        def experts(m, rows_d, res_d):
            s = moe_sems[m.name]

            def former_added(e):
                pool.wait_ge(s["added"], 16 * NT * (e + 1))
                pool.sem_inc(s["gy_free"], 1)

            def expert(e, par, more, first=False):
                branch(pool, e, m, lambda b, q: further(m, rows_d, res_d, e, q, first))
                if more:
                    gather(m, rows_d, e + 2, par)
                if not first:
                    former_added(e - 1)
                pool.wait_ge(s["to_ready"], e + 1)
                pool.wait_ge(s["gy_ready"], e + 2)
                pool.sem_inc(dma_go, 1)
                for t in range(NT):
                    pool.indirect_dma_start(res_d, bass.IndirectOffsetOnAxis(to_row[:, par, t:t + 1], 0),
                                            gated_y[:, par, t, :], None, compute_op=ALU.add
                                            ).then_inc(s["added"], 16)

            pool.wait_ge(s["rows_out"], 16)
            pool.wait_ge(s["res_in"], 32)
            if m.gated:
                pool.wait_ge(moe_sems["l1"]["res_in"], 16)
            gather(m, rows_d, 0, 0)
            gather(m, rows_d, 1, 1)
            pool.wait_ge(ran_ready, 1 + (not m.gated))
            expert(0, 0, True, True)
            with pool.Fori(0, E // 2 - 2) as pair:
                e = 2 * pair + 1
                expert(e, 1, True)
                expert(e + 1, 0, True)
            expert(E - 3, 1, True)
            expert(E - 2, 0, False)
            expert(E - 1, 1, False)
            former_added(E - 1)
            pool.sem_inc(s["all_added"], 1)

        experts(L0, rows0_d, res0_d)
        pool.wait_ge(moe_sems["l0"]["gy_ready"], E + 1)
        pool.memset(k_st[:, 1].bitcast(F32), 0.0).then_inc(cleared, 1)
        pool.memset(max_t[:, :, :, :], 0.0).then_inc(cleared, 1)
        pool.wait_ge(wo_in, 32)
        pool.wait_ge(normed, TT)
        for tt in range(TT):
            ins = pool.tensor_tensor(tok[:, tt, :], tok[:, tt, :], bo[:, :], ALU.add)
        ins.then_inc(biased, 1)
        for g in range(GROUPS):
            stack_free(pool, g)
            for pr in range(2):
                for c in range(3):
                    stack_part(pool, g, pr, c, 1, 1).then_inc(stacked_k1[g % 2][pr], 16)
        experts(L1, rows1_d, res1_d)

    @block.tensor
    def _(pe):
        def three(out, pairs, start, stop):
            terms = [(wh, xh) for wh, wl, xh, xl in pairs] + [(wh, xl) for wh, wl, xh, xl in pairs] + \
                    [(wl, xh) for wh, wl, xh, xl in pairs]
            for i, (w, x) in enumerate(terms):
                last = pe.matmul(out, w, x, start=start and i == 0, stop=stop and i == len(terms) - 1)
            return last

        def logits(weights):
            for tt in range(TT):
                for k in range(KC):
                    mm = pe.matmul(bank[7][:, tt * E:(tt + 1) * E], xnT[:, k, tt * P:(tt + 1) * P],
                                   weights[:, k, :], start=k == 0, stop=k == KC - 1)
            mm.then_inc(logits_done, 1)

        def rank(i):
            pe.wait_ge(sel_ready, i + 1)
            pe.matmul(bank[6][:, 0:TT * E], before[:, :], sel[:, :, :], start=True, stop=True)
            for d in range(1, TT):
                pe.matmul(bank[6][:, d * E:TT * E], ones[:, :], sel[:, 0:TT - d, :], start=False, stop=True,
                          skip_group_check=True)
            for tt in range(TT):
                mm = pe.matmul(bank[5][:, 0:E], ones[:, :], sel[:, tt, :], start=tt == 0, stop=tt == TT - 1)
            mm.then_inc(ranked, 1)

        def find(out, one_hot):
            for t in range(NT):
                for tt in range(TT):
                    mm = pe.matmul(out[:, 2 * t:2 * t + 2], one_hot[:, tt, t * P:(t + 1) * P],
                                   token_of[:, tt, :], start=tt == 0, stop=tt == TT - 1)
            return mm

        def turn(m, out, source, k):
            for t, n in m.tiles:
                mm = pe.transpose(out[:, t * P:t * P + n], source[0:n, t, k * P:(k + 1) * P], ident[0:n, 0:n])
            return mm

        def up_products(m, f, h, g, hi, lo):
            for kind, out in enumerate((h, g)[:m.ups // KC]):
                mm = three(out, [(w_hi[:, f, (KC * kind + k) * P:(KC * kind + k + 1) * P],
                                  w_lo[:, f, (KC * kind + k) * P:(KC * kind + k + 1) * P],
                                  hi[:, k, 0:m.nb], lo[:, k, 0:m.nb]) for k in range(KC)], True, True)
            return mm

        def down_products(m, f, par, wait_lo):
            n = m.ups * P
            w_parts = w_hi[:, f, n:n + C], w_lo[:, f, n:n + C]
            for t, rows_n in m.tiles:
                for i in range(2):
                    pe.matmul(bank[4 + t][0:rows_n, 0:C], a_hi[:, par, t * P:t * P + rows_n], w_parts[i],
                              start=f == 0 and i == 0, stop=False)
            wait_lo()
            for t, rows_n in m.tiles:
                mm = pe.matmul(bank[4 + t][0:rows_n, 0:C], a_lo[:, par, t * P:t * P + rows_n], w_parts[0],
                               start=False, stop=f == m.nf - 1)
            return mm

        def further_up(m, f):
            h = bank[1] if m.gated or f % 2 == 0 else bank[3]
            up_products(m, f, h[:, 0:m.nb], bank[3][:, 0:m.nb], xo_hi, xo_lo
                        ).then_inc(moe_sems[m.name]["o_up_done"], 1)

        def further(m, e, q, last=None):
            s = moe_sems[m.name]
            pe.wait_ge(s["o_hot_ready"], q + 1)
            pe.wait_ge(s["from_ready"], e + 2 if last is None else last)
            find(bank[7], hot_o).then_inc(s["o_found"], 1)
            pe.wait_ge(s["o_from_ready"], q + 1)
            pe.wait_ge(s["o_gathered"], 16 * NT * (q + 1))
            pe.wait_ge(s["a_hi_done"], e * m.nf + 1)
            for k in range(KC):
                turn(m, (bank[7], bank[2])[k], got_o, k).then_inc(s["o_xt"], 1)
            pe.wait_ge(s["o_xlo"], KC * (q + 1))
            pe.wait_ge(s["wlo_done"], (e + 1) * m.nf)
            for f in range(m.nf):
                if m.gated or f == 0:
                    further_up(m, f)
                if not m.gated and f + 1 < m.nf:
                    further_up(m, f + 1)
                pe.wait_ge(s["o_a_hi_done"], m.nf * q + f + 1)
                if f == 0:
                    pe.wait_ge(s["gy_ready"], e + 1)
                down_products(m, f, 1, lambda: pe.wait_ge(s["o_a_ready"], m.nf * q + f + 1)
                              ).then_inc(s["o_a_free"], 1)
            pe.wait_ge(s["o_gy_ready"], q + 1)
            pe.wait_ge(s["o_a_free"], m.nf * (q + 1))

        def experts(m):
            s = moe_sems[m.name]
            x_banks = (bank[7], bank[7]) if m.gated else (bank[2], bank[3])

            def up(e, par, f):
                pe.wait_ge(s["wlo_done"], e * m.nf + f + 1)
                pe.wait_ge(s["up_free"], e * m.nf + f + 1)
                up_products(m, f, bank[f % 2][:, 0:m.nb], bank[2 + f % 2][:, 0:m.nb], xg_hi[:, par], xg_lo[:, par]
                            ).then_inc(s["up_done"], 1)

            def down(e, f):
                if f == 0:
                    pe.wait_ge(s["gy_ready"], e + 1)
                pe.wait_ge(s["a_hi_done"], e * m.nf + f + 1)
                down_products(m, f, f % 2, lambda: pe.wait_ge(s["a_ready"], e * m.nf + f + 3)
                              ).then_inc(s["a_free"], 1)

            def locate(e):
                pe.wait_ge(s["hot_ready"], e + 1)
                pe.wait_ge(s["from_ready"], e)
                pe.wait_ge(s["xlo"], KC * (e - 1))
                find(bank[7], hot).then_inc(s["found"], 1)

            def bring(e, par, k, located):
                if k == 0:
                    pe.wait_ge(s["from_ready"], located)
                    pe.wait_ge(s[f"gathered{par}"], 8 * NT * (e - par) + 16 * NT)
                elif m.gated:
                    pe.wait_ge(s["xlo"], KC * e + k)
                turn(m, x_banks[k], got[:, par], k).then_inc(s["xt"], 1)

            def expert(e, par, more):
                located = e + 3 if more == 2 else E
                branch(pe, e, m, lambda b, q: further(m, e, q, min(e + 2, E) if more < 2 else None))
                if more == 2:
                    locate(e + 2)
                for f in range(m.nf):
                    if f < m.nf - 1:
                        up(e, par, f + 1)
                    elif more:
                        pe.wait_ge(s["xlo"], KC * (e + 2))
                        up(e + 1, 1 - par, 0)
                    if more and f == m.bring_at:
                        bring(e + 1, 1 - par, 0, located)
                    down(e, f)
                    if more and f == m.bring_at:
                        bring(e + 1, 1 - par, 1, located)

            pe.wait_ge(s["hot_ready"], 1)
            find(bank[7], hot).then_inc(s["found"], 1)
            pe.wait_ge(s["hot_ready"], 2)
            pe.wait_ge(s["from_ready"], 1)
            find(bank[7], hot).then_inc(s["found"], 1)
            bring(0, 0, 0, 2)
            bring(0, 0, 1, 2)
            pe.wait_ge(s["xlo"], KC)
            pe.wait_ge(ran_ready, 1 + (not m.gated))
            up(0, 0, 0)
            with pe.Fori(0, E // 2 - 1) as pair:
                e = 2 * pair
                expert(e, 0, 2)
                expert(e + 1, 1, 2)
            expert(E - 2, 0, 1)
            expert(E - 1, 1, 0)

        for m in (L0, L1):
            pe.sem_inc(moe_sems[m.name]["a_free"], m.nf)
            pe.sem_inc(moe_sems[m.name]["gy_ready"], 1)

        pe.wait_ge(group_ready, 1)
        pe.wait_ge(gn_stats, 1)
        pe.matmul(bank[0][:, 0:KC], group_mat[:, :], small[:, 0:KC], start=True, stop=True).then_inc(gn_mean, 1)
        pe.wait_ge(gn_stats, 2)
        pe.matmul(bank[1][:, 0:KC], group_mat[:, :], small[:, KC:2 * KC], start=True, stop=True
                  ).then_inc(gn_var, 1)
        pe.wait_ge(gatew_in, 16)
        pe.wait_ge(xnT_ready, 1)
        logits(gate_w)
        pe.wait_ge(ident_ready, 1)
        for tt in range(TT):
            for k in range(KC):
                mm = pe.transpose(bank[2 + tt // 2][:, (tt % 2) * C + k * P:(tt % 2) * C + (k + 1) * P],
                                  xnT[:, k, tt * P:(tt + 1) * P], ident[:, :])
            if tt % 2:
                mm.then_inc(turned, 1)
        pe.wait_ge(rows_copied, TT // 2)
        pe.wait_ge(consts_ready, 1)
        rank(0)
        experts(L0)

        def turn_rows(i):
            for tt in range(TT):
                pe.wait_ge(normed, i * TT + tt + 1)
                for k in range(KC):
                    mm = pe.transpose(bank[2 * k + tt // QT][:, (tt % QT) * P:(tt % QT + 1) * P],
                                      rows[:, tt, k * P:(k + 1) * P], ident[:, :])
                    if tt % QT == QT - 1:
                        mm.then_inc(turned, 1)

        turn_rows(0)

        pe.wait_ge(wqkv_lo_done, 1)
        pe.wait_ge(turned_lo, KC * NH)

        def vector_bank(piece):
            n = BY_VECTOR[piece]
            if n >= TURN_BANKS:
                pe.wait_ge(by_vector, n - TURN_BANKS + 1)
            return bank[n % TURN_BANKS]

        def scalar_bank(piece):
            n = BY_SCALAR[piece]
            if n >= TURN_BANKS:
                pe.wait_ge(by_scalar, n - TURN_BANKS + 1)
            return bank[3 + n % TURN_BANKS]

        for piece in ORDER:
            kind = piece[0]
            if kind == "proj":
                qk, mt, th = piece[1:]
                n = PROJS[piece]
                if n >= 2:
                    pe.wait_ge(proj_free, n - 1)
                col = qk * C + mt * P
                three(bank[6 + n % 2][:, :],
                      [(wqkv_hi[:, k, col:col + P], wqkv_lo[:, k, col:col + P],
                        x_hi[:, k, th * HALF:(th + 1) * HALF],
                        x_lo[:, k, th * HALF:(th + 1) * HALF]) for k in range(KC)],
                      True, True).then_inc(proj_mm, 1)
            elif kind == "v":
                tt = piece[1]
                out = vector_bank(piece)
                three(out[:, 0:C],
                      [(x_hi[:, k, tt * P:(tt + 1) * P], x_lo[:, k, tt * P:(tt + 1) * P],
                        wqkv_hi[:, k, 2 * C:3 * C], wqkv_lo[:, k, 2 * C:3 * C]) for k in range(KC)],
                      True, True).then_inc(to_vector, 1)
            elif kind == "rows":
                g, j, i, c = piece[1:]
                out = vector_bank(piece)
                pe.wait_ge(stacked[g % 2][j // 2], 16 * 6 * (g // 2 + 1))
                pe.wait_ge(stacked_k1[g % 2][j // 2], 16 * 3 * (g // 2 + 1))
                w = min(HALF, (i + 1) * P - c * HALF)
                mm = pe.matmul(out[:, 0:max(w, 2 * P)], q_st[0:MAX_ROW, g % 2, j // 2, i * P:(i + 1) * P],
                               k_st[0:MAX_ROW, g % 2, j // 2, j % 2, c * HALF:c * HALF + max(w, 2 * P)],
                               start=True, stop=True)
                if c == i // QT:
                    mm = pe.matmul(out[:, w - P:w], identb[:, :], mask_q[:, :], start=False, stop=True,
                                   skip_group_check=True)
                mm.then_inc(to_vector, 1)
            elif kind == "maxrow":
                g, pr, th = piece[1:]
                out = vector_bank(piece)
                pe.wait_ge(maxcol_ready, 2 * g + pr + 1)
                for t in range(QT):
                    mm = pe.transpose(out[:, t * P:(t + 1) * P], max_t[:, pr, QT * th + t, :], ident[:, :])
                mm.then_inc(to_vector, 1)
            elif kind == "cols":
                g, s, j = piece[1:]
                qb, kt = STEPS[s]
                out = scalar_bank(piece)
                if (g, s, j) == (0, 0, 0):
                    pe.wait_ge(key_rows, 2)
                pe.wait_ge(by_vector, BY_VECTOR["maxrow", g, j // 2, qb] + 1)
                c0 = max(0, kt - QT * qb) * P
                c1 = min(c0, HALF - 2 * P)
                mm = pe.matmul(out[:, c1:HALF], k_st[:, g % 2, j // 2, j % 2, kt * P:(kt + 1) * P],
                               q_st[:, g % 2, j // 2, qb * HALF + c1:(qb + 1) * HALF], start=True, stop=True)
                if kt >= QT * qb:
                    mm = pe.matmul(out[:, c0:c0 + P], identb[:, :], mask_k[:, :], start=False, stop=True,
                                   skip_group_check=True)
                mm.then_inc(to_scalar, 1)
            elif kind == "values":
                g, s = piece[1:]
                qb, kt = STEPS[s]
                c0 = max(0, kt - QT * qb) * P
                if g == 0 and s == 0:
                    pe.wait_ge(by_vector, BY_VECTOR["v", TT - 1] + 1)
                    pe.wait_ge(proj_free, len(PROJS))
                if kt == 0 and g:
                    pe.wait_ge(taken_out, (g - 1) * NH + qb + 1)
                pe.wait_ge(by_scalar, BY_SCALAR["cols", g, s, HG - 1] + 1)
                for j in range(HG):
                    mm = pe.matmul(bank[6 + qb][2 * D * j:2 * D * (j + 1), c0:HALF],
                                   v_sb[:, kt, HG * g + j, :], probs[:, (s % 2) * HG + j, c0:HALF],
                                   start=kt == 0, stop=kt == QT * (qb + 1) - 1)
                mm.then_inc(pv_done, 1)
            elif kind == "out":
                g, qb = piece[1:]
                out = vector_bank(piece)
                pe.wait_ge(taken_out, g * NH + qb + 1)
                for t in range(QT):
                    mm = pe.transpose(out[:, t * P:(t + 1) * P], taken[:, qb, t * P:(t + 1) * P], ident[:, :])
                mm.then_inc(to_vector, 1)
            elif kind == "turn":
                th, k = piece[1:]
                out = vector_bank(piece)
                pe.wait_ge(by_vector, BY_VECTOR["out", GROUPS - 1, th] + 1)
                for t in range(QT):
                    mm = pe.transpose(out[:, t * P:(t + 1) * P], att_tok[:, QT * th + t, k * P:(k + 1) * P],
                                      ident[:, :])
                mm.then_inc(to_vector, 1)
            elif kind == "wo":
                tt = piece[1]
                out = vector_bank(piece)
                if tt == 0:
                    pe.wait_ge(wo_in, 32)
                pe.wait_ge(by_vector, BY_VECTOR["turn", tt // QT, KC - 1] + 1)
                for k in range(KC):
                    mm = pe.matmul(out[:, 0:C], att[:, k, tt * P:(tt + 1) * P], wo_sb[:, k, :], start=k == 0,
                                   stop=k == KC - 1)
                mm.then_inc(to_vector, 1)

        turn_rows(1)
        pe.wait_ge(routerw_in, 16)
        pe.wait_ge(xnT_ready, 1 + KC * NH)
        logits(router_w)
        rank(1)
        experts(L1)

    @block.scalar
    def _(act):
        def tokens_std(i):
            act.wait_ge(ln_var, i + 1)
            act.activation(std[:, :], tok_mv[:, :, 1], ACT.Sqrt, bias=eps[:, 0:1]).then_inc(ln_std, 1)

        def exp_logits(i):
            act.wait_ge(logits_centred, i + 1)
            act.activation(rt[:, 1], rt[:, 0], ACT.Exp).then_inc(logits_exp, 1)

        def split_hi(m, e, f):
            s = moe_sems[m.name]
            act.wait_ge(s[f"staged{f // m.per_chunk}"], m.staged * (e + 1))
            act.wait_ge(s["a_free"], e * m.nf + f + 1)
            for dst, src in slot_parts(m, f, w_hi):
                ins = act.activation(dst, src, ACT.Copy)
            ins.then_inc(s["whi_done"], 1)

        def further(m, e, q):
            s = moe_sems[m.name]
            for k in range(KC):
                act.wait_ge(s["o_xt"], KC * q + k + 1)
                act.activation(xo_hi[:, k, 0:m.nb], (bank[7], bank[2])[k][:, 0:m.nb], ACT.Copy).then_inc(s["o_xhi"], 1)
            for f in range(m.nf):
                act.wait_ge(s["o_up_done"], m.nf * q + f + 1)
                if m.gated:
                    act.activation(sil[:, 1, 0:m.nb], bank[1][:, 0:m.nb], ACT.Silu).then_inc(s["o_sil_done"], 1)
                else:
                    if f:
                        act.wait_ge(s["o_a_ready"], m.nf * q + f)
                    act.activation(prod[:, 1, 0:m.nb], bank[1 + 2 * (f % 2)][:, 0:m.nb], ACT.Gelu
                                   ).then_inc(s["o_prod_done"], 1)
            act.wait_ge(s["o_a_ready"], m.nf * (q + 1))
            act.sem_inc(act_left, 1)

        def experts(m):
            s = moe_sems[m.name]

            def round_x(e, par, k):
                act.wait_ge(s["xt"], KC * e + k + 1)
                b = bank[7] if m.gated else bank[2 + k]
                act.activation(xg_hi[:, par, k, 0:m.nb], b[:, 0:m.nb], ACT.Copy).then_inc(s["xhi"], 1)

            def stage(e, f):
                act.wait_ge(s["up_done"], e * m.nf + f + 1)
                if m.gated:
                    act.wait_ge(s["up_free"], e * m.nf + f + 1)
                    act.activation(sil[:, f % 2, 0:m.nb], bank[f % 2][:, 0:m.nb], ACT.Silu
                                   ).then_inc(s["sil_done"], 1)
                else:
                    act.wait_ge(s["a_free"], e * m.nf + f - 1 + m.nf)
                    act.activation(a_hi[:, f % 2, 0:m.nb], bank[f % 2][:, 0:m.nb], ACT.Gelu
                                   ).then_inc(s["a_hi_done"], 1)
                    act.wait_ge(s["a_ready"], e * m.nf + f + 1)
                    act.activation(prod[:, f % 2, 0:m.nb], bank[f % 2][:, 0:m.nb], ACT.Gelu
                                   ).then_inc(s["up_free"], 1)

            def gated_outputs(e, par):
                act.wait_ge(s["a_free"], (e + 2) * m.nf)
                act.wait_ge(s["gy_free"], e + 1)
                act.wait_ge(s["gates"], e + 1)
                for t, rows_n in m.tiles:
                    ins = act.activation(gated_y[0:rows_n, par, t, :], bank[4 + t][0:rows_n, 0:C], ACT.Copy,
                                         scale=gate_of[0:rows_n, par, t:t + 1])
                ins.then_inc(s["gy_ready"], 1)

            def expert(e, par, more, first=False):
                for f in range(m.nf):
                    stage(e, f)
                    if f == 0:
                        if not first:
                            gated_outputs(e - 1, 1 - par)
                        split_hi(m, e, m.nf - 2)
                        split_hi(m, e, m.nf - 1)
                        branch(act, e, m, lambda b, q: further(m, e, q))
                    elif f >= 2 and more:
                        split_hi(m, e + 1, f - 2)
                    if more and f == m.bring_at:
                        for k in range(KC):
                            round_x(e + 1, 1 - par, k)

            for k in range(KC):
                round_x(0, 0, k)
            act.wait_ge(ran_ready, 1 + (not m.gated))
            expert(0, 0, True, True)
            with act.Fori(0, E // 2 - 1) as pair:
                e = 2 * pair + 1
                expert(e, 1, True)
                expert(e + 1, 0, True)
            expert(E - 1, 1, False)
            gated_outputs(E - 1, 1)

        act.wait_ge(group_ready, 1)
        act.wait_ge(gn_var, 1)
        act.activation(small[:, 8:8 + KC], bank[1][:, 0:KC], ACT.Sqrt, bias=eps[:, 0:1]).then_inc(gn_std, 1)
        for f in range(L0.nf - 2):
            split_hi(L0, 0, f)
        exp_logits(0)
        for i in range(TT // 2):
            act.wait_ge(turned, i + 1)
            act.activation(rows[:, 2 * i:2 * i + 2, 0:C], bank[2 + i][:, :].rearrange("p (t c) -> p t c", c=C),
                           ACT.Copy).then_inc(rows_copied, 1)
        experts(L0)

        act.wait_ge(attn_in, 16 * (2 * KC + 2))
        act.wait_ge(moe_sems["l0"]["added"], 16 * NT * E)
        act.wait_ge(moe_sems["l0"]["all_added"], 1)
        act.activation(wqkv_hi[:, :, :], wqkv[:, :, :], ACT.Copy).then_inc(wqkv_hi_done, 1)
        tokens_std(0)
        for th in range(NH):
            for k in range(KC):
                act.wait_ge(turned, TT // 2 + KC * th + k + 1)
                act.activation(x_hi[:, k, th * HALF:(th + 1) * HALF], bank[2 * k + th][:, :], ACT.Copy
                               ).then_inc(turned_hi, 1)
        for piece in ORDER:
            kind = piece[0]
            if piece == ("cols", 0, 0, 0):
                act.wait_ge(consts_ready, 1)
                act.wait_ge(cleared, 1)
                act.wait_ge(k_zeros, 1)
                for h in range(2):
                    part = k_st[MAX_ROW:P, :, :, h, :].rearrange("p a b t -> p (a b) t")
                    act.activation(part, part.bitcast(F32), ACT.Identity, bias=key_ones[MAX_ROW:P, h:h + 1]
                                   ).then_inc(key_rows, 1)
            if kind == "proj":
                qk, mt, th = piece[1:]
                n = PROJS[piece]
                act.wait_ge(proj_mm, n + 1)
                act.activation(qk_hi[:, qk, mt, th * HALF:(th + 1) * HALF], bank[6 + n % 2][:, :],
                               ACT.Identity, bias=bqk[:, qk, mt:mt + 1]).then_inc(proj_hi, 1)
            elif kind == "cols":
                g, s, j = piece[1:]
                qb, kt = STEPS[s]
                c0 = max(0, kt - QT * qb) * P
                n = BY_SCALAR[piece]
                act.wait_ge(to_scalar, n + 1)
                if j == 0 and g * NSTEPS + s >= 2:
                    act.wait_ge(pv_done, g * NSTEPS + s - 1)
                act.activation(probs[:, (s % 2) * HG + j, c0:HALF], bank[3 + n % TURN_BANKS][:, c0:HALF],
                               ACT.Exp, scale=float(C) ** -0.5).then_inc(by_scalar, 1)

        tokens_std(1)
        act.wait_ge(by_vector, len(BY_VECTOR))
        for f in range(L1.nf - 2):
            split_hi(L1, 0, f)
        for th in range(NH):
            for k in range(KC):
                act.wait_ge(turned, TT // 2 + KC * NH + KC * th + k + 1)
                act.activation(xnT[:, k, th * HALF:(th + 1) * HALF], bank[2 * k + th][:, :], ACT.Copy
                               ).then_inc(xnT_ready, 1)
        exp_logits(1)
        experts(L1)

    @block.vector
    def _(dve):
        n_link = [0]

        def link(ins):
            n_link[0] += 1
            ins.then_inc(dve_step, 1)
            dve.wait_ge(dve_step, n_link[0])

        def f32(ap):
            return ap.bitcast(F32)

        def layer_norm(i):
            if i == 0:
                for tt in range(TT):
                    if tt % QT == 0:
                        dve.wait_ge(tok_in[tt // QT], 16)
                    ins = dve.bn_stats(tok_stats[:, tt, :], tok[:, tt, :])
                ins.then_inc(ln_stats, 1)
            dve.wait_ge(ln_stats, i + 1)
            for tt in range(TT):
                ins = dve.bn_aggr(tok_mv[:, tt, :], tok_stats[:, tt, :])
            ins.then_inc(ln_var, 1)
            dve.wait_ge(ln_std, i + 1)
            link(dve.reciprocal(rstd[:, :], std[:, :]))
            for tt in range(TT):
                dve.tensor_scalar(rows[:, tt, 0:C], tok[:, tt, :], tok_mv[:, tt, 0:1], rstd[:, tt:tt + 1],
                                  ALU.subtract, ALU.mult).then_inc(normed, 1)

        def over(col):
            return col.unsqueeze(2).to_broadcast([P, TT, E])

        def routing(i, first_of_ties):
            logits = bank[7][:, 0:TT * E].rearrange("p (t e) -> p t e", e=E)
            dve.wait_ge(logits_done, i + 1)
            link(dve.tensor_reduce(rs[:, 0], logits, AX_X, ALU.max))
            dve.tensor_tensor(rt[:, 0], logits, over(rs[:, 0]), ALU.subtract).then_inc(logits_centred, 1)
            dve.wait_ge(logits_exp, i + 1)
            link(dve.tensor_reduce(rs[:, 1], rt[:, 1], AX_X, ALU.add))
            link(dve.reciprocal(rs[:, 2], rs[:, 1]))
            link(dve.tensor_tensor(rt[:, 2], rt[:, 1], over(rs[:, 2]), ALU.mult))

            def top(values, value, hot, tmp):
                link(dve.tensor_reduce(value, values, AX_X, ALU.max))
                link(dve.tensor_tensor(hot, values, over(value), ALU.is_equal))
                if first_of_ties:
                    link(dve.tensor_tensor(tmp, hot, order[:, :, :], ALU.mult))
                    link(dve.tensor_reduce(rs[:, 8], tmp, AX_X, ALU.max))
                    link(dve.tensor_tensor(hot, tmp, over(rs[:, 8]), ALU.is_equal))

            top(rt[:, 2], rs[:, 3], rt[:, 3], rt[:, 4])
            if first_of_ties:
                link(dve.scalar_tensor_tensor(out=rt[:, 5], in0=rt[:, 3], scalar=-2.0, in1=rt[:, 2],
                                              op0=ALU.mult, op1=ALU.add))
            else:
                link(dve.tensor_tensor(rt[:, 4], rt[:, 2], rt[:, 3], ALU.mult))
                link(dve.tensor_tensor(rt[:, 5], rt[:, 2], rt[:, 4], ALU.subtract))
            top(rt[:, 5], rs[:, 4], rt[:, 6], rt[:, 4])
            link(dve.tensor_tensor(rs[:, 5], rs[:, 3], rs[:, 4], ALU.add))
            link(dve.reciprocal(rs[:, 6], rs[:, 5]))
            link(dve.tensor_tensor(rs[:, 7], rs[:, 6], rs[:, 3], ALU.mult))
            link(dve.tensor_tensor(rs[:, 9], rs[:, 6], rs[:, 4], ALU.mult))
            link(dve.tensor_tensor(rt[:, 7], rt[:, 3], over(rs[:, 7]), ALU.mult))
            link(dve.tensor_tensor(rt[:, 8], rt[:, 6], over(rs[:, 9]), ALU.mult))
            gates = rows[:, :, C:C + E]
            dve.tensor_tensor(gates, rt[:, 7], rt[:, 8], ALU.add).then_inc(rows_ready, 1)
            dve.wait_ge(rows_ready, i + 1)
            dve.tensor_scalar(sel[:, :, :], gates, 0.0, None, ALU.not_equal).then_inc(sel_ready, 1)
            dve.wait_ge(sel_ready, i + 1)
            dve.wait_ge(ranked, i + 1)
            link(dve.tensor_copy(count[:, :], bank[5][:, 0:E]))
            link(dve.memset(pos[:, :, :], 0.0))
            link(dve.scalar_tensor_tensor(out=pos[:, :, 0:E], in0=bank[6][:, 0:TT * E].rearrange(
                "p (t e) -> p t e", e=E), scalar=1.0, in1=sel[:, :, :], op0=ALU.add, op1=ALU.mult))
            link(dve.tensor_scalar(pos[:, :, :], pos[:, :, :], -1.0, None, ALU.add))

        def one_hots(m, out, e, b):
            for tt in range(TT):
                ins = dve.tensor_scalar(out[:, tt, 0:m.nb], places[:, b * m.nb:(b + 1) * m.nb],
                                        pos[:, tt, bass.ds(e, 1)], None, ALU.is_equal)
            return ins

        def split_lo(m, e, f):
            s = moe_sems[m.name]
            dve.wait_ge(s["whi_done"], e * m.nf + f + 1)
            for (hi, src), (lo, _) in zip(slot_parts(m, f, w_hi), slot_parts(m, f, w_lo)):
                ins = dve.tensor_tensor(lo, src, f32(hi), ALU.subtract)
            ins.then_inc(s["wlo_done"], 1)

        def further(m, e, b, q):
            s = moe_sems[m.name]
            one_hots(m, hot_o, e, b).then_inc(s["o_hot_ready"], 1)
            dve.wait_ge(s["o_found"], q + 1)
            numbers = bank[7][:, 0:2 * NT].rearrange("p (t c) -> p t c", c=2)
            dve.tensor_copy(found_o[:, :, :], numbers)
            dve.tensor_copy(from_row_o[:, :], numbers[:, :, 0]).then_inc(s["o_from_ready"], 1)
            dve.wait_ge(s["o_from_ready"], q + 1)
            dve.scalar_tensor_tensor(out=missing[:, 1, :], in0=found_o[:, :, 1], scalar=0.0, in1=spare_row[:, :],
                                     op0=ALU.is_equal, op1=ALU.mult).then_inc(s["o_missing"], 1)
            dve.wait_ge(s["o_missing"], q + 1)
            dve.tensor_tensor(to_row_o[:, :], missing[:, 1, :], found_o[:, :, 0], ALU.add
                              ).then_inc(s["o_to_ready"], 1)
            for k in range(KC):
                dve.wait_ge(s["o_xhi"], KC * q + k + 1)
                dve.tensor_tensor(xo_lo[:, k, 0:m.nb], (bank[7], bank[2])[k][:, 0:m.nb],
                                  f32(xo_hi[:, k, 0:m.nb]), ALU.subtract
                                  ).then_inc(s["o_xlo"], 1)
            for f in range(m.nf):
                n = m.nf * q + f
                if m.gated:
                    dve.wait_ge(s["o_sil_done"], n + 1)
                    dve.tensor_tensor(prod[:, 1, 0:m.nb], sil[:, 1, 0:m.nb], bank[3][:, 0:m.nb], ALU.mult
                                      ).then_inc(s["o_prod_done"], 1)
                dve.wait_ge(s["o_prod_done"], n + 1)
                if f:
                    dve.wait_ge(s["o_a_free"], n)
                dve.tensor_copy(a_hi[:, 1, 0:m.nb], prod[:, 1, 0:m.nb]).then_inc(s["o_a_hi_done"], 1)
                dve.wait_ge(s["o_a_hi_done"], n + 1)
                dve.tensor_tensor(a_lo[:, 1, 0:m.nb], prod[:, 1, 0:m.nb], f32(a_hi[:, 1, 0:m.nb]), ALU.subtract
                                  ).then_inc(s["o_a_ready"], 1)
            dve.wait_ge(s["o_a_free"], m.nf * (q + 1))
            for t, rows_n in m.tiles:
                ins = dve.tensor_scalar(gated_o[0:rows_n, t, :], bank[4 + t][0:rows_n, 0:C],
                                        got_o[0:rows_n, t, bass.ds(e + C, 1)],
                                        None, ALU.mult)
            ins.then_inc(s["o_gy_ready"], 1)
            dve.wait_ge(s["o_added"], 16 * NT * (q + 1))
            dve.sem_inc(dve_left, 1)

        def sum_further(m):
            link(dve.tensor_scalar(extra[:, :], count[:, :], float(m.nb), None, ALU.is_gt))
            for b in range(2, m.blocks):
                link(dve.tensor_scalar(extra2[:, :], count[:, :], float(b * m.nb), None, ALU.is_gt))
                link(dve.tensor_tensor(extra[:, :], extra[:, :], extra2[:, :], ALU.add))
            link(dve.tensor_tensor(extra_of[:, :, :], earlier[:, :, :],
                                   extra[:, :].unsqueeze(1).to_broadcast([P, E, E]), ALU.mult))
            link(dve.tensor_reduce(extra2[:, :], extra_of[:, :, :], AX_X, ALU.add))
            dve.tensor_copy(ran_before[:, :], extra2[:, :]).then_inc(ran_ready, 1)

        def experts(m):
            s = moe_sems[m.name]

            def stage(e, f):
                n = e * m.nf + f
                b = f % 2
                if m.gated:
                    dve.wait_ge(s["sil_done"], n + 1)
                    dve.tensor_tensor(prod[:, b, 0:m.nb], sil[:, b, 0:m.nb], bank[2 + b][:, 0:m.nb], ALU.mult
                                      ).then_inc(s["up_free"], 1)
                dve.wait_ge(s["up_free"], n + 3)
                dve.wait_ge(s["a_free"], n - 1 + m.nf)
                if m.gated:
                    dve.tensor_copy(a_hi[:, b, 0:m.nb], prod[:, b, 0:m.nb]).then_inc(s["a_hi_done"], 1)
                dve.wait_ge(s["a_hi_done"], n + 1)
                dve.tensor_tensor(a_lo[:, b, 0:m.nb], prod[:, b, 0:m.nb], f32(a_hi[:, b, 0:m.nb]), ALU.subtract
                                  ).then_inc(s["a_ready"], 1)

            def located(e, par):
                dve.wait_ge(s["found"], e + 1)
                numbers = bank[7][:, 0:2 * NT].rearrange("p (t c) -> p t c", c=2)
                dve.tensor_copy(found[:, par], numbers)
                dve.tensor_copy(from_row[:, par, :], numbers[:, :, 0]).then_inc(s["from_ready"], 1)

            def destination(e, par):
                dve.wait_ge(s["from_ready"], e + 1)
                dve.scalar_tensor_tensor(out=missing[:, 0, :], in0=found[:, par, :, 1], scalar=0.0,
                                         in1=spare_row[:, :], op0=ALU.is_equal, op1=ALU.mult
                                         ).then_inc(s["missing"], 1)
                dve.wait_ge(s["missing"], e + 1)
                dve.wait_ge(s["gy_free"], e + 1)
                dve.tensor_tensor(to_row[:, par, :], missing[:, 0, :], found[:, par, :, 0], ALU.add
                                  ).then_inc(s["to_ready"], 1)

            def rest_x(e, par, used):
                for k in range(KC):
                    dve.wait_ge(s["xhi"], KC * e + k + 1)
                    b = bank[7] if m.gated else bank[2 + k]
                    dve.tensor_tensor(xg_lo[:, par, k, 0:m.nb], b[:, 0:m.nb],
                                      f32(xg_hi[:, par, k, 0:m.nb]), ALU.subtract
                                      ).then_inc(s["xlo"], 1)
                dve.wait_ge(s["gy_ready"], used)
                dve.tensor_copy(gate_of[:, par, :], got[:, par, :, bass.ds(e + C, 1)].rearrange("p t a -> p (t a)")
                                ).then_inc(s["gates"], 1)

            def expert(e, par, more):
                for f in range(m.nf):
                    stage(e, f)
                    if f == 0:
                        split_lo(m, e, m.nf - 2)
                        split_lo(m, e, m.nf - 1)
                        branch(dve, e, m, lambda b, q: further(m, e, b, q))
                        if more == 2:
                            dve.wait_ge(s["to_ready"], e + 1)
                            located(e + 2, par)
                    elif f >= 2 and more:
                        split_lo(m, e + 1, f - 2)
                    if more == 2 and f == 1:
                        one_hots(m, hot, e + 3, 0).then_inc(s["hot_ready"], 1)
                    if more and f == m.bring_at:
                        rest_x(e + 1, 1 - par, e + 1)
                if more:
                    destination(e + 1, 1 - par)

            one_hots(m, hot, 0, 0).then_inc(s["hot_ready"], 1)
            located(0, 0)
            one_hots(m, hot, 1, 0).then_inc(s["hot_ready"], 1)
            destination(0, 0)
            sum_further(m)
            located(1, 1)
            one_hots(m, hot, 2, 0).then_inc(s["hot_ready"], 1)
            rest_x(0, 0, 1)
            with dve.Fori(0, E // 2 - 1) as pair:
                e = 2 * pair
                expert(e, 0, 2)
                expert(e + 1, 1, 2)
            expert(E - 2, 0, 1)
            expert(E - 1, 1, 0)

        for m in (L0, L1):
            s = moe_sems[m.name]
            dve.sem_inc(s["up_free"], 2)
            dve.sem_inc(s["a_ready"], 2)

        dve.wait_ge(x_in, 16 * KC)
        for k in range(KC):
            for th in range(NH):
                link(dve.bn_stats(stats[:, k, th, :], xT[:, k, th * HALF:(th + 1) * HALF]))
            link(dve.bn_aggr(small[:, 4 + 2 * k:6 + 2 * k], stats[:, k, :, :]))
        mv = small[:, 4:8].rearrange("p (k s) -> p s k", s=2)
        mean, dev, square = small[:, 16:16 + KC], small[:, 18:18 + KC], small[:, 20:20 + KC]
        inv = small[:, 22:22 + KC]
        dve.tensor_copy(small[:, 0:KC], mv[:, 0, :]).then_inc(gn_stats, 1)
        dve.wait_ge(gn_mean, 1)
        link(dve.tensor_copy(mean, bank[0][:, 0:KC]))
        link(dve.tensor_tensor(dev, mv[:, 0, :], mean, ALU.subtract))
        link(dve.tensor_tensor(square, dev, dev, ALU.mult))
        dve.tensor_tensor(small[:, KC:2 * KC], square, mv[:, 1, :], ALU.add).then_inc(gn_stats, 1)
        dve.wait_ge(gn_std, 1)
        link(dve.reciprocal(inv, small[:, 8:8 + KC]))
        for k in range(KC):
            ins = dve.tensor_scalar(xnT[:, k, :], xT[:, k, :], mean[:, k:k + 1], inv[:, k:k + 1],
                                    ALU.subtract, ALU.mult)
        ins.then_inc(xnT_ready, 1)
        for f in range(L0.nf - 2):
            split_lo(L0, 0, f)
        dve.wait_ge(blank_ready, 1)
        routing(0, False)
        experts(L0)

        dve.wait_ge(moe_sems["l0"]["gy_ready"], E + 1)
        dve.memset(k_st[:, 0].bitcast(F32), 0.0).then_inc(k_zeros, 1)
        dve.wait_ge(wqkv_hi_done, 1)
        dve.tensor_tensor(wqkv_lo[:, :, :], wqkv[:, :, :], f32(wqkv_hi[:, :, :]), ALU.subtract
                          ).then_inc(wqkv_lo_done, 1)
        layer_norm(0)
        for th in range(NH):
            for k in range(KC):
                c = slice(th * HALF, (th + 1) * HALF)
                dve.wait_ge(turned_hi, KC * th + k + 1)
                dve.tensor_tensor(x_lo[:, k, c], bank[2 * k + th][:, :], f32(x_hi[:, k, c]), ALU.subtract
                                  ).then_inc(turned_lo, 1)
        for piece in ORDER:
            kind = piece[0]
            n = BY_VECTOR.get(piece)
            if n is not None:
                dve.wait_ge(to_vector, n + 1)
                out = bank[n % TURN_BANKS]
            if kind == "proj":
                qk, mt, th = piece[1:]
                p = PROJS[piece]
                c = slice(th * HALF, (th + 1) * HALF)
                dve.wait_ge(proj_hi, p + 1)
                dve.scalar_tensor_tensor(out=qk_lo[:, qk, mt, c], in0=bank[6 + p % 2][:, :],
                                         scalar=bqk[:, qk, mt:mt + 1], in1=f32(qk_hi[:, qk, mt, c]),
                                         op0=ALU.add, op1=ALU.subtract).then_inc(proj_free, 1)
            elif kind == "v":
                dve.tensor_tensor(v_sb[:, piece[1], :, 0:D], out[:, 0:C].rearrange("p (h d) -> p h d", d=D),
                                  bv[:, :].rearrange("p (h d) -> p h d", d=D), ALU.add).then_inc(by_vector, 1)
            elif kind == "rows":
                g, j, i, c = piece[1:]
                w = min(HALF, (i + 1) * P - c * HALF)
                dve.tensor_reduce(maxes[:, g % 2, j, i:i + 1, c], out[:, 0:w], AX_X, ALU.max
                                  ).then_inc(by_vector, 1)
            elif kind == "maxcol":
                g, pr = piece[1:]
                dve.wait_ge(by_vector, BY_VECTOR["rows", g, 2 * pr + 1, TT - 1, 1] + 1)
                if g == 0 and pr == 0:
                    dve.wait_ge(cleared, 2)
                both = maxes[:, g % 2, 2 * pr:2 * pr + 2, QT:TT, :]
                link(dve.tensor_tensor(both[:, :, :, 0], both[:, :, :, 0], both[:, :, :, 1], ALU.max))
                top = maxes[:, g % 2, 2 * pr:2 * pr + 2, :, 0].rearrange("p j t -> p t j")
                cols = max_t[:, pr, :, MAX_ROW:MAX_ROW + 4].rearrange("p t (j c) -> p t j c", j=2)
                hi, lo = cols[:, :, :, 0], cols[:, :, :, 1]
                link(dve.tensor_scalar(hi.bitcast(F32R), top, -1.0, None, ALU.mult))
                dve.scalar_tensor_tensor(out=lo.bitcast(F32R), in0=top, scalar=-1.0, in1=hi,
                                         op0=ALU.mult, op1=ALU.subtract).then_inc(maxcol_ready, 1)
            elif kind == "maxrow":
                g, pr, th = piece[1:]
                dve.tensor_copy(q_st[MAX_ROW:P, g % 2, pr, th * HALF:(th + 1) * HALF], out[MAX_ROW:P, :]
                                ).then_inc(by_vector, 1)
            elif kind == "take":
                g, qb = piece[1:]
                dve.wait_ge(pv_done, g * NSTEPS + (NSTEPS if qb else QT))
                dve.tensor_copy(taken[:, qb, :], bank[6 + qb][:, :]).then_inc(taken_out, 1)
            elif kind == "out":
                g, qb = piece[1:]
                heads = out[:, :].rearrange("p (t j d) -> p t j d", t=QT, j=HG)
                link(dve.reciprocal(rsum[:, :, :], heads[:, :, :, D]))
                dest = att_tok[:, QT * qb:QT * (qb + 1), HG * D * g:HG * D * (g + 1)].rearrange(
                    "p t (j d) -> p t j d", d=D)
                dve.tensor_tensor(dest, heads[:, :, :, 0:D], rsum[:, :, :].unsqueeze(3).to_broadcast([P, QT, HG, D]),
                                  ALU.mult).then_inc(by_vector, 1)
            elif kind == "turn":
                th, k = piece[1:]
                dve.tensor_copy(att[:, k, th * HALF:(th + 1) * HALF], out[:, :]).then_inc(by_vector, 1)
            elif kind == "wo":
                tt = piece[1]
                if tt == 0:
                    dve.wait_ge(biased, 1)
                dve.tensor_tensor(tok[:, tt, :], tok[:, tt, :], out[:, 0:C], ALU.add
                                  ).then_inc(by_vector, 1)
                dve.wait_ge(by_vector, n + 1)
                ins = dve.bn_stats(tok_stats[:, tt, :], tok[:, tt, :])
                if tt == TT - 1:
                    ins.then_inc(ln_stats, 1)

        dve.wait_ge(by_vector, len(BY_VECTOR))
        layer_norm(1)
        for f in range(L1.nf - 2):
            split_lo(L1, 0, f)
        routing(1, True)
        experts(L1)

    ctx.close()


def kernel(x, L0_conv_gate_w, L0_conv_w1, L0_conv_w3, L0_conv_w2, L1_attn_Wqkv, L1_attn_bqkv, L1_attn_Wo,
           L1_attn_bo, L1_ffn_router_w, L1_ffn_w1, L1_ffn_w2):
    import numpy as np
    import concourse.bacc as bacc
    from concourse.bass_utils import run_bass_kernel_spmd

    nc = bacc.Bacc("TRN2", target_bir_lowering=False, num_devices=1)
    x = np.asarray(x)
    named = [
        ("x", np.ascontiguousarray(x.reshape(T, C))),
        ("xT", np.ascontiguousarray(x.reshape(T, C).T)),
        ("gate_w", np.ascontiguousarray(L0_conv_gate_w)),
        ("w1", np.ascontiguousarray(L0_conv_w1)),
        ("w3", np.ascontiguousarray(L0_conv_w3)),
        ("w2", np.ascontiguousarray(L0_conv_w2)),
        ("Wqkv", np.ascontiguousarray(L1_attn_Wqkv)),
        ("bqkv", np.ascontiguousarray(L1_attn_bqkv)),
        ("Wo", np.ascontiguousarray(L1_attn_Wo)),
        ("bo", np.ascontiguousarray(L1_attn_bo)),
        ("router_wT", np.ascontiguousarray(np.asarray(L1_ffn_router_w).T)),
        ("ffn_w1", np.ascontiguousarray(L1_ffn_w1)),
        ("ffn_w2", np.ascontiguousarray(L1_ffn_w2)),
    ]
    arrays, args = {}, []
    for name, a in named:
        arrays[f"in_{name}"] = a
        args.append(nc.dram_tensor(f"in_{name}", a.shape, mybir.dt.from_np(a.dtype), kind="ExternalInput").ap())
    args.append(nc.dram_tensor("rows0", (T, ROW), F32, kind="Internal").ap())
    args.append(nc.dram_tensor("res0", (T + NB, C), F32, kind="Internal").ap())
    args.append(nc.dram_tensor("rows1", (T, ROW), F32, kind="Internal").ap())
    args.append(nc.dram_tensor("out", (T + NB, C), F32, kind="ExternalOutput").ap())
    build(nc, *args)
    r = run_bass_kernel_spmd(nc, [arrays], core_ids=[0])
    out = r.results[0]["out"]
    return np.ascontiguousarray(out[:T]).reshape(x.shape)
```
